# Optimizing a Trainium2 kernel written in Bass

```python
import numpy as np
import jax
import jax.numpy as jnp

def _softmax(x, axis=-1):
    return jax.nn.softmax(x, axis=axis)

def _gelu(x):
    return jax.nn.gelu(x, approximate=True)

def _silu(x):
    return jax.nn.silu(x)

def _sigmoid(x):
    return jax.nn.sigmoid(x)

def _layernorm(x, axis=-1, eps=1e-05):
    m = jnp.mean(x, axis=axis, keepdims=True)
    v = jnp.var(x, axis=axis, keepdims=True)
    return (x - m) / jnp.sqrt(v + eps)

def _scatter_add(tgt, idx, src, axis=0):
    return tgt.at[idx].add(src)

def _segment_sum(src, seg, n):
    return jax.ops.segment_sum(src, seg, n)
kernel_name = 'mk_xattn_ffn_d2_seqx_r8_613740'

def setup_inputs(seed: int=0):
    np.random.seed(seed)
    _w = jnp.asarray

    def _rec_inputs():
        import jax
        import jax.numpy as jnp
        _rk = jax.random.key(seed)
        x = -0.0005207 + 1.001 * jax.random.normal(jax.random.fold_in(_rk, 1), (16, 128, 256), jnp.float32)
        _lenS = 128 - jax.random.randint(jax.random.fold_in(_rk, 7), (16,), 0, max(1, 128 // 4) + 1, jnp.int32)
        _lenS2 = 128 - jax.random.randint(jax.random.fold_in(_rk, 8), (16,), 0, max(1, 128 // 4) + 1, jnp.int32)
        _ctx_2048P = jax.random.normal(jax.random.fold_in(_rk, 12), (16, 16, 256), jnp.float32)
        _ctx_2048c = jax.random.dirichlet(jax.random.fold_in(_rk, 512), 0.3 * jnp.ones((16,), jnp.float32), (16, 128))
        _ctx_2048t = jnp.einsum('bsk,bkd->bsd', _ctx_2048c, _ctx_2048P)
        _ctx_2048t = _ctx_2048t * jax.lax.rsqrt(jnp.mean(jnp.square(_ctx_2048t)) + 1e-12) * 0.953939
        ctx_2048 = -5.72187e-05 + 0.999849 * (_ctx_2048t + 0.3 * jax.random.normal(jax.random.fold_in(_rk, 612), (16, 128, 256), jnp.float32))
        _validS = jnp.arange(128)[None, :] < _lenS[:, None]
        _validS2 = jnp.arange(128)[None, :] < _lenS2[:, None]
        _causal = jnp.tril(jnp.ones((128, 128), dtype=bool))
        mask_BxSx4224_bf0 = jnp.logical_not(jnp.ones((16, 128, 528), dtype=bool))
        return (x, ctx_2048, mask_BxSx4224_bf0)
    x, ctx_2048, mask_BxSx4224_bf0 = _rec_inputs()

    def _L0_xattn_setup():
        import jax, jax.numpy as jnp
        import numpy as np
        import math
        DIM = 256
        B, Q_LEN, KV_LEN = (8, 128, 512)
        key = jax.random.key(seed)
        ks = jax.random.split(key, 8)
        x = jax.random.normal(ks[0], (B, Q_LEN, DIM), dtype=jnp.float32)
        mask = jnp.zeros((B, Q_LEN, KV_LEN + Q_LEN), dtype=bool)
        k_cache = jax.random.normal(ks[1], (B, KV_LEN, DIM), dtype=jnp.float32)
        v_cache = jax.random.normal(ks[2], (B, KV_LEN, DIM), dtype=jnp.float32)
        scale = 1.0 / math.sqrt(DIM)
        wq = jax.random.normal(ks[3], (DIM, DIM), dtype=jnp.float32) * scale
        wk = jax.random.normal(ks[4], (DIM, DIM), dtype=jnp.float32) * scale
        wv = jax.random.normal(ks[5], (DIM, DIM), dtype=jnp.float32) * scale
        wo = jax.random.normal(ks[6], (DIM, DIM), dtype=jnp.float32) * scale
        return {'x': x, 'mask': mask, 'k_cache': k_cache, 'v_cache': v_cache, 'wq': wq, 'wk': wk, 'wv': wv, 'wo': wo}
    _L0_xattn_all = _L0_xattn_setup()
    _L0_xattn_in = {k: v for k, v in _L0_xattn_all.items() if k in ('wq', 'wk', 'wv', 'wo')}
    del _L0_xattn_all

    def _L0_ffn_setup():
        import jax, jax.numpy as jnp
        import numpy as np
        B, S, D, F, E, SH, K = (2, 256, 256, 128, 16, 2, 2)

        def _experts_all(x, g, gb, w1, b1, w2, b2):
            y = jax.nn.gelu(jnp.einsum('bsd,edf->bsef', x, g) + gb, approximate=False)
            y = y * (jnp.einsum('bsd,edf->bsef', x, w1) + b1)
            return jnp.einsum('bsef,efd->bsed', y, w2) + b2
        key = jax.random.key(seed)
        ks = jax.random.split(key, 8)
        std = 0.02
        mk = lambda k, sh: jax.random.normal(k, sh, jnp.float32) * std
        return {'x': jax.random.normal(ks[0], (B, S, D), jnp.float32), 'wa': mk(ks[1], (D, E)), 'rg': mk(ks[2], (E, D, F)), 'rgb': jnp.zeros((E, F), jnp.float32), 'rw1': mk(ks[3], (E, D, F)), 'rb1': jnp.zeros((E, F), jnp.float32), 'rw2': mk(ks[4], (E, F, D)), 'rb2': jnp.zeros((E, D), jnp.float32), 'sg': mk(ks[5], (SH, D, F)), 'sgb': jnp.zeros((SH, F), jnp.float32), 'sw1': mk(ks[6], (SH, D, F)), 'sb1': jnp.zeros((SH, F), jnp.float32), 'sw2': mk(ks[7], (SH, F, D)), 'sb2': jnp.zeros((SH, D), jnp.float32)}
    _L0_ffn_all = _L0_ffn_setup()
    _L0_ffn_in = {k: v for k, v in _L0_ffn_all.items() if k in ('wa', 'rg', 'rgb', 'rw1', 'rb1', 'rw2', 'rb2', 'sg', 'sgb', 'sw1', 'sb1', 'sw2', 'sb2')}
    del _L0_ffn_all

    def _L1_xattn_setup():
        import jax, jax.numpy as jnp
        import numpy as np
        N_HEADS = 16
        N_KV_HEADS = 4

        def _rope_cos_sin(T, d, dtype):
            inv_freq = 1.0 / 10000.0 ** (jnp.arange(0, d, 2, dtype=dtype) / d)
            t = jnp.arange(T, dtype=dtype)
            freqs = jnp.einsum('i,j->ij', t, inv_freq)
            emb = jnp.concatenate([freqs, freqs], axis=-1)
            return (jnp.cos(emb), jnp.sin(emb))

        def _rotate_half(x):
            h = x.shape[-1] // 2
            return jnp.concatenate([-x[..., h:], x[..., :h]], axis=-1)
        key = jax.random.key(seed)
        ks = jax.random.split(key, 12)
        B, C, T = (4, 128, 256)
        d = C // N_HEADS
        kv_dim = d * N_KV_HEADS
        out_ch = C

        def xavier(k, shape):
            fan_out, fan_in = shape
            lim = np.sqrt(6.0 / (fan_in + fan_out))
            return jax.random.uniform(k, shape, jnp.float32, -lim, lim)
        return {'query': jax.random.normal(ks[0], (B, C, T), jnp.float32), 'key_value': jax.random.normal(ks[1], (B, C, T), jnp.float32), 'Wq': xavier(ks[2], (C, C)), 'bq': jnp.zeros((C,), jnp.float32), 'Wk': xavier(ks[3], (kv_dim, C)), 'bk': jnp.zeros((kv_dim,), jnp.float32), 'Wv': xavier(ks[4], (kv_dim, C)), 'bv': jnp.zeros((kv_dim,), jnp.float32), 'Wo': xavier(ks[5], (out_ch, C)), 'bo': jax.random.normal(ks[6], (out_ch,), jnp.float32) * 0.02}
    _L1_xattn_all = _L1_xattn_setup()
    _L1_xattn_in = {k: v for k, v in _L1_xattn_all.items() if k in ('Wq', 'bq', 'Wk', 'bk', 'Wv', 'bv', 'Wo', 'bo')}
    del _L1_xattn_all

    def _L1_ffn_setup():
        import jax, jax.numpy as jnp
        import numpy as np
        D_MODEL = 256
        D_EXPERT = 1024
        EPS = 1e-08

        def ternary_quant(w):
            scale = jnp.mean(jnp.abs(w)) + EPS
            q = jnp.clip(jnp.round(w / scale), -1.0, 1.0) * scale
            return w + jax.lax.stop_gradient(q - w)
        key = jax.random.key(seed)
        k_x, k_up, k_gate, k_down = jax.random.split(key, 4)
        std_in = 1.0 / np.sqrt(D_MODEL)
        std_exp = 1.0 / np.sqrt(D_EXPERT)
        return {'x': jax.random.normal(k_x, (4, 256, D_MODEL), dtype=jnp.float32), 'W_up': jax.random.normal(k_up, (D_EXPERT, D_MODEL), dtype=jnp.float32) * std_in, 'W_gate': jax.random.normal(k_gate, (D_EXPERT, D_MODEL), dtype=jnp.float32) * std_in, 'W_down': jax.random.normal(k_down, (D_MODEL, D_EXPERT), dtype=jnp.float32) * std_exp}
    _L1_ffn_all = _L1_ffn_setup()
    _L1_ffn_in = {k: v for k, v in _L1_ffn_all.items() if k in ('W_up', 'W_gate', 'W_down')}
    del _L1_ffn_all
    return {'x': x, 'ctx_2048': ctx_2048, 'mask_BxSx4224_bf0': mask_BxSx4224_bf0, 'L0_xattn_wq': _L0_xattn_in['wq'], 'L0_xattn_wk': _L0_xattn_in['wk'], 'L0_xattn_wv': _L0_xattn_in['wv'], 'L0_xattn_wo': _L0_xattn_in['wo'], 'L0_ffn_wa': _L0_ffn_in['wa'], 'L0_ffn_rg': _L0_ffn_in['rg'], 'L0_ffn_rgb': _L0_ffn_in['rgb'], 'L0_ffn_rw1': _L0_ffn_in['rw1'], 'L0_ffn_rb1': _L0_ffn_in['rb1'], 'L0_ffn_rw2': _L0_ffn_in['rw2'], 'L0_ffn_rb2': _L0_ffn_in['rb2'], 'L0_ffn_sg': _L0_ffn_in['sg'], 'L0_ffn_sgb': _L0_ffn_in['sgb'], 'L0_ffn_sw1': _L0_ffn_in['sw1'], 'L0_ffn_sb1': _L0_ffn_in['sb1'], 'L0_ffn_sw2': _L0_ffn_in['sw2'], 'L0_ffn_sb2': _L0_ffn_in['sb2'], 'L1_xattn_Wq': _L1_xattn_in['Wq'], 'L1_xattn_bq': _L1_xattn_in['bq'], 'L1_xattn_Wk': _L1_xattn_in['Wk'], 'L1_xattn_bk': _L1_xattn_in['bk'], 'L1_xattn_Wv': _L1_xattn_in['Wv'], 'L1_xattn_bv': _L1_xattn_in['bv'], 'L1_xattn_Wo': _L1_xattn_in['Wo'], 'L1_xattn_bo': _L1_xattn_in['bo'], 'L1_ffn_W_up': _L1_ffn_in['W_up'], 'L1_ffn_W_gate': _L1_ffn_in['W_gate'], 'L1_ffn_W_down': _L1_ffn_in['W_down']}

def reference(x, ctx_2048, mask_BxSx4224_bf0, L0_xattn_wq, L0_xattn_wk, L0_xattn_wv, L0_xattn_wo, L0_ffn_wa, L0_ffn_rg, L0_ffn_rgb, L0_ffn_rw1, L0_ffn_rb1, L0_ffn_rw2, L0_ffn_rb2, L0_ffn_sg, L0_ffn_sgb, L0_ffn_sw1, L0_ffn_sb1, L0_ffn_sw2, L0_ffn_sb2, L1_xattn_Wq, L1_xattn_bq, L1_xattn_Wk, L1_xattn_bk, L1_xattn_Wv, L1_xattn_bv, L1_xattn_Wo, L1_xattn_bo, L1_ffn_W_up, L1_ffn_W_gate, L1_ffn_W_down):
    import jax
    import jax.numpy as jnp

    def _L0_xattn_ref(x, mask, k_cache, v_cache, wq, wk, wv, wo):
        import jax, jax.numpy as jnp
        import numpy as np
        import math
        DIM = 256
        B, Q_LEN, KV_LEN = (8, 128, 512)
        q = jnp.einsum('bsd,ed->bse', x, wq)
        k_new = jnp.einsum('bsd,ed->bse', x, wk)
        v_new = jnp.einsum('bsd,ed->bse', x, wv)
        k = jnp.concatenate([k_cache, k_new], axis=1)
        v = jnp.concatenate([v_cache, v_new], axis=1)
        scale = 1.0 / math.sqrt(q.shape[-1])
        scores = jnp.einsum('bqd,bkd->bqk', q, k) * scale
        attn = jax.nn.softmax(scores, axis=-1)
        out = jnp.einsum('bqk,bkd->bqd', attn, v)
        return jnp.einsum('bqd,ed->bqe', out, wo)

    def _L0_ffn_ref(x, wa, rg, rgb, rw1, rb1, rw2, rb2, sg, sgb, sw1, sb1, sw2, sb2):
        import jax, jax.numpy as jnp
        import numpy as np
        B, S, D, F, E, SH, K = (2, 256, 256, 128, 16, 2, 2)

        def _experts_all(x, g, gb, w1, b1, w2, b2):
            y = jax.nn.gelu(jnp.einsum('bsd,edf->bsef', x, g) + gb, approximate=False)
            y = y * (jnp.einsum('bsd,edf->bsef', x, w1) + b1)
            return jnp.einsum('bsef,efd->bsed', y, w2) + b2
        aff = jax.nn.sigmoid(jnp.einsum('bsd,de->bse', x, wa))
        topk_p, topk_i = jax.lax.top_k(aff, K)
        topk_p = topk_p / jnp.sum(topk_p, axis=-1, keepdims=True)
        combine = jnp.sum(jax.nn.one_hot(topk_i, E, dtype=x.dtype) * topk_p[..., None], axis=2)
        routed = jnp.einsum('bsed,bse->bsd', _experts_all(x, rg, rgb, rw1, rb1, rw2, rb2), combine)
        shared = jnp.sum(_experts_all(x, sg, sgb, sw1, sb1, sw2, sb2), axis=2)
        return x + shared + routed

    def _L1_xattn_ref(query, key_value, Wq, bq, Wk, bk, Wv, bv, Wo, bo):
        import jax, jax.numpy as jnp
        import numpy as np
        N_HEADS = 16
        N_KV_HEADS = 4

        def _rope_cos_sin(T, d, dtype):
            inv_freq = 1.0 / 10000.0 ** (jnp.arange(0, d, 2, dtype=dtype) / d)
            t = jnp.arange(T, dtype=dtype)
            freqs = jnp.einsum('i,j->ij', t, inv_freq)
            emb = jnp.concatenate([freqs, freqs], axis=-1)
            return (jnp.cos(emb), jnp.sin(emb))

        def _rotate_half(x):
            h = x.shape[-1] // 2
            return jnp.concatenate([-x[..., h:], x[..., :h]], axis=-1)
        B, C, T = query.shape
        Hq, Hkv = (N_HEADS, N_KV_HEADS)
        d = C // Hq
        q = jnp.einsum('oc,bct->bot', Wq, query) + bq[None, :, None]
        k = jnp.einsum('oc,bct->bot', Wk, key_value) + bk[None, :, None]
        v = jnp.einsum('oc,bct->bot', Wv, key_value) + bv[None, :, None]
        q = q.reshape(B, Hq, d, T).transpose(0, 1, 3, 2)
        k = k.reshape(B, Hkv, d, T).transpose(0, 1, 3, 2)
        v = v.reshape(B, Hkv, d, T).transpose(0, 1, 3, 2)
        cos, sin = _rope_cos_sin(T, d, q.dtype)
        cos, sin = (cos[None, None], sin[None, None])
        q = q * cos + _rotate_half(q) * sin
        k = k * cos + _rotate_half(k) * sin
        rep = Hq // Hkv
        k = jnp.repeat(k, rep, axis=1)
        v = jnp.repeat(v, rep, axis=1)
        scale = 1.0 / jnp.sqrt(jnp.asarray(d, q.dtype))
        scores = jnp.einsum('bhqd,bhkd->bhqk', q, k) * scale
        attn = jax.nn.softmax(scores, axis=-1)
        out = jnp.einsum('bhqk,bhkd->bhqd', attn, v)
        out = out.transpose(0, 1, 3, 2).reshape(B, C, T)
        out = jnp.einsum('oc,bct->bot', Wo, out) + bo[None, :, None]
        return out

    def _L1_ffn_ref(x, W_up, W_gate, W_down):
        import jax, jax.numpy as jnp
        import numpy as np
        D_MODEL = 256
        D_EXPERT = 1024
        EPS = 1e-08

        def ternary_quant(w):
            scale = jnp.mean(jnp.abs(w)) + EPS
            q = jnp.clip(jnp.round(w / scale), -1.0, 1.0) * scale
            return w + jax.lax.stop_gradient(q - w)
        wu = ternary_quant(W_up)
        wg = ternary_quant(W_gate)
        wd = ternary_quant(W_down)
        up = jnp.einsum('bsd,ed->bse', x, wu)
        gate = jnp.einsum('bsd,ed->bse', x, wg)
        hidden = jax.nn.silu(up) * gate
        return jnp.einsum('bse,de->bsd', hidden, wd)
    x = x + _L0_xattn_ref(_layernorm(x, axis=-1), mask_BxSx4224_bf0, ctx_2048, ctx_2048, L0_xattn_wq, L0_xattn_wk, L0_xattn_wv, L0_xattn_wo)
    x = x + _L0_ffn_ref(_layernorm(x, axis=-1), L0_ffn_wa, L0_ffn_rg, L0_ffn_rgb, L0_ffn_rw1, L0_ffn_rb1, L0_ffn_rw2, L0_ffn_rb2, L0_ffn_sg, L0_ffn_sgb, L0_ffn_sw1, L0_ffn_sb1, L0_ffn_sw2, L0_ffn_sb2)
    x = x + _L1_xattn_ref(_layernorm(x, axis=-1), ctx_2048, L1_xattn_Wq, L1_xattn_bq, L1_xattn_Wk, L1_xattn_bk, L1_xattn_Wv, L1_xattn_bv, L1_xattn_Wo, L1_xattn_bo)
    x = x + _L1_ffn_ref(_layernorm(x, axis=-1), L1_ffn_W_up, L1_ffn_W_gate, L1_ffn_W_down)
    return x

_drawn_inputs = setup_inputs


def setup_inputs(seed=0):
    import zlib

    import numpy as np

    out = dict(_drawn_inputs(seed))
    spreads = {'L0_ffn_rgb': (0.0, 0.8),
     'L0_ffn_rb1': (0.0, 0.8),
     'L0_ffn_rb2': (0.0, 0.8),
     'L0_ffn_sgb': (0.0, 0.8),
     'L0_ffn_sb1': (0.0, 0.8),
     'L0_ffn_sb2': (0.0, 0.497),
     'L1_xattn_bq': (0.0, 1.319),
     'L1_xattn_bk': (0.0, 2.0),
     'L1_xattn_bv': (0.0, 0.708)}
    factors = {'L0_ffn_rg': 8.0,
     'L0_ffn_rw1': 8.0,
     'L0_ffn_rw2': 8.0,
     'L0_ffn_sg': 6.286,
     'L0_ffn_sw1': 6.047,
     'L0_ffn_sw2': 5.788,
     'L1_xattn_bo': 23.932,
     'L1_ffn_W_up': 3.262,
     'L1_ffn_W_gate': 3.152,
     'L1_ffn_W_down': 3.156}
    for name, (base, spread) in spreads.items():
        noise = np.random.default_rng([zlib.crc32(name.encode()), seed]).standard_normal(out[name].shape)
        drawn = base * np.exp(spread * noise) if base else spread * noise
        out[name] = jnp.asarray(drawn.astype(out[name].dtype))
    for name, factor in factors.items():
        out[name] = (out[name] * factor).astype(out[name].dtype)
    return out
```

```python
from contextlib import ExitStack

import numpy as np

import concourse.bass as bass
from concourse import mybir

ALU = mybir.AluOpType
ACT = mybir.ActivationFunctionType
AX = mybir.AxisListType
F32 = mybir.dt.float32
BF16 = mybir.dt.bfloat16
F16 = mybir.dt.float16
U32 = mybir.dt.uint32

P = 128
B = 16
D = 256
DB = D // P
GB = 4
NG = B // GB
TOK = GB * P
E = 16
ES = 18
F = 128
DE = 1024
EB = DE // P
H = 16
KV = 4
HD = P // H
T = D
TERMS = 3
ROWS = 48
MROW = ROWS
UNITS = GB * KV
LAG = 6
STEPS = UNITS + LAG + 1
QUANT_AT = (3, 7, 11)
LN_EPS = 1e-5
QUANT_EPS = 1e-8


BANKS = 8
PV_BANK = 7


def tile_order():
    pairs = range(GB // 2)
    t = [("k1", 0, 1, "dve", 2), ("v1", 0, 1, "dve", 1)]
    t += [("xt", d, 1, "act", 1) for d in range(DB)]
    t += [("q", e, 1, "act", 1) for e in range(DB)]
    t += [("k", e, 1, "dve", 1) for e in range(DB)]
    t += [("v", n, 1, "dve", 1) for n in pairs]
    t += [("s", n, 1, "act", 2) for n in pairs]
    t += [("pt", n, 1, "dve", 1) for n in pairs]
    t += [("at", n, 1, "act", 1) for n in pairs]
    t += [("o", n, 1, "dve", 2) for n in pairs]
    t += [("xt2", d, 1, "act", 1) for d in range(DB)]
    t += [("route", 0, 1, "act", 1), ("gate", 0, 1, "act", 1), ("up", 0, 1, "dve", 1)]
    t += [("gate", 1, 1, "act", 1), ("up", 1, 1, "dve", 1), ("ct", 0, 1, "act", 1)]
    t += [("bias2", n, 1, "dve", 1) for n in pairs]
    for e in range(ES):
        t += [("down", 2 * e + n, 1, "dve", 2) for n in pairs]
        if e + 2 < ES:
            t += [("gate", e + 2, 1, "act", 1), ("up", e + 2, 1, "dve", 1)]
    for n in pairs:
        t += [("q1", n, 1, "dve", 1), ("q1r", n, 1, "dve", 1)]
    for s in range(STEPS):
        if s < UNITS:
            t += [("smax", 4 * s + h, 1, "dve", 1) for h in range(KV)]
        if s % KV == 0 and 0 <= s // KV - 1 < GB:
            t += [("mt", s // KV - 1, 1, "dve", 2)]
        if 0 <= s - LAG < UNITS:
            t += [("st", 2 * (s - LAG) + kb, 2, "act", 1) for kb in range(2)]
        if 0 <= s - LAG - 1 < UNITS and (s - LAG - 1) % 2:
            t += [("pv", (s - LAG - 1) // 2, 0, "act", 1)]
    t += [("o1", n, 1, "dve", 1) for n in pairs]
    t += [("xt4", d, 1, "dve", 1) for d in range(DB)]
    for e in range(EB):
        t += [("up4", e, 1, "act", 1), ("gate4", e, 1, "dve", 1)]
    t += [("down4", n, 1, "dve", 2) for n in pairs]
    return t


class Ring:

    def __init__(self):
        self.bank, self.full, self.empty, self.after = {}, {}, {}, {}
        self.counts = {"act": 0, "dve": 0}
        order, places, at = tile_order(), [], 0
        for stage, n, banks, engine, parts in order:
            if at % PV_BANK + banks > PV_BANK:
                at += PV_BANK - at % PV_BANK
            places.append([PV_BANK] if not banks else [(at + b) % PV_BANK for b in range(banks)])
            at += banks
            self.counts[engine] += parts
            self.bank[stage, n] = places[-1][0]
            self.full[stage, n] = len(places)
            self.empty[stage, n] = (engine, self.counts[engine])
        owner = {}
        for again in (False, True):
            for (stage, n, *_), banks in zip(order, places):
                if again:
                    self.after[stage, n] = sorted({(not owner[b][0], *owner[b][1:]) for b in banks})
                for b in banks:
                    owner[b] = (again, stage, n)
        self.n_full = len(places)


RING = Ring()
GROUP_TILES = RING.n_full
PARTS = {stage: parts for stage, _, _, _, parts in tile_order()}


def rope_tables():
    inv = (np.float32(1.0) / np.float32(10000.0) ** (np.arange(0, HD, 2, dtype=np.float32) / np.float32(HD)))
    freq = np.arange(T, dtype=np.float32)[:, None] * inv.astype(np.float32)[None, :]
    emb = np.concatenate([freq, freq], axis=-1).astype(np.float32)
    cos, sin = np.cos(emb).astype(np.float32), np.sin(emb).astype(np.float32)
    sin[:, : HD // 2] = -sin[:, : HD // 2]
    q = [np.repeat(a.T, H, axis=0) for a in (cos, sin)]
    k = [np.tile(np.repeat(a.T, KV, axis=0), (GB, 1)) for a in (cos, sin)]
    return np.ascontiguousarray(np.stack(q + k, axis=1))


def build(nc, a):
    with ExitStack() as ctx:
        def sb(name, shape, dt=F32):
            return ctx.enter_context(nc.sbuf_tensor(name, shape, dt))

        class Sem:

            def __init__(self, name, per, step=1):
                self.sem, self.per, self.step = ctx.enter_context(nc.semaphore(name)), per, step

            def at(self, g, n):
                return (g * self.per + n) * self.step

        ident = sb("ident", [P, P])
        wq0, wk0, wv0, wo0 = (sb(f"w{n}0", [P, DB, D]) for n in "qkvo")
        wa = sb("wa", [P, DB, E])
        wg = sb("wg", [P, ES, DB, F])
        wu = sb("wu", [P, ES, DB, F])
        w2 = sb("w2", [P, ES, D])
        gb = sb("gb", [P, ES])
        ub = sb("ub", [P, ES])
        b2 = sb("b2", [ES, D])
        wq1, wq1r = sb("wq1", [P, P]), sb("wq1r", [P, P])
        wk1, wk1r, wv1 = sb("wk1", [P, KV * HD]), sb("wk1r", [P, KV * HD]), sb("wv1", [P, KV * HD])
        bq1 = sb("bq1", [P, 2])
        bk1 = sb("bk1", [P, 2])
        bv1 = sb("bv1", [P, KV * HD])
        wo1 = sb("wo1", [P, P])
        bo1 = sb("bo1", [P, 1])
        rope = sb("rope", [P, 4, T])
        tern = [sb(f"tern_{n}", [P, 2048], F16) for n in ("up", "gate", "down")]
        iota_e = sb("iota_e", [P, E])
        wsum = sb("wsum", [P, 3, 2])
        wscale = sb("wscale", [P, 3])
        half = sb("half", [P, 3, 2])
        ffn_c = sb("ffn_c", [P, 4])
        x_in = sb("x_in", [P, GB, D])
        ctx_sb = sb("ctx_sb", [P, GB, D])
        kcat = sb("kcat", [P, DB, GB, 2, P])
        stats = sb("stats", [P, GB, 6])
        mv = sb("mv", [P, GB, 2])
        rstd, var, minus_half = sb("rstd", [P, GB]), sb("var", [P, GB]), sb("minus_half", [P, GB])
        xn = sb("xn", [P, GB, D])
        xnT = sb("xnT", [P, DB, TOK])
        nmax = sb("nmax", [P, GB])
        rsum = sb("rsum", [P, GB])
        rinv = sb("rinv", [P, GB])
        acc = sb("acc", [P, GB, D])
        x3 = sb("x3", [P, GB, D])
        el = sb("el", [P, GB, E])
        el1 = sb("el1", [P, GB, E])
        prob = sb("prob", [P, GB, E])
        top = sb("top", [P, GB, 8])
        topi = sb("topi", [P, GB, 8], U32)
        topf = sb("topf", [P, GB, 2])
        psum2 = sb("psum2", [P, GB, 1])
        pinv = sb("pinv", [P, GB, 1])
        topw = sb("topw", [P, GB, 2])
        hot0, hot1 = sb("hot0", [P, GB, E]), sb("hot1", [P, GB, E])
        comb = sb("comb", [P, GB, ES])
        ksplit = sb("ksplit", [P, TERMS, T], BF16)
        KS = sb("KS", [P, GB, KV, T], BF16)
        Vs = sb("Vs", [P, GB, 2, KV, 32])
        M = sb("M", [P, GB, 2 * H])
        ps = ctx.enter_context(nc.psum_tensor("ps", [P, BANKS, 512], F32))

        def part(region, at, size, dt=F32):
            v = region[:, at:at + size]
            return v if dt == F32 else v.bitcast(dt)

        r1 = sb("r1", [P, 8192])
        g_sb = part(r1, 6144, 1024).rearrange("p (a b) -> p a b", a=2)
        y_sb = part(r1, 7168, 1024).rearrange("p (a b) -> p a b", a=2)
        s_sb = part(r1, 0, 1024).rearrange("p (a b) -> p a b", a=2)
        h_sb = part(r1, 1024, 1024).rearrange("p (a b) -> p a b", a=2)
        hhi = part(r1, 2048, 2048, F16).rearrange("p (a b) -> p a b", a=EB)
        hlo = part(r1, 4096, 2048, F16).rearrange("p (a b) -> p a b", a=EB)
        QS = part(r1, 0, 8192, BF16).rearrange("p (b h k) -> p b h k", b=GB, h=H)
        r2 = sb("r2", [P, 4096])
        qT = part(r2, 0, 1024).rearrange("p (a b) -> p a b", a=DB)
        v_sb = part(r2, 1024, 1024).rearrange("p (a b) -> p a b", a=GB)
        pr = part(r2, 2048, 1024).rearrange("p (a b) -> p a b", a=GB)
        prT = part(r2, 3072, 1024).rearrange("p (a b c) -> p a b c", a=GB, b=2)
        PT = part(r2, 0, 4096).rearrange("p (n a b) -> p n a b", n=4, a=2)
        r3 = sb("r3", [P, 1024])
        atT = part(r3, 0, 1024).rearrange("p (a b c) -> p a b c", a=GB, b=DB)
        combT = part(r3, 0, TOK)[0:ES, :]
        mhi = part(r3, 512, 256, BF16)[0:2 * H, :].rearrange("p (b k) -> p b k", b=GB)
        mlo = part(r3, 768, 256, BF16)[0:2 * H, :].rearrange("p (b k) -> p b k", b=GB)
        xhi = part(r3, 0, 512, F16).rearrange("p (a b) -> p a b", a=DB)
        xlo = part(r3, 512, 512, F16).rearrange("p (a b) -> p a b", a=DB)
        r4 = sb("r4", [P, 2048])
        raw = part(r4, 0, 2048)
        qr = part(r4, 0, 1024).rearrange("p (r a b) -> p r a b", r=2, a=2)
        qres = part(r4, 1024, 1024).rearrange("p (a b) -> p a b", a=GB)
        U = part(r4, 1024, 1024).rearrange("p (a b) -> p a b", a=KV)
        r5 = sb("r5", [P, 1536])
        tpos = part(r5, 0, 1024, F16)
        qsplit = part(r5, 0, 1536, BF16).rearrange("p (b t k) -> p b t k", b=GB, t=TERMS)
        r6 = sb("r6", [P, 2048])
        kr = part(r6, 0, 768).rearrange("p (a b) -> p a b", a=3)
        kres = part(r6, 768, 256)
        num = part(r6, 0, 1024).rearrange("p (a b) -> p a b", a=GB)
        den = part(r6, 1024, 1024).rearrange("p (a b) -> p a b", a=GB)
        x_res = acc
        q_rot = y_out = x3

        qd = nc.dram_tensor("q_scratch", [GB, TERMS, P, T], BF16, kind="Internal").ap()
        kd = nc.dram_tensor("k_scratch", [TERMS, GB, HD, KV, T], BF16, kind="Internal").ap()
        ud = nc.dram_tensor("pv_scratch", [GB, HD + 1, KV, KV, T], F32, kind="Internal").ap()

        w_attn0 = Sem("w_attn0", 4, 16)
        w_experts = Sem("w_experts", 7, 16)
        w_attn1 = Sem("w_attn1", 12, 16)
        raw_in = Sem("raw_in", 3, 16)
        consts = Sem("consts", 1)
        passed = Sem("passed", 0)
        zeroed = Sem("zeroed", 2)
        pads = Sem("pads", 4)
        abs_sums, abs_total = Sem("abs_sums", 3), Sem("abs_total", 3)
        quant_step, tern_done = Sem("quant_step", 12), Sem("tern_done", 3)
        ffn_consts = Sem("ffn_consts", 7)
        x_loaded, ctx_loaded = Sem("x_loaded", 1, 16), Sem("ctx_loaded", 1, 16)
        ctxT_loaded = Sem("ctxT_loaded", DB, 16)
        tiles_ready = Sem("tiles_ready", GROUP_TILES)
        act_emptied = Sem("act_emptied", RING.counts["act"])
        dve_emptied = Sem("dve_emptied", RING.counts["dve"])
        ln_stats = Sem("ln_stats", 4 * GB)
        ln_mv = Sem("ln_mv", 4)
        ln_var, ln_rstd = Sem("ln_var", 4), Sem("ln_rstd", 4)
        ln_done = Sem("ln_done", 4 * GB)
        neg_max = Sem("neg_max", GB // 2)
        sums_inv = Sem("sums_inv", 1)
        base_sum = Sem("base_sum", 1)
        route_step = Sem("route_step", 5 + GB)
        top_step = Sem("top_step", 2 * GB)
        hots = Sem("hots", 2 * GB)
        comb_done = Sem("comb_done", 1)
        kr_done, kres_done = Sem("kr_done", 1), Sem("kres_done", 1)
        k_hi = Sem("k_hi", 2)
        k_split_done = Sem("k_split_done", 1)
        k_stored, k_stacked = Sem("k_stored", 1, 16), Sem("k_stacked", 6, 16)
        q_rotated, q_res_done = Sem("q_rotated", 2), Sem("q_res_done", 2)
        q_hi = Sem("q_hi", GB)
        pv_even = Sem("pv_even", UNITS // 2)
        x_hi = Sem("x_hi", DB)
        q_split_done = Sem("q_split_done", 2)
        q_cleared = Sem("q_cleared", GB)
        q_stored = [Sem(f"q_stored{n}", 2, 16) for n in range(GB // 2)]
        q_stacked = [Sem(f"q_stacked{j}", 3, 16) for j in range(GB)]
        m_stacked = [Sem(f"m_stacked{j}", 2, 16) for j in range(GB)]
        u_stored = Sem("u_stored", KV * GB, 16)
        nd_loaded = [Sem(f"nd_loaded{j}", 2, 16) for j in range(GB)]
        den_inv, normed = Sem("den_inv", GB), Sem("normed", GB)
        h_hi, h_lo = Sem("h_hi", EB), Sem("h_lo", EB)
        stored = Sem("stored", 1, 16)

        block = ctx.enter_context(nc.Block())

        def tile(stage, n, banks=1):
            at = RING.bank[stage, n]
            return ps[:, at, :] if banks == 1 else ps[:, at:at + banks, :].rearrange("p a b -> p (a b)")

        def full(g, stage, n):
            return g * tiles_ready.per + RING.full[stage, n]

        def empty(g, stage, n, part=None):
            engine, count = RING.empty[stage, n]
            per = (act_emptied if engine == "act" else dve_emptied).per
            return g * per + (count if part is None else count - PARTS[stage] + part)

        def before(g, again, stage, n):
            for earlier, st, k in RING.after[stage, n]:
                if again or not earlier:
                    yield (act_emptied if RING.empty[st, k][0] == "act" else dve_emptied).sem, \
                        empty(g - 1 if earlier else g, st, k)

        def weighted(g, u):
            if u % 2:
                return tiles_ready.sem, full(g, "pv", u // 2)
            return pv_even.sem, pv_even.at(g, u // 2 + 1)

        @block.sync
        def _(sp):
            def load_x(g):
                sp.dma_start(x_in[:], a["x"][bass.ts(g, GB)].rearrange("b s d -> s b d")).then_inc(x_loaded.sem, 16)

            def load_ctx(g):
                sp.dma_start(ctx_sb[:], a["ctx"][bass.ts(g, GB)].rearrange("b s d -> s b d")).then_inc(ctx_loaded.sem, 16)
                for eb in range(DB):
                    sp.dma_start(kcat[:, eb, :, 0, :], a["ctxT"][bass.ts(g, GB), eb].rearrange("b p k -> p b k"))\
                        .then_inc(ctxT_loaded.sem, 16)

            load_x(0)
            load_ctx(0)
            for dst, src in ((wq0, "wq0"), (wk0, "wk0"), (wv0, "wv0"), (wo0, "wo0")):
                sp.dma_start(dst[:], a[src].rearrange("(b p) e -> p b e", p=P)).then_inc(w_attn0.sem, 16)
            for dst, src in ((wq1, "wq1"), (wq1r, "wq1r"), (wk1, "wk1"), (wk1r, "wk1r"), (wv1, "wv1"), (bq1, "bq1"),
                             (bk1, "bk1"), (wo1, "wo1"), (bo1, "bo1"), (rope, "rope")):
                sp.dma_start(dst[:], a[src]).then_inc(w_attn1.sem, 16)
            sp.dma_start(bv1[:], a["bv1"].broadcast_to([P, KV * HD])).then_inc(w_attn1.sem, 16)
            sp.dma_start(iota_e[:], a["iota"].broadcast_to([P, E])).then_inc(w_attn1.sem, 16)
            sp.dma_start(wa[:], a["wa"].rearrange("(b p) e -> p b e", p=P)).then_inc(w_experts.sem, 16)
            for dst, src in ((gb, "gb"), (ub, "ub")):
                sp.dma_start(dst[:], a[src]).then_inc(w_experts.sem, 16)
            sp.dma_start(b2[:], a["b2"]).then_inc(w_experts.sem, 16)
            for dst, src in ((wg, "wg"), (wu, "wu")):
                sp.dma_start(dst[:], a[src].rearrange("e (b p) f -> p (e b) f", p=P)).then_inc(w_experts.sem, 16)
            sp.dma_start(w2[:], a["w2"].rearrange("e f d -> f e d")).then_inc(w_experts.sem, 16)
            def body(g, again, last=False):
                sp.wait_ge(k_split_done.sem, k_split_done.at(g, 1))
                if again:
                    sp.wait_ge(k_stacked.sem, k_stacked.at(g - 1, 6))
                sp.dma_start(kd.rearrange("t b d h k -> (b d h) t k"), ksplit[:]).then_inc(k_stored.sem, 16)
                sp.wait_ge(k_stored.sem, k_stored.at(g, 1))
                if again:
                    sp.wait_ge(tiles_ready.sem, full(g - 1, "st", 2 * UNITS - 1))
                sp.wait_ge(pads.sem, pads.at(0, 4))
                for r, term in enumerate((0, 0, 0, 1, 1, 2)):
                    sp.dma_start(KS[8 * r:8 * r + 8, :, :, :].rearrange("d b h k -> d b (h k)"),
                                 kd[term].rearrange("b d h k -> d b (h k)")).then_inc(k_stacked.sem, 16)
                if not last:
                    sp.wait_ge(tiles_ready.sem, full(g, "at", GB // 2 - 1))
                    load_ctx(g + 1)
                    sp.wait_ge(dve_emptied.sem, empty(g, "o", GB // 2 - 1))
                    load_x(g + 1)
                for n in range(GB // 2):
                    sp.wait_ge(q_split_done.sem, q_split_done.at(g, n + 1))
                    for j in (2 * n, 2 * n + 1):
                        if again:
                            sp.wait_ge(q_stacked[j].sem, q_stacked[j].at(g - 1, 3))
                        sp.dma_start(qd[j].rearrange("t p k -> p t k"), qsplit[:, j, :, :])\
                            .then_inc(q_stored[n].sem, 16)
                    sp.wait_ge(q_stored[n].sem, q_stored[n].at(g, 2))
                    if again:
                        sp.sem_inc(passed.sem, 1)
                    for j in (2 * n, 2 * n + 1):
                        flat = qd[j].rearrange("t (d h) k -> (t d) (h k)", h=H)
                        sp.wait_ge(q_cleared.sem, q_cleared.at(g, j + 1))
                        for r0, rows in ((0, 3), (3, 2), (5, 1)):
                            sp.dma_start(QS[8 * r0:8 * r0 + 8 * rows, j, :, :].rearrange("r h k -> r (h k)"),
                                         flat[0:8 * rows]).then_inc(q_stacked[j].sem, 16)
                for s in range(KV + 1, STEPS + 1):
                    if s % KV == 1 and s // KV - 1 < GB:
                        j = s // KV - 1
                        for r, part in enumerate((mhi, mlo)):
                            sp.wait_ge(dve_emptied.sem, empty(g, "mt", j, r + 1))
                            sp.dma_start(QS[MROW + r:MROW + r + 1, j, :, :].rearrange("r h k -> r (h k)"),
                                         part[:, j, :]).then_inc(m_stacked[j].sem, 16)
                    u = s - LAG - 1
                    if u >= 0 and u % KV == KV - 1:
                        j = u // KV
                        sp.wait_ge(act_emptied.sem, empty(g, "pv", 2 * j + 1))
                        if again:
                            sp.wait_ge(nd_loaded[j].sem, nd_loaded[j].at(g - 1, 2))
                        for q in range(KV):
                            sp.dma_start(ud[j, :, q, :, :].rearrange("r h k -> r (h k)"),
                                         U[32 * q:32 * q + HD + 1, :, :].rearrange("r h k -> r (h k)"))\
                                .then_inc(u_stored.sem, 16)
                        sp.wait_ge(u_stored.sem, u_stored.at(g, KV * (j + 1)))
                        if again:
                            sp.sem_inc(passed.sem, 1)
                        if again:
                            sp.wait_ge(tiles_ready.sem, full(g - 1, "o1", j // 2))
                        sp.dma_start(num[:, j, :], ud[j, 0:HD].rearrange("r q h k -> (r q h) k"))\
                            .then_inc(nd_loaded[j].sem, 16)
                        sp.dma_start(den[:, j, :], ud[j, HD].rearrange("(o q) h k -> o (q h) k", o=1)
                                     .broadcast_to([HD, H, T])).then_inc(nd_loaded[j].sem, 16)
                sp.wait_ge(dve_emptied.sem, empty(g, "down4", GB // 2 - 1))
                sp.dma_start(a["out"][bass.ts(g, GB)].rearrange("b s d -> s b d"), y_out[:]).then_inc(stored.sem, 16)

            body(0, False)
            with sp.Fori(1, NG - 1) as g:
                body(g, True)
            body(NG - 1, True, last=True)
            sp.wait_ge(stored.sem, stored.at(NG - 1, 1))

        @block.gpsimd
        def _(pool):
            pool.memset(ident[:], 0.0).then_inc(zeroed.sem, 1)
            pool.wait_ge(zeroed.sem, zeroed.at(0, 1))
            pool.affine_select(out=ident[:], in_=ident[:], compare_op=ALU.not_equal, fill=1.0, base=0,
                               pattern=[[-1, P]], channel_multiplier=1).then_inc(consts.sem, 1)
            pool.memset(KS[:], 1.0).then_inc(pads.sem, 1)
            pool.memset(Vs[:], 0.0).then_inc(zeroed.sem, 1)
            pool.wait_ge(zeroed.sem, zeroed.at(0, 2))
            pool.memset(Vs[:, :, :, :, HD:HD + 1], 1.0).then_inc(pads.sem, 1)
            pool.memset(comb[:, :, E:ES], 1.0).then_inc(pads.sem, 1)
            pool.memset(minus_half[:], -0.5).then_inc(pads.sem, 1)
            pool.wait_ge(pads.sem, pads.at(0, 4))

            def quantise_sums():
                for n, src in enumerate(("wup", "wgate", "wdown")):
                    if n:
                        pool.wait_ge(tern_done.sem, tern_done.at(0, n))
                    pool.dma_start(raw, a[src]).then_inc(raw_in.sem, 16)
                    pool.wait_ge(abs_sums.sem, abs_sums.at(0, n + 1))
                    pool.partition_all_reduce(wsum[:, n, 1:2], wsum[:, n, 0:1], P, bass.bass_isa.ReduceOp.add)\
                        .then_inc(abs_total.sem, 1)

            def body(g, again):
                def rsqrt(n):
                    pool.wait_ge(ln_mv.sem, ln_mv.at(g, n + 1))
                    if again:
                        pool.sem_inc(passed.sem, 1)
                    pool.tensor_scalar(var[:], mv[:, :, 1], LN_EPS, None, ALU.add).then_inc(ln_var.sem, 1)
                    pool.wait_ge(ln_var.sem, ln_var.at(g, n + 1))
                    pool.tensor_tensor(rstd[:], var[:], minus_half[:], ALU.pow).then_inc(ln_rstd.sem, 1)

                def clear(j):
                    pool.memset(QS[:, j, :, :], 0.0).then_inc(q_cleared.sem, 1)

                rsqrt(0)
                rsqrt(1)
                if again:
                    pool.wait_ge(tiles_ready.sem, full(g - 1, "down4", GB // 2 - 1))
                    pool.sem_inc(passed.sem, 1)
                for j in range(GB - 1):
                    clear(j)
                if not again:
                    quantise_sums()
                pool.wait_ge(tiles_ready.sem, full(g, "down", 2 * ES - 1))
                if again:
                    pool.sem_inc(passed.sem, 1)
                clear(GB - 1)
                rsqrt(2)
                rsqrt(3)
                for e in range(EB):
                    pool.wait_ge(h_hi.sem, h_hi.at(g, e + 1))
                    if e == 0:
                        if again:
                            pool.wait_ge(tiles_ready.sem, full(g - 1, "down4", GB // 2 - 1))
                    pool.tensor_tensor(hlo[:, e, :], h_sb[:, e % 2, :], hhi[:, e, :], ALU.subtract)\
                        .then_inc(h_lo.sem, 1)

            body(0, False)
            with pool.Fori(1, NG) as g:
                body(g, True)

        @block.scalar
        def _(act):
            def body(g, again):
                for d in range(DB):
                    act.wait_ge(tiles_ready.sem, full(g, "xt", d))
                    act.activation(xnT[:, d, :], tile("xt", d), ACT.Copy).then_inc(act_emptied.sem, 1)
                for e in range(DB):
                    act.wait_ge(tiles_ready.sem, full(g, "q", e))
                    act.activation(qT[:, e, :], tile("q", e), ACT.Copy, scale=1.0 / 16.0)\
                        .then_inc(act_emptied.sem, 1)
                for n in range(2):
                    rotated = kres_done if n else kr_done
                    act.wait_ge(rotated.sem, rotated.at(g, 1))
                    if n == 0:
                        if again:
                            act.wait_ge(k_stored.sem, k_stored.at(g - 1, 1))
                    act.activation(ksplit[:, n, :], kr[:, 2, :] if n == 0 else kres, ACT.Copy)\
                        .then_inc(k_hi.sem, 1)
                for j in range(GB):
                    act.wait_ge(neg_max.sem, neg_max.at(g, j // 2 + 1))
                    t = tile("s", j // 2)[:, (j % 2) * D:(j % 2 + 1) * D]
                    i = act.activation(pr[:, j, :], t, ACT.Exp, bias=nmax[:, j:j + 1], accum_out=rsum[:, j:j + 1])
                    i.then_inc(act_emptied.sem, 1)
                for n in range(GB // 2):
                    act.wait_ge(tiles_ready.sem, full(g, "at", n))
                    act.activation(atT[:, 2 * n:2 * n + 2, :, :].rearrange("p a b c -> p (a b c)"), tile("at", n),
                                   ACT.Copy).then_inc(act_emptied.sem, 1)
                for d in range(DB):
                    act.wait_ge(tiles_ready.sem, full(g, "xt2", d))
                    act.activation(xnT[:, d, :], tile("xt2", d), ACT.Copy).then_inc(act_emptied.sem, 1)
                act.wait_ge(tiles_ready.sem, full(g, "route", 0))
                act.activation(el[:], tile("route", 0)[:, 0:GB * E].rearrange("p (b e) -> p b e", b=GB), ACT.Exp,
                               scale=-1.0).then_inc(act_emptied.sem, 1)

                def gelu(e):
                    act.wait_ge(tiles_ready.sem, full(g, "gate", e))
                    if e == 0 and not again:
                        act.wait_ge(w_experts.sem, w_experts.at(0, 7))
                    if e >= 2:
                        act.wait_ge(dve_emptied.sem, empty(g, "up", e - 2))
                    else:
                        if again:
                            act.wait_ge(dve_emptied.sem, empty(g - 1, "up", ES - 2 + e))
                    act.activation(g_sb[:, e % 2, :], tile("gate", e), ACT.Gelu, bias=gb[:, e:e + 1])\
                        .then_inc(act_emptied.sem, 1)

                gelu(0)
                gelu(1)
                act.wait_ge(tiles_ready.sem, full(g, "ct", 0))
                act.activation(combT, tile("ct", 0)[0:ES, :], ACT.Copy).then_inc(act_emptied.sem, 1)
                for e in range(2, ES):
                    gelu(e)
                for n in range(GB // 2):
                    act.wait_ge(q_rotated.sem, q_rotated.at(g, n + 1))
                    if again:
                        act.wait_ge(q_stored[n].sem, q_stored[n].at(g - 1, 2))
                    for k in range(2):
                        if k:
                            act.wait_ge(q_res_done.sem, q_res_done.at(g, n + 1))
                        act.activation(qsplit[:, 2 * n:2 * n + 2, k, :],
                                       (q_rot if k == 0 else qres)[:, 2 * n:2 * n + 2, :], ACT.Copy)\
                            .then_inc(q_hi.sem, 1)
                for s in range(STEPS):
                    u = s - LAG
                    if 0 <= u < UNITS:
                        for kb in range(2):
                            act.wait_ge(tiles_ready.sem, full(g, "st", 2 * u + kb))
                            if u >= 2 or again:
                                used, count = weighted(g if u >= 2 else g - 1, (u - 2) % UNITS)
                                act.wait_ge(used, count)
                            act.activation(PT[:, 2 * (u % 2) + kb, :, :].rearrange("p a b -> p (a b)"),
                                           tile("st", 2 * u + kb, 2), ACT.Exp, scale=float(HD) ** -0.5)\
                                .then_inc(act_emptied.sem, 1)
                    u = s - LAG - 1
                    if u >= 0 and u % 2 == 1:
                        act.wait_ge(tiles_ready.sem, full(g, "pv", u // 2))
                        j = u // KV
                        if u % KV == 1:
                            if j or again:
                                act.wait_ge(u_stored.sem, u_stored.at(g, KV * j))
                        act.activation(U[:, u % KV - 1:u % KV + 1, :].rearrange("p h k -> p (h k)"),
                                       tile("pv", u // 2), ACT.Copy).then_inc(act_emptied.sem, 1)
                for d in range(DB):
                    act.wait_ge(tiles_ready.sem, full(g, "xt4", d))
                    act.activation(xhi[:, d, :], tile("xt4", d), ACT.Copy).then_inc(x_hi.sem, 1)
                if not again:
                    act.wait_ge(ffn_consts.sem, ffn_consts.at(0, 7))
                for e in range(EB):
                    act.wait_ge(tiles_ready.sem, full(g, "up4", e))
                    if e >= 2 or again:
                        act.wait_ge(dve_emptied.sem, empty(g if e >= 2 else g - 1, "gate4", (e - 2) % EB))
                    act.activation(s_sb[:, e % 2, :], tile("up4", e), ACT.Silu, scale=ffn_c[:, 0:1])\
                        .then_inc(act_emptied.sem, 1)
                    if e:
                        hidden_hi(g, again, e - 1)
                hidden_hi(g, again, EB - 1)

            def hidden_hi(g, again, e):
                act.wait_ge(dve_emptied.sem, empty(g, "gate4", e))
                if e == 0:
                    if again:
                        act.wait_ge(tiles_ready.sem, full(g - 1, "down4", GB // 2 - 1))
                act.activation(hhi[:, e, :], h_sb[:, e % 2, :], ACT.Copy).then_inc(h_hi.sem, 1)

            body(0, False)
            with act.Fori(1, NG) as g:
                body(g, True)

        @block.tensor
        def _(pe):
            def done(i):
                i.then_inc(tiles_ready.sem, 1)

            def mm(out, lhsT, rhs, first=True, last=True):
                return pe.matmul(out, lhsT, rhs, start=first, stop=last)

            def transposes(g, again, stage, ln):
                for d in range(DB):
                    for held, count in before(g, again, stage, d):
                        pe.wait_ge(held, count)
                    for j in range(GB):
                        if d == 0:
                            pe.wait_ge(ln_done.sem, ln_done.at(g, GB * ln + j + 1))
                        i = pe.transpose(tile(stage, d)[:, j * P:(j + 1) * P], xn[:, j, d * P:(d + 1) * P], ident[:])
                    done(i)

            def body(g, again):
                for held, count in before(g, again, "k1", 0):
                    pe.wait_ge(held, count)
                pe.wait_ge(ctx_loaded.sem, ctx_loaded.at(g, 1))
                if not again:
                    pe.wait_ge(w_attn1.sem, w_attn1.at(0, 12))
                    pe.wait_ge(w_attn0.sem, w_attn0.at(0, 4))
                    pe.wait_ge(consts.sem, consts.at(0, 1))
                for r, w in enumerate((wk1, wk1r)):
                    for j in range(GB):
                        i = mm(tile("k1", 0)[32 * j:32 * j + 32, r * T:(r + 1) * T], w[:], ctx_sb[:, j, :])
                done(i)
                for held, count in before(g, again, "v1", 0):
                    pe.wait_ge(held, count)
                for j in range(GB):
                    for kb in range(2):
                        n = 2 * j + kb
                        i = mm(tile("v1", 0)[:, 32 * n:32 * n + 32], ctx_sb[:, j, kb * P:(kb + 1) * P], wv1[:])
                done(i)
                transposes(g, again, "xt", 0)
                for stage, w in (("q", wq0), ("k", wk0)):
                    for e in range(DB):
                        for held, count in before(g, again, stage, e):
                            pe.wait_ge(held, count)
                        if stage == "q" and e == 0:
                            pe.wait_ge(act_emptied.sem, empty(g, "xt", DB - 1))
                        for d in range(DB):
                            i = mm(tile(stage, e), w[:, d, e * P:(e + 1) * P], xnT[:, d, :], d == 0, d == DB - 1)
                        done(i)
                for n in range(GB // 2):
                    for held, count in before(g, again, "v", n):
                        pe.wait_ge(held, count)
                    for j in (2 * n, 2 * n + 1):
                        for d in range(DB):
                            i = mm(tile("v", n)[:, (j % 2) * D:(j % 2 + 1) * D], xnT[:, d, j * P:(j + 1) * P],
                                   wv0[:, d, :], d == 0, d == DB - 1)
                    done(i)
                for n in range(GB // 2):
                    for held, count in before(g, again, "s", n):
                        pe.wait_ge(held, count)
                    if n == 0:
                        pe.wait_ge(act_emptied.sem, empty(g, "q", DB - 1))
                        pe.wait_ge(dve_emptied.sem, empty(g, "k", DB - 1))
                        pe.wait_ge(ctxT_loaded.sem, ctxT_loaded.at(g, DB))
                    for j in (2 * n, 2 * n + 1):
                        for e in range(DB):
                            i = mm(tile("s", n)[:, (j % 2) * D:(j % 2 + 1) * D], qT[:, e, j * P:(j + 1) * P],
                                   kcat[:, e, j, :, :].rearrange("p a b -> p (a b)"), e == 0, e == DB - 1)
                    done(i)
                for n in range(GB // 2):
                    for held, count in before(g, again, "pt", n):
                        pe.wait_ge(held, count)
                    for j in (2 * n, 2 * n + 1):
                        pe.wait_ge(act_emptied.sem, empty(g, "s", n, j % 2 + 1))
                        for kb in range(2):
                            i = pe.transpose(tile("pt", n)[:, (j % 2) * D + kb * P:(j % 2) * D + (kb + 1) * P],
                                             pr[:, j, kb * P:(kb + 1) * P], ident[:])
                    done(i)
                for n in range(GB // 2):
                    for held, count in before(g, again, "at", n):
                        pe.wait_ge(held, count)
                    pe.wait_ge(dve_emptied.sem, empty(g, "pt", n))
                    for j in (2 * n, 2 * n + 1):
                        for d in range(DB):
                            for kb, v in enumerate((ctx_sb, v_sb)):
                                i = mm(tile("at", n)[:, (j % 2) * D + d * P:(j % 2) * D + (d + 1) * P],
                                       v[:, j, d * P:(d + 1) * P], prT[:, j, kb, :], kb == 0, kb == 1)
                    done(i)
                for n in range(GB // 2):
                    for held, count in before(g, again, "o", n):
                        pe.wait_ge(held, count)
                    pe.wait_ge(act_emptied.sem, empty(g, "at", n))
                    for j in (2 * n, 2 * n + 1):
                        for d in range(DB):
                            i = mm(tile("o", n)[:, (j % 2) * D:(j % 2 + 1) * D], atT[:, j, d, :], wo0[:, d, :],
                                   d == 0, d == DB - 1)
                    done(i)
                transposes(g, again, "xt2", 1)
                for held, count in before(g, again, "route", 0):
                    pe.wait_ge(held, count)
                pe.wait_ge(act_emptied.sem, empty(g, "xt2", DB - 1))
                if not again:
                    pe.wait_ge(w_experts.sem, w_experts.at(0, 7))
                for j in range(GB):
                    for d in range(DB):
                        i = mm(tile("route", 0)[:, j * E:(j + 1) * E], xnT[:, d, j * P:(j + 1) * P], wa[:, d, :],
                               d == 0, d == DB - 1)
                done(i)

                def up(e):
                    for stage, w in (("gate", wg), ("up", wu)):
                        for held, count in before(g, again, stage, e):
                            pe.wait_ge(held, count)
                        for d in range(DB):
                            i = mm(tile(stage, e), w[:, e, d, :], xnT[:, d, :], d == 0, d == DB - 1)
                        done(i)

                up(0)
                up(1)
                for held, count in before(g, again, "ct", 0):
                    pe.wait_ge(held, count)
                pe.wait_ge(comb_done.sem, comb_done.at(g, 1))
                for j in range(GB):
                    i = pe.transpose(tile("ct", 0)[0:ES, j * P:(j + 1) * P], comb[:, j, :], ident[:])
                done(i)
                for n in range(GB // 2):
                    for held, count in before(g, again, "bias2", n):
                        pe.wait_ge(held, count)
                    pe.wait_ge(act_emptied.sem, empty(g, "ct", 0))
                    for j in (2 * n, 2 * n + 1):
                        i = mm(tile("bias2", n)[:, (j % 2) * D:(j % 2 + 1) * D], combT[:, j * P:(j + 1) * P], b2[:])
                    done(i)
                for e in range(ES):
                    pe.wait_ge(dve_emptied.sem, empty(g, "up", e))
                    for n in range(GB // 2):
                        for held, count in before(g, again, "down", 2 * e + n):
                            pe.wait_ge(held, count)
                        for j in (2 * n, 2 * n + 1):
                            i = mm(tile("down", 2 * e + n)[:, (j % 2) * D:(j % 2 + 1) * D],
                                   y_sb[:, e % 2, j * P:(j + 1) * P], w2[:, e, :])
                        done(i)
                    if e + 2 < ES:
                        up(e + 2)
                for n in range(GB // 2):
                    for stage, w in (("q1", wq1), ("q1r", wq1r)):
                        for held, count in before(g, again, stage, n):
                            pe.wait_ge(held, count)
                        pe.wait_ge(ln_done.sem, ln_done.at(g, 2 * GB + 2 * n + 2))
                        done(mm(tile(stage, n), w[:], xn[:, 2 * n:2 * n + 2, :].rearrange("p a b -> p (a b)")))
                for s in range(STEPS):
                    if s < UNITS:
                        j, kv = divmod(s, KV)
                        if kv == 0:
                            pe.wait_ge(q_stacked[j].sem, q_stacked[j].at(g, 3))
                            if j == 0:
                                pe.wait_ge(k_stacked.sem, k_stacked.at(g, 6))
                                if not again:
                                    pe.wait_ge(pads.sem, pads.at(0, 4))
                        for hh in range(KV):
                            h = KV * kv + hh
                            for held, count in before(g, again, "smax", 4 * s + hh):
                                pe.wait_ge(held, count)
                            for qb in range(2):
                                i = mm(tile("smax", 4 * s + hh)[:, qb * T:(qb + 1) * T],
                                       QS[:, j, h, qb * P:(qb + 1) * P], KS[:, j, kv, :])
                            done(i)
                    if s % KV == 0 and s >= KV and s // KV - 1 < GB:
                        j = s // KV - 1
                        for held, count in before(g, again, "mt", j):
                            pe.wait_ge(held, count)
                        pe.wait_ge(dve_emptied.sem, empty(g, "smax", 16 * j + 15))
                        done(pe.transpose(tile("mt", j)[0:2 * H, 0:P], M[:, j, :], ident[:]))
                    u = s - LAG
                    if 0 <= u < UNITS:
                        j, kv = divmod(u, KV)
                        if kv == 0:
                            pe.wait_ge(m_stacked[j].sem, m_stacked[j].at(g, 2))
                        for kb in range(2):
                            for held, count in before(g, again, "st", 2 * u + kb):
                                pe.wait_ge(held, count)
                            for half in range(2):
                                i = mm(tile("st", 2 * u + kb, 2)[:, half * 512:(half + 1) * 512],
                                       KS[:, j, kv, kb * P:(kb + 1) * P],
                                       QS[:, j, KV * kv + 2 * half:KV * kv + 2 * half + 2, :]
                                       .rearrange("p a b -> p (a b)"))
                            done(i)
                    u = s - LAG - 1
                    if 0 <= u < UNITS:
                        j, kv = divmod(u, KV)
                        if u % 2 == 0:
                            for held, count in before(g, again, "pv", u // 2):
                                pe.wait_ge(held, count)
                        pe.wait_ge(act_emptied.sem, empty(g, "st", 2 * u + 1))
                        if u == 0:
                            pe.wait_ge(dve_emptied.sem, empty(g, "v1", 0))
                        for kb in range(2):
                            for hh in range(KV):
                                i = mm(tile("pv", u // 2)[32 * hh:32 * hh + 32, (u % 2) * T:(u % 2 + 1) * T],
                                       Vs[:, j, kb, kv, :], PT[:, 2 * (u % 2) + kb, hh // 2, (hh % 2) * T:(hh % 2 + 1) * T],
                                       kb == 0, kb == 1)
                        if u % 2:
                            done(i)
                        else:
                            i.then_inc(pv_even.sem, 1)
                for n in range(GB // 2):
                    for held, count in before(g, again, "o1", n):
                        pe.wait_ge(held, count)
                    for j in (2 * n, 2 * n + 1):
                        pe.wait_ge(normed.sem, normed.at(g, j + 1))
                        i = mm(tile("o1", n)[:, (j % 2) * T:(j % 2 + 1) * T], wo1[:], num[:, j, :])
                    done(i)
                transposes(g, again, "xt4", 3)
                for e in range(EB):
                    for k, stage in enumerate(("up4", "gate4")):
                        for held, count in before(g, again, stage, e):
                            pe.wait_ge(held, count)
                        if e == 0 and k == 0:
                            pe.wait_ge(dve_emptied.sem, empty(g, "xt4", DB - 1))
                            if not again:
                                pe.wait_ge(ffn_consts.sem, ffn_consts.at(0, 7))
                        n = 0
                        for part in (xhi, xlo):
                            for d in range(DB):
                                i = mm(tile(stage, e), tern[k][:, d * DE + e * P:d * DE + (e + 1) * P], part[:, d, :],
                                       n == 0, n == 3)
                                n += 1
                        done(i)
                for n in range(GB // 2):
                    for held, count in before(g, again, "down4", n):
                        pe.wait_ge(held, count)
                    for j in (2 * n, 2 * n + 1):
                        k = 0
                        for part, sem in ((hhi, h_hi), (hlo, h_lo)):
                            for e in range(EB):
                                if n == 0 and j == 0:
                                    pe.wait_ge(sem.sem, sem.at(g, e + 1))
                                i = mm(tile("down4", n)[:, (j % 2) * D:(j % 2 + 1) * D], part[:, e, j * P:(j + 1) * P],
                                       tern[2][:, e * D:(e + 1) * D], k == 0, k == 2 * EB - 1)
                                k += 1
                    done(i)

            body(0, False)
            with pe.Fori(1, NG) as g:
                body(g, True)

        @block.vector
        def _(dve):
            def layernorm(g, again, n, src):
                for j in range(GB):
                    dve.bn_stats(stats[:, j, :], src[:, j, :]).then_inc(ln_stats.sem, 1)
                for j in range(GB):
                    dve.wait_ge(ln_stats.sem, ln_stats.at(g, GB * n + j + 1))
                    if again:
                        dve.sem_inc(passed.sem, 1)
                    i = dve.bn_aggr(mv[:, j, :], stats[:, j, :])
                i.then_inc(ln_mv.sem, 1)
                dve.wait_ge(ln_rstd.sem, ln_rstd.at(g, n + 1))
                dve.wait_ge(ln_mv.sem, ln_mv.at(g, n + 1))
                for j in range(GB):
                    dve.tensor_scalar(xn[:, j, :], src[:, j, :], mv[:, j, 0:1], rstd[:, j:j + 1], ALU.subtract,
                                      ALU.mult).then_inc(ln_done.sem, 1)

            def quantise(n):
                steps = [4 * n]

                def step(i):
                    steps[0] += 1
                    i.then_inc(quant_step.sem, 1)
                    dve.wait_ge(quant_step.sem, quant_step.at(0, steps[0]))

                dve.wait_ge(raw_in.sem, raw_in.at(0, n + 1))
                dve.tensor_reduce(wsum[:, n, 0:1], raw, AX.X, ALU.add, apply_absolute_value=True)\
                    .then_inc(abs_sums.sem, 1)
                dve.wait_ge(abs_total.sem, abs_total.at(0, n + 1))
                step(dve.tensor_scalar(wscale[:, n:n + 1], wsum[:, n, 1:2], 1.0 / (D * DE), QUANT_EPS, ALU.mult, ALU.add))
                step(dve.tensor_scalar(half[:, n, 0:1], wscale[:, n:n + 1], 0.5, None, ALU.mult))
                step(dve.tensor_scalar(half[:, n, 1:2], wscale[:, n:n + 1], -0.5, None, ALU.mult))
                step(dve.tensor_scalar(tpos, raw, half[:, n, 0:1], None, ALU.is_gt))
                dve.scalar_tensor_tensor(out=tern[n][:], in0=raw, scalar=half[:, n, 1:2], in1=tpos, op0=ALU.is_lt,
                                         op1=ALU.subtract).then_inc(tern_done.sem, 1)

            def ffn_scales():
                def step(n, i):
                    i.then_inc(ffn_consts.sem, 1)
                    dve.wait_ge(ffn_consts.sem, ffn_consts.at(0, n))

                step(1, dve.tensor_scalar(ffn_c[:, 0:1], wscale[:, 0:1], -1.0, None, ALU.mult))
                step(2, dve.reciprocal(ffn_c[:, 2:3], ffn_c[:, 0:1]))
                step(3, dve.tensor_scalar(ffn_c[:, 1:2], ffn_c[:, 2:3], 0.5, None, ALU.mult))
                step(4, dve.tensor_tensor(ffn_c[:, 2:3], wscale[:, 1:2], wscale[:, 2:3], ALU.mult))
                step(5, dve.tensor_tensor(ffn_c[:, 3:4], ffn_c[:, 0:1], ffn_c[:, 2:3], ALU.mult))
                step(6, dve.tensor_scalar(ffn_c[:, 2:3], ffn_c[:, 3:4], 2.0, None, ALU.mult))
                dve.wait_ge(tern_done.sem, tern_done.at(0, 3))
                dve.tensor_copy(ffn_c[:, 3:4], ffn_c[:, 2:3]).then_inc(ffn_consts.sem, 1)

            out = dve_emptied.sem

            def body(g, again):
                dve.wait_ge(x_loaded.sem, x_loaded.at(g, 1))
                layernorm(g, again, 0, x_in)
                dve.wait_ge(tiles_ready.sem, full(g, "k1", 0))
                if not again:
                    dve.wait_ge(w_attn1.sem, w_attn1.at(0, 12))
                    dve.wait_ge(pads.sem, pads.at(0, 4))
                kt = tile("k1", 0)
                for r in range(2):
                    dve.scalar_tensor_tensor(out=kr[:, r, :], in0=kt[:, r * T:(r + 1) * T], scalar=bk1[:, r:r + 1],
                                             in1=rope[:, 2 + r, :], op0=ALU.add, op1=ALU.mult).then_inc(out, 1)
                dve.wait_ge(dve_emptied.sem, empty(g, "k1", 0))
                dve.tensor_tensor(kr[:, 2, :], kr[:, 0, :], kr[:, 1, :], ALU.add).then_inc(kr_done.sem, 1)
                dve.wait_ge(tiles_ready.sem, full(g, "v1", 0))
                if again:
                    dve.wait_ge(tiles_ready.sem, full(g - 1, "pv", UNITS // 2 - 1))
                dve.tensor_tensor(Vs[:].rearrange("p b k h c -> p (b k) h c")[:, :, :, 0:HD],
                                  tile("v1", 0)[:, 0:8 * 32].rearrange("p (n h d) -> p n h d", n=8, h=KV),
                                  bv1[:].rearrange("p (o h d) -> p o h d", o=1, h=KV).broadcast_to([P, 8, KV, HD]),
                                  ALU.add).then_inc(out, 1)
                dve.wait_ge(kr_done.sem, kr_done.at(g, 1))
                dve.wait_ge(k_hi.sem, k_hi.at(g, 1))
                dve.tensor_tensor(kres, kr[:, 2, :], ksplit[:, 0, :], ALU.subtract).then_inc(kres_done.sem, 1)
                dve.wait_ge(kres_done.sem, kres_done.at(g, 1))
                dve.wait_ge(k_hi.sem, k_hi.at(g, 2))
                dve.tensor_tensor(ksplit[:, 2, :], kres, ksplit[:, 1, :], ALU.subtract)\
                    .then_inc(k_split_done.sem, 1)
                for e in range(DB):
                    dve.wait_ge(tiles_ready.sem, full(g, "k", e))
                    dve.tensor_copy(kcat[:, e, :, 1, :], tile("k", e).rearrange("p (b k) -> p b k", b=GB))\
                        .then_inc(out, 1)
                for n in range(GB // 2):
                    dve.wait_ge(tiles_ready.sem, full(g, "v", n))
                    dve.tensor_copy(v_sb[:, 2 * n:2 * n + 2, :].rearrange("p a b -> p (a b)"), tile("v", n))\
                        .then_inc(out, 1)
                for n in range(GB // 2):
                    dve.wait_ge(tiles_ready.sem, full(g, "s", n))
                    dve.tensor_reduce(nmax[:, 2 * n:2 * n + 2], tile("s", n).rearrange("p (a b) -> p a b", a=2), AX.X,
                                      ALU.max, negate=True).then_inc(neg_max.sem, 1)
                for n in range(GB // 2):
                    dve.wait_ge(tiles_ready.sem, full(g, "pt", n))
                    dve.tensor_copy(prT[:, 2 * n:2 * n + 2, :, :].rearrange("p a b c -> p (a b c)"), tile("pt", n))\
                        .then_inc(out, 1)
                dve.wait_ge(act_emptied.sem, empty(g, "s", GB // 2 - 1))
                dve.reciprocal(rinv[:], rsum[:]).then_inc(sums_inv.sem, 1)
                dve.wait_ge(sums_inv.sem, sums_inv.at(g, 1))
                for n in range(GB // 2):
                    dve.wait_ge(tiles_ready.sem, full(g, "o", n))
                    for j in (2 * n, 2 * n + 1):
                        i = dve.scalar_tensor_tensor(out=x_res[:, j, :], in0=tile("o", n)[:, (j % 2) * D:(j % 2 + 1) * D],
                                                     scalar=rinv[:, j:j + 1], in1=x_in[:, j, :], op0=ALU.mult,
                                                     op1=ALU.add)
                        i.then_inc(out, 1)
                dve.wait_ge(dve_emptied.sem, empty(g, "o", GB // 2 - 1))
                layernorm(g, again, 1, x_res)
                dve.wait_ge(ln_done.sem, ln_done.at(g, 2 * GB))
                dve.tensor_tensor(acc[:].rearrange("p a b -> p (a b)"), x_res[:].rearrange("p a b -> p (a b)"),
                                  xn[:].rearrange("p a b -> p (a b)"), ALU.add).then_inc(base_sum.sem, 1)
                dve.wait_ge(act_emptied.sem, empty(g, "route", 0))
                dve.tensor_scalar(el1[:], el[:], 1.0, None, ALU.add).then_inc(route_step.sem, 1)
                dve.wait_ge(route_step.sem, route_step.at(g, 1))
                dve.reciprocal(prob[:], el1[:]).then_inc(route_step.sem, 1)
                dve.wait_ge(route_step.sem, route_step.at(g, 2))
                if again:
                    dve.sem_inc(passed.sem, 1)
                for j in range(GB):
                    dve.max(top[:, j, :], prob[:, j, :]).then_inc(top_step.sem, 1)
                for j in range(GB):
                    dve.wait_ge(top_step.sem, top_step.at(g, j + 1))
                    if again:
                        dve.sem_inc(passed.sem, 1)
                    dve.max_index(topi[:, j, :], top[:, j, :], prob[:, j, :]).then_inc(top_step.sem, 1)
                dve.tensor_tensor(psum2[:], top[:, :, 0:1], top[:, :, 1:2], ALU.add).then_inc(route_step.sem, 1)
                dve.wait_ge(route_step.sem, route_step.at(g, 3))
                dve.reciprocal(pinv[:], psum2[:]).then_inc(route_step.sem, 1)
                dve.wait_ge(top_step.sem, top_step.at(g, 2 * GB))
                dve.tensor_copy(topf[:], topi[:, :, 0:2]).then_inc(route_step.sem, 1)
                dve.wait_ge(route_step.sem, route_step.at(g, 4))
                for j in range(GB):
                    dve.tensor_scalar(topw[:, j, :], top[:, j, 0:2], pinv[:, j, 0:1], None, ALU.mult)\
                        .then_inc(route_step.sem, 1)
                dve.wait_ge(route_step.sem, route_step.at(g, 5 + GB))
                for j in range(GB):
                    for k, hot in enumerate((hot0, hot1)):
                        dve.tensor_scalar(hot[:, j, :], iota_e[:], topf[:, j, k:k + 1], topw[:, j, k:k + 1],
                                          ALU.is_equal, ALU.mult).then_inc(hots.sem, 1)
                dve.wait_ge(hots.sem, hots.at(g, 2 * GB))
                dve.tensor_tensor(comb[:, :, 0:E], hot0[:], hot1[:], ALU.add).then_inc(comb_done.sem, 1)

                def product(e):
                    dve.wait_ge(tiles_ready.sem, full(g, "up", e))
                    dve.wait_ge(act_emptied.sem, empty(g, "gate", e))
                    if e >= 2:
                        dve.wait_ge(tiles_ready.sem, full(g, "down", 2 * (e - 2) + 1))
                    else:
                        if again:
                            dve.wait_ge(tiles_ready.sem, full(g - 1, "down", 2 * (ES - 2 + e) + 1))
                    dve.scalar_tensor_tensor(out=y_sb[:, e % 2, :], in0=tile("up", e), scalar=ub[:, e:e + 1],
                                             in1=g_sb[:, e % 2, :], op0=ALU.add, op1=ALU.mult).then_inc(out, 1)

                product(0)
                product(1)
                for n in range(GB // 2):
                    dve.wait_ge(tiles_ready.sem, full(g, "bias2", n))
                    dve.wait_ge(base_sum.sem, base_sum.at(g, 1))
                    half = acc[:, 2 * n:2 * n + 2, :].rearrange("p a b -> p (a b)")
                    dve.tensor_tensor(half, half, tile("bias2", n), ALU.add).then_inc(out, 1)
                dve.wait_ge(comb_done.sem, comb_done.at(g, 1))
                for e in range(ES):
                    for n in range(GB // 2):
                        dve.wait_ge(tiles_ready.sem, full(g, "down", 2 * e + n))
                        if e == 0:
                            dve.wait_ge(dve_emptied.sem, empty(g, "bias2", n))
                        for j in (2 * n, 2 * n + 1):
                            if e:
                                dve.wait_ge(dve_emptied.sem, empty(g, "down", 2 * (e - 1) + n, j % 2 + 1))
                            t = tile("down", 2 * e + n)[:, (j % 2) * D:(j % 2 + 1) * D]
                            dve.scalar_tensor_tensor(out=acc[:, j, :], in0=t, scalar=comb[:, j, e:e + 1],
                                                     in1=acc[:, j, :], op0=ALU.mult, op1=ALU.add)\
                                .then_inc(out, 1)
                    if e + 2 < ES:
                        product(e + 2)
                    if not again and e in QUANT_AT:
                        quantise(QUANT_AT.index(e))
                if not again:
                    ffn_scales()
                dve.wait_ge(dve_emptied.sem, empty(g, "down", 2 * ES - 1))
                layernorm(g, again, 2, acc)
                for n in range(GB // 2):
                    for r, stage in enumerate(("q1", "q1r")):
                        dve.wait_ge(tiles_ready.sem, full(g, stage, n))
                        dve.scalar_tensor_tensor(out=qr[:, r, :, :].rearrange("p b k -> p b k"),
                                                 in0=tile(stage, n).rearrange("p (b k) -> p b k", b=2),
                                                 scalar=bq1[:, r:r + 1],
                                                 in1=rope[:, r:r + 1, :].broadcast_to([P, 2, T]),
                                                 op0=ALU.add, op1=ALU.mult).then_inc(out, 1)
                    dve.wait_ge(dve_emptied.sem, empty(g, "q1r", n))
                    if n == 0:
                        if again:
                            dve.wait_ge(stored.sem, stored.at(g - 1, 1))
                    dve.tensor_tensor(q_rot[:, 2 * n:2 * n + 2, :], qr[:, 0, :, :], qr[:, 1, :, :], ALU.add)\
                        .then_inc(q_rotated.sem, 1)
                    dve.wait_ge(q_rotated.sem, q_rotated.at(g, n + 1))
                    dve.wait_ge(q_hi.sem, q_hi.at(g, 2 * n + 1))
                    dve.tensor_tensor(qres[:, 2 * n:2 * n + 2, :], q_rot[:, 2 * n:2 * n + 2, :],
                                      qsplit[:, 2 * n:2 * n + 2, 0, :], ALU.subtract).then_inc(q_res_done.sem, 1)
                    dve.wait_ge(q_res_done.sem, q_res_done.at(g, n + 1))
                    dve.wait_ge(q_hi.sem, q_hi.at(g, 2 * n + 2))
                    dve.tensor_tensor(qsplit[:, 2 * n:2 * n + 2, 2, :], qres[:, 2 * n:2 * n + 2, :],
                                      qsplit[:, 2 * n:2 * n + 2, 1, :], ALU.subtract).then_inc(q_split_done.sem, 1)
                for s in range(STEPS):
                    if s < UNITS:
                        j, kv = divmod(s, KV)
                        for hh in range(KV):
                            h = KV * kv + hh
                            dve.wait_ge(tiles_ready.sem, full(g, "smax", 4 * s + hh))
                            dve.tensor_reduce(M[:, j, 2 * h:2 * h + 2],
                                              tile("smax", 4 * s + hh).rearrange("p (a b) -> p a b", a=2), AX.X,
                                              ALU.max).then_inc(out, 1)
                    if s % KV == 0 and s >= KV and s // KV - 1 < GB:
                        j = s // KV - 1
                        dve.wait_ge(tiles_ready.sem, full(g, "mt", j))
                        if again:
                            dve.wait_ge(m_stacked[j].sem, m_stacked[j].at(g - 1, 2))
                        t = tile("mt", j)[0:2 * H, 0:P]
                        dve.tensor_scalar(mhi[:, j, :], t, -1.0, None, ALU.mult).then_inc(out, 1)
                        dve.wait_ge(dve_emptied.sem, empty(g, "mt", j, 1))
                        dve.scalar_tensor_tensor(out=mlo[:, j, :], in0=t, scalar=-1.0, in1=mhi[:, j, :],
                                                 op0=ALU.mult, op1=ALU.subtract).then_inc(out, 1)
                for j in range(GB):
                    dve.wait_ge(nd_loaded[j].sem, nd_loaded[j].at(g, 2))
                    dve.reciprocal(den[:, j, :], den[:, j, :]).then_inc(den_inv.sem, 1)
                    dve.wait_ge(den_inv.sem, den_inv.at(g, j + 1))
                    dve.tensor_tensor(num[:, j, :], num[:, j, :], den[:, j, :], ALU.mult).then_inc(normed.sem, 1)
                for n in range(GB // 2):
                    dve.wait_ge(tiles_ready.sem, full(g, "o1", n))
                    dve.scalar_tensor_tensor(out=x3[:, 2 * n:2 * n + 2, :].rearrange("p a b -> p (a b)"),
                                             in0=tile("o1", n), scalar=bo1[:, 0:1],
                                             in1=acc[:, 2 * n:2 * n + 2, :].rearrange("p a b -> p (a b)"),
                                             op0=ALU.add, op1=ALU.add).then_inc(out, 1)
                dve.wait_ge(dve_emptied.sem, empty(g, "o1", GB // 2 - 1))
                layernorm(g, again, 3, x3)
                for d in range(DB):
                    dve.wait_ge(x_hi.sem, x_hi.at(g, d + 1))
                    dve.wait_ge(tiles_ready.sem, full(g, "xt4", d))
                    dve.tensor_tensor(xlo[:, d, :], tile("xt4", d), xhi[:, d, :], ALU.subtract).then_inc(out, 1)
                for e in range(EB):
                    dve.wait_ge(tiles_ready.sem, full(g, "gate4", e))
                    dve.wait_ge(act_emptied.sem, empty(g, "up4", e))
                    if e >= 2:
                        dve.wait_ge(h_lo.sem, h_lo.at(g, e - 1))
                        dve.wait_ge(h_hi.sem, h_hi.at(g, e - 1))
                    else:
                        if again:
                            dve.wait_ge(h_lo.sem, h_lo.at(g - 1, EB - 1 + e))
                        if again:
                            dve.wait_ge(h_hi.sem, h_hi.at(g - 1, EB - 1 + e))
                    dve.scalar_tensor_tensor(out=h_sb[:, e % 2, :], in0=tile("gate4", e), scalar=ffn_c[:, 1:2],
                                             in1=s_sb[:, e % 2, :], op0=ALU.mult, op1=ALU.mult)\
                        .then_inc(out, 1)
                for n in range(GB // 2):
                    dve.wait_ge(tiles_ready.sem, full(g, "down4", n))
                    for j in (2 * n, 2 * n + 1):
                        dve.scalar_tensor_tensor(out=y_out[:, j, :], in0=tile("down4", n)[:, (j % 2) * D:(j % 2 + 1) * D],
                                                 scalar=ffn_c[:, 3:4], in1=x3[:, j, :], op0=ALU.mult, op1=ALU.add)\
                            .then_inc(out, 1)

            body(0, False)
            with dve.Fori(1, NG) as g:
                body(g, True)


def layouts(i):
    f = lambda v: np.ascontiguousarray(v)
    heads = np.arange(P).reshape(H, HD)
    by_d = heads.T.reshape(-1)
    turned = np.roll(heads, -(HD // 2), axis=1).T.reshape(-1)
    kheads = np.arange(KV * HD).reshape(KV, HD)
    k_by_d = kheads.T.reshape(-1)
    k_turned = np.roll(kheads, -(HD // 2), axis=1).T.reshape(-1)
    pv = np.arange(P).reshape(KV, KV, HD).transpose(2, 1, 0).reshape(-1)
    Wq, Wk, Wv, Wo = (i[f"L1_xattn_W{n}"] for n in "qkvo")
    bq, bk = i["L1_xattn_bq"], i["L1_xattn_bk"]
    halves = lambda w: f(w.T.reshape(DB, P, DE).transpose(1, 0, 2).reshape(P, DB * DE))
    return {
        "x": f(i["x"]), "ctx": f(i["ctx_2048"]),
        "ctxT": f(i["ctx_2048"].transpose(0, 2, 1).reshape(B, DB, P, P)),
        "wq0": f(i["L0_xattn_wq"].T), "wk0": f(i["L0_xattn_wk"].T), "wv0": f(i["L0_xattn_wv"].T),
        "wo0": f(i["L0_xattn_wo"].T), "wa": f(i["L0_ffn_wa"]),
        "wg": f(np.concatenate([i["L0_ffn_rg"], i["L0_ffn_sg"]])), "wu": f(np.concatenate([i["L0_ffn_rw1"], i["L0_ffn_sw1"]])),
        "w2": f(np.concatenate([i["L0_ffn_rw2"], i["L0_ffn_sw2"]])),
        "gb": f(np.concatenate([i["L0_ffn_rgb"], i["L0_ffn_sgb"]]).T), "ub": f(np.concatenate([i["L0_ffn_rb1"], i["L0_ffn_sb1"]]).T),
        "b2": f(np.concatenate([i["L0_ffn_rb2"], i["L0_ffn_sb2"]])),
        "wq1": f(Wq[by_d].T), "wq1r": f(Wq[turned].T), "wk1": f(Wk[k_by_d].T), "wk1r": f(Wk[k_turned].T), "wv1": f(Wv.T),
        "bq1": f(np.stack([bq[by_d], bq[turned]], axis=1)),
        "bk1": f(np.tile(np.stack([bk[k_by_d], bk[k_turned]], axis=1), (GB, 1))),
        "bv1": f(i["L1_xattn_bv"][None]), "wo1": f(Wo.T[pv]), "bo1": f(i["L1_xattn_bo"][:, None]),
        "wup": halves(i["L1_ffn_W_up"]), "wgate": halves(i["L1_ffn_W_gate"]),
        "wdown": f(i["L1_ffn_W_down"].T.reshape(EB, P, D).transpose(1, 0, 2).reshape(P, EB * D)),
        "rope": rope_tables(), "iota": np.arange(E, dtype=np.float32)[None],
    }


def kernel(**inputs):
    import concourse.bacc as bacc
    from concourse.bass_utils import run_bass_kernel_spmd

    arrays = layouts({k: np.asarray(v) for k, v in inputs.items() if k != "mask_BxSx4224_bf0"})
    nc = bacc.Bacc("TRN2", target_bir_lowering=False, num_devices=1)
    aps = {n: nc.dram_tensor(f"in_{n}", v.shape, mybir.dt.from_np(v.dtype), kind="ExternalInput").ap() for n, v in arrays.items()}
    aps["out"] = nc.dram_tensor("out", (B, P, D), F32, kind="ExternalOutput").ap()
    build(nc, aps)
    r = run_bass_kernel_spmd(nc, [{f"in_{n}": v for n, v in arrays.items()}], core_ids=[0])
    return r.results[0]["out"]
```

```python
from contextlib import ExitStack

import numpy as np

import concourse.bass as bass
from concourse import mybir

ALU = mybir.AluOpType
ACT = mybir.ActivationFunctionType
AX = mybir.AxisListType
F32 = mybir.dt.float32
BF16 = mybir.dt.bfloat16
F16 = mybir.dt.float16
U32 = mybir.dt.uint32

P = 128
B = 16
D = 256
DB = D // P
GB = 4
NG = B // GB
TOK = GB * P
E = 16
ES = 18
F = 128
DE = 1024
EB = DE // P
H = 16
KV = 4
HD = P // H
T = D
TERMS = 3
ROWS = 48
MROW = ROWS
UNITS = GB * KV
LAG = 6
STEPS = UNITS + LAG + 1
LN_NEXT_AT = 7
ROWS_NEXT_AT = 13
QUANT_AT = (3, 7, 11)
LN_EPS = 1e-5
QUANT_EPS = 1e-8


BANKS = 8
PV_BANK = 7


FRONT = ("xt", "q", "k", "s", "v", "pt", "at", "o")


def tile_order():
    pairs = range(GB // 2)
    t = [("k1", 0, 1, "dve", 2), ("v1", 0, 1, "dve", 1)]
    t += [("xt2", d, 1, "act", 1) for d in range(DB)]
    t += [("route", 0, 1, "act", 1), ("gate", 0, 1, "act", 1), ("up", 0, 1, "dve", 1)]
    t += [("gate", 1, 1, "act", 1), ("up", 1, 1, "dve", 1), ("ct", 0, 1, "act", 1)]
    t += [("bias2", n, 1, "dve", 1) for n in pairs]
    for e in range(ES):
        t += [("down", 2 * e + n, 1, "dve", 2) for n in pairs]
        if e + 2 < ES:
            t += [("gate", e + 2, 1, "act", 1), ("up", e + 2, 1, "dve", 1)]
    t += [("xt", d, 1, "act", 1) for d in range(DB)]
    t += [("q", e, 1, "act", 1) for e in range(DB)]
    for n in pairs:
        t += [("q1", n, 1, "dve", 1), ("q1r", n, 1, "dve", 1)]
    t += [("k", e, 1, "dve", 1) for e in range(DB)]
    t += [("s", n, 1, "act", 2) for n in pairs]
    for s in range(STEPS):
        if s < UNITS:
            t += [("smax", 4 * s + h, 1, "dve", 1) for h in range(KV)]
        if s % KV == 0 and 0 <= s // KV - 1 < GB:
            t += [("mt", s // KV - 1, 1, "dve", 2)]
        if 0 <= s - LAG < UNITS:
            t += [("st", 2 * (s - LAG) + kb, 2, "act", 1) for kb in range(2)]
        if 0 <= s - LAG - 1 < UNITS and (s - LAG - 1) % 2:
            t += [("pv", (s - LAG - 1) // 2, 0, "act", 1)]
    t += [("v", n, 1, "dve", 1) for n in pairs]
    t += [("pt", n, 1, "dve", 1) for n in pairs]
    t += [("at", n, 1, "act", 1) for n in pairs]
    t += [("o1", n, 1, "dve", 1) for n in pairs]
    t += [("o", n, 1, "dve", 2) for n in pairs]
    t += [("xt4", d, 1, "dve", 1) for d in range(DB)]
    for e in range(EB):
        t += [("up4", e, 1, "act", 1), ("gate4", e, 1, "dve", 1)]
    t += [("down4", n, 1, "dve", 2) for n in pairs]
    return t


class Ring:

    def __init__(self):
        self.bank, self.full, self.empty = {}, {}, {}
        self.counts = {(kind, front): 0 for kind in ("full", "act", "dve") for front in (False, True)}
        order, places, at = tile_order(), [], 0
        for stage, n, banks, engine, parts in order:
            if at % PV_BANK + banks > PV_BANK:
                at += PV_BANK - at % PV_BANK
            places.append([PV_BANK] if not banks else [(at + b) % PV_BANK for b in range(banks)])
            at += banks
            front = stage in FRONT
            self.counts["full", front] += 1
            self.counts[engine, front] += parts
            self.bank[stage, n] = places[-1][0]
            self.full[stage, n] = self.counts["full", front]
            self.empty[stage, n] = (engine, self.counts[engine, front])
        self.after = {}
        owner = {}
        for body, phase in enumerate(("front", "first", "again", "last")):
            for (stage, n, *_), banks in zip(order, places):
                if (phase == "front" and stage not in FRONT) or (phase == "last" and stage in FRONT):
                    continue
                self.after[phase, stage, n] = sorted({(owner[b][0] < body, *owner[b][1:]) for b in banks if b in owner})
                for b in banks:
                    owner[b] = (body, stage, n)


RING = Ring()
PARTS = {stage: parts for stage, _, _, _, parts in tile_order()}


def rope_tables():
    inv = (np.float32(1.0) / np.float32(10000.0) ** (np.arange(0, HD, 2, dtype=np.float32) / np.float32(HD)))
    freq = np.arange(T, dtype=np.float32)[:, None] * inv.astype(np.float32)[None, :]
    emb = np.concatenate([freq, freq], axis=-1).astype(np.float32)
    cos, sin = np.cos(emb).astype(np.float32), np.sin(emb).astype(np.float32)
    sin[:, : HD // 2] = -sin[:, : HD // 2]
    q = [np.repeat(a.T, H, axis=0) for a in (cos, sin)]
    k = [np.tile(np.repeat(a.T, KV, axis=0), (GB, 1)) for a in (cos, sin)]
    return np.ascontiguousarray(np.stack(q + k, axis=1))


def build(nc, a):
    with ExitStack() as ctx:
        def sb(name, shape, dt=F32):
            return ctx.enter_context(nc.sbuf_tensor(name, shape, dt))

        class Sem:

            def __init__(self, name, per, step=1):
                self.sem, self.per, self.step = ctx.enter_context(nc.semaphore(name)), per, step

            def at(self, g, n):
                return (g * self.per + n) * self.step

        ident = sb("ident", [P, P])
        wq0, wk0, wv0, wo0 = (sb(f"w{n}0", [P, DB, D]) for n in "qkvo")
        wa = sb("wa", [P, DB, E])
        wg = sb("wg", [P, ES, DB, F])
        wu = sb("wu", [P, ES, DB, F])
        w2 = sb("w2", [P, ES, D])
        gb = sb("gb", [P, ES])
        ub = sb("ub", [P, ES])
        b2 = sb("b2", [ES, D])
        wq1, wq1r = sb("wq1", [P, P]), sb("wq1r", [P, P])
        wk1, wk1r, wv1 = sb("wk1", [P, KV * HD]), sb("wk1r", [P, KV * HD]), sb("wv1", [P, KV * HD])
        bq1 = sb("bq1", [P, 2])
        bk1 = sb("bk1", [P, 2])
        bv1 = sb("bv1", [P, KV * HD])
        wo1 = sb("wo1", [P, P])
        bo1 = sb("bo1", [P, 1])
        rope = sb("rope", [P, 4, T])
        tern = [sb(f"tern_{n}", [P, 2048], F16) for n in ("up", "gate", "down")]
        iota_e = sb("iota_e", [P, E])
        wsum = sb("wsum", [P, 3, 2])
        wscale = sb("wscale", [P, 3])
        half = sb("half", [P, 3, 2])
        ffn_c = sb("ffn_c", [P, 4])
        x_in = sb("x_in", [P, GB, D])
        ctx_sb = sb("ctx_sb", [P, GB, D])
        kcat = sb("kcat", [P, DB, GB, 2, P])
        stats = sb("stats", [P, GB, 6])
        mv = sb("mv", [P, GB, 2])
        rstd, var, minus_half = sb("rstd", [P, GB]), sb("var", [P, GB]), sb("minus_half", [P, GB])
        xn = sb("xn", [P, GB, D])
        pr = sb("pr", [P, GB, D])
        xnT = sb("xnT", [P, DB, TOK])
        nmax = sb("nmax", [P, GB])
        rsum = sb("rsum", [P, GB])
        rinv = sb("rinv", [P, GB])
        acc = sb("acc", [P, GB, D])
        x3 = sb("x3", [P, GB, D])
        top = sb("top", [P, GB, 8])
        topi = sb("topi", [P, GB, 8], U32)
        topf = sb("topf", [P, GB, 2])
        psum2 = sb("psum2", [P, GB, 1])
        pinv = sb("pinv", [P, GB, 1])
        topw = sb("topw", [P, GB, 2])
        comb = sb("comb", [P, GB, ES])
        ksplit = sb("ksplit", [P, TERMS, T], BF16)
        KS = sb("KS", [P, GB, KV, T], BF16)
        Vs = sb("Vs", [P, GB, 2, KV, 32])
        M = sb("M", [P, GB, 2 * H])
        ps = ctx.enter_context(nc.psum_tensor("ps", [P, BANKS, 512], F32))

        def part(region, at, size, dt=F32):
            v = region[:, at:at + size]
            return v if dt == F32 else v.bitcast(dt)

        r1 = sb("r1", [P, 8192])
        g_sb = part(r1, 6144, 1024).rearrange("p (a b) -> p a b", a=2)
        y_sb = part(r1, 7168, 1024).rearrange("p (a b) -> p a b", a=2)
        s_sb = part(r1, 0, 1024).rearrange("p (a b) -> p a b", a=2)
        h_sb = part(r1, 1024, 1024).rearrange("p (a b) -> p a b", a=2)
        hhi = part(r1, 2048, 2048, F16).rearrange("p (a b) -> p a b", a=EB)
        hlo = part(r1, 4096, 2048, F16).rearrange("p (a b) -> p a b", a=EB)
        QS = part(r1, 0, 8192, BF16).rearrange("p (b h k) -> p b h k", b=GB, h=H)
        r2 = sb("r2", [P, 4096])
        v_sb = part(r2, 1024, 1024).rearrange("p (a b) -> p a b", a=GB)
        prT = part(r2, 3072, 1024).rearrange("p (a b c) -> p a b c", a=GB, b=2)
        PT = part(r2, 0, 4096).rearrange("p (n a b) -> p n a b", n=4, a=2)
        r3 = sb("r3", [P, 1024])
        combT = part(r3, 0, TOK)[0:ES, :]
        mhi = part(r3, 512, 256, BF16)[0:2 * H, :].rearrange("p (b k) -> p b k", b=GB)
        mlo = part(r3, 768, 256, BF16)[0:2 * H, :].rearrange("p (b k) -> p b k", b=GB)
        xhi = part(r3, 0, 512, F16).rearrange("p (a b) -> p a b", a=DB)
        xlo = part(r3, 512, 512, F16).rearrange("p (a b) -> p a b", a=DB)
        r4 = sb("r4", [P, 2048])
        raw = part(r4, 0, 2048)
        qr = part(r4, 0, 1024).rearrange("p (r a b) -> p r a b", r=2, a=2)
        qres = part(r4, 1024, 1024).rearrange("p (a b) -> p a b", a=GB)
        U = part(r4, 1024, 1024).rearrange("p (a b) -> p a b", a=KV)
        atT = part(r4, 0, 1024).rearrange("p (a b c) -> p a b c", a=GB, b=DB)
        r5 = sb("r5", [P, 1536])
        tpos = part(r5, 0, 1024, F16)
        el, el1, prob, hot0, hot1 = (part(r5, 1024 + n * GB * E, GB * E).rearrange("p (b e) -> p b e", b=GB)
                                     for n in range(5))
        qsplit = part(r5, 0, 1536, BF16).rearrange("p (b t k) -> p b t k", b=GB, t=TERMS)
        r6 = sb("r6", [P, 2048])
        kr = part(r6, 0, 768).rearrange("p (a b) -> p a b", a=3)
        kres = part(r6, 768, 256)
        num = part(r6, 0, 1024).rearrange("p (a b) -> p a b", a=GB)
        den = part(r6, 1024, 1024).rearrange("p (a b) -> p a b", a=GB)
        xn0 = part(r6, 0, 1024).rearrange("p (a b) -> p a b", a=GB)
        qT = part(r6, 1024, 1024).rearrange("p (a b) -> p a b", a=DB)
        x_res = acc
        q_rot = y_out = x3

        qd = nc.dram_tensor("q_scratch", [GB, TERMS, P, T], BF16, kind="Internal").ap()
        kd = nc.dram_tensor("k_scratch", [TERMS, GB, HD, KV, T], BF16, kind="Internal").ap()
        ud = nc.dram_tensor("pv_scratch", [GB, HD + 1, KV, KV, T], F32, kind="Internal").ap()

        w_attn0, w_attn0v = Sem("w_attn0", 2, 16), Sem("w_attn0v", 2, 16)
        w_experts = Sem("w_experts", 7, 16)
        w_attn1 = Sem("w_attn1", 12, 16)
        raw_in = Sem("raw_in", 3, 16)
        consts = Sem("consts", 1)
        passed = Sem("passed", 0)
        zeroed = Sem("zeroed", 2)
        pads = Sem("pads", 4)
        abs_sums, abs_total = Sem("abs_sums", 3), Sem("abs_total", 3)
        quant_step, tern_done = Sem("quant_step", 12), Sem("tern_done", 3)
        ffn_consts = Sem("ffn_consts", 7)
        x_loaded, ctx_loaded = Sem("x_loaded", 1, 16), Sem("ctx_loaded", 1, 16)
        ctxT_loaded = Sem("ctxT_loaded", DB, 16)
        tiles_ready, front_ready = Sem("tiles_ready", RING.counts["full", False]), Sem("front_ready", RING.counts["full", True])
        act_emptied = Sem("act_emptied", RING.counts["act", False])
        dve_emptied = Sem("dve_emptied", RING.counts["dve", False])
        act_front, dve_front = Sem("act_front", RING.counts["act", True]), Sem("dve_front", RING.counts["dve", True])
        ln_stats = [Sem(f"ln_stats{n}", GB) for n in range(4)]
        ln_mv, ln_var, ln_rstd = ([Sem(f"{name}{n}", 1) for n in range(4)] for name in ("ln_mv", "ln_var", "ln_rstd"))
        ln_done = [Sem(f"ln_done{n}", GB) for n in range(4)]
        neg_max = Sem("neg_max", GB // 2)
        sums_inv = Sem("sums_inv", 1)
        base_sum = Sem("base_sum", 1)
        route_step = Sem("route_step", 5 + GB)
        top_step = Sem("top_step", 2 * GB)
        hots = Sem("hots", 2 * GB)
        comb_done = Sem("comb_done", 1)
        kr_done, kres_done = Sem("kr_done", 1), Sem("kres_done", 1)
        k_hi = Sem("k_hi", 2)
        k_split_done = Sem("k_split_done", 1)
        k_stored, k_stacked = Sem("k_stored", 1, 16), Sem("k_stacked", 6, 16)
        q_rotated, q_res_done = Sem("q_rotated", 2), Sem("q_res_done", 2)
        q_hi = Sem("q_hi", GB)
        pv_even = Sem("pv_even", UNITS // 2)
        x_hi = Sem("x_hi", DB)
        q_split_done = Sem("q_split_done", 2)
        q_cleared = Sem("q_cleared", GB)
        q_stored = [Sem(f"q_stored{n}", 2, 16) for n in range(GB // 2)]
        q_stacked = [Sem(f"q_stacked{j}", 3, 16) for j in range(GB)]
        m_stacked = [Sem(f"m_stacked{j}", 2, 16) for j in range(GB)]
        u_stored = Sem("u_stored", KV * GB, 16)
        nd_loaded = [Sem(f"nd_loaded{j}", 2, 16) for j in range(GB)]
        den_inv, normed = Sem("den_inv", GB), Sem("normed", GB)
        h_hi, h_lo = Sem("h_hi", EB), Sem("h_lo", EB)
        stored = Sem("stored", 1, 16)

        block = ctx.enter_context(nc.Block())

        def tile(stage, n, banks=1):
            at = RING.bank[stage, n]
            return ps[:, at, :] if banks == 1 else ps[:, at:at + banks, :].rearrange("p a b -> p (a b)")

        def full(g, stage, n):
            return g * (front_ready if stage in FRONT else tiles_ready).per + RING.full[stage, n]

        def empty(g, stage, n, part=None):
            engine, count = RING.empty[stage, n]
            return g * RING.counts[engine, stage in FRONT] + (count if part is None else count - PARTS[stage] + part)

        def before(body, phase, stage, n):
            for earlier, st, k in RING.after[phase, stage, n]:
                ahead = (st in FRONT) - earlier
                sems = (act_front, dve_front) if st in FRONT else (act_emptied, dve_emptied)
                yield sems[RING.empty[st, k][0] == "dve"].sem, empty(body + ahead if ahead else body, st, k)

        def weighted(g, u):
            if u % 2:
                return tiles_ready.sem, full(g, "pv", u // 2)
            return pv_even.sem, pv_even.at(g, u // 2 + 1)

        @block.sync
        def _(sp):
            def load_x(g):
                sp.dma_start(x_in[:], a["x"][bass.ts(g, GB)].rearrange("b s d -> s b d")).then_inc(x_loaded.sem, 16)

            def load_ctx(g):
                sp.dma_start(ctx_sb[:], a["ctx"][bass.ts(g, GB)].rearrange("b s d -> s b d")).then_inc(ctx_loaded.sem, 16)
                for eb in range(DB):
                    sp.dma_start(kcat[:, eb, :, 0, :], a["ctxT"][bass.ts(g, GB), eb].rearrange("b p k -> p b k"))\
                        .then_inc(ctxT_loaded.sem, 16)

            load_x(0)
            for dst, src in ((wq0, "wq0"), (wk0, "wk0")):
                sp.dma_start(dst[:], a[src].rearrange("(b p) e -> p b e", p=P)).then_inc(w_attn0.sem, 16)
            load_ctx(0)
            for dst, src in ((wv0, "wv0"), (wo0, "wo0")):
                sp.dma_start(dst[:], a[src].rearrange("(b p) e -> p b e", p=P)).then_inc(w_attn0v.sem, 16)
            for dst, src in ((wq1, "wq1"), (wq1r, "wq1r"), (wk1, "wk1"), (wk1r, "wk1r"), (wv1, "wv1"), (bq1, "bq1"),
                             (bk1, "bk1"), (wo1, "wo1"), (bo1, "bo1"), (rope, "rope")):
                sp.dma_start(dst[:], a[src]).then_inc(w_attn1.sem, 16)
            sp.dma_start(bv1[:], a["bv1"].broadcast_to([P, KV * HD])).then_inc(w_attn1.sem, 16)
            sp.dma_start(iota_e[:], a["iota"].broadcast_to([P, E])).then_inc(w_attn1.sem, 16)
            sp.dma_start(wa[:], a["wa"].rearrange("(b p) e -> p b e", p=P)).then_inc(w_experts.sem, 16)
            for dst, src in ((gb, "gb"), (ub, "ub")):
                sp.dma_start(dst[:], a[src]).then_inc(w_experts.sem, 16)
            sp.dma_start(b2[:], a["b2"]).then_inc(w_experts.sem, 16)
            for dst, src in ((wg, "wg"), (wu, "wu")):
                sp.dma_start(dst[:], a[src].rearrange("e (b p) f -> p (e b) f", p=P)).then_inc(w_experts.sem, 16)
            sp.dma_start(w2[:], a["w2"].rearrange("e f d -> f e d")).then_inc(w_experts.sem, 16)
            def body(g, again, last=False):
                if not last:
                    sp.wait_ge(tiles_ready.sem, full(g, "v1", 0))
                    load_ctx(g + 1)
                    sp.wait_ge(dve_front.sem, empty(g, "o", GB // 2 - 1))
                    load_x(g + 1)
                sp.wait_ge(k_split_done.sem, k_split_done.at(g, 1))
                if again:
                    sp.wait_ge(k_stacked.sem, k_stacked.at(g - 1, 6))
                sp.dma_start(kd.rearrange("t b d h k -> (b d h) t k"), ksplit[:]).then_inc(k_stored.sem, 16)
                sp.wait_ge(k_stored.sem, k_stored.at(g, 1))
                if again:
                    sp.wait_ge(tiles_ready.sem, full(g - 1, "st", 2 * UNITS - 1))
                sp.wait_ge(pads.sem, pads.at(0, 4))
                for r, term in enumerate((0, 0, 0, 1, 1, 2)):
                    sp.dma_start(KS[8 * r:8 * r + 8, :, :, :].rearrange("d b h k -> d b (h k)"),
                                 kd[term].rearrange("b d h k -> d b (h k)")).then_inc(k_stacked.sem, 16)
                for n in range(GB // 2):
                    sp.wait_ge(q_split_done.sem, q_split_done.at(g, n + 1))
                    for j in (2 * n, 2 * n + 1):
                        if again:
                            sp.wait_ge(q_stacked[j].sem, q_stacked[j].at(g - 1, 3))
                        sp.dma_start(qd[j].rearrange("t p k -> p t k"), qsplit[:, j, :, :])\
                            .then_inc(q_stored[n].sem, 16)
                    sp.wait_ge(q_stored[n].sem, q_stored[n].at(g, 2))
                    if again:
                        sp.sem_inc(passed.sem, 1)
                    for j in (2 * n, 2 * n + 1):
                        flat = qd[j].rearrange("t (d h) k -> (t d) (h k)", h=H)
                        sp.wait_ge(q_cleared.sem, q_cleared.at(g, j + 1))
                        for r0, rows in ((0, 3), (3, 2), (5, 1)):
                            sp.dma_start(QS[8 * r0:8 * r0 + 8 * rows, j, :, :].rearrange("r h k -> r (h k)"),
                                         flat[0:8 * rows]).then_inc(q_stacked[j].sem, 16)
                for s in range(KV + 1, STEPS + 1):
                    if s % KV == 1 and s // KV - 1 < GB:
                        j = s // KV - 1
                        for r, part in enumerate((mhi, mlo)):
                            sp.wait_ge(dve_emptied.sem, empty(g, "mt", j, r + 1))
                            sp.dma_start(QS[MROW + r:MROW + r + 1, j, :, :].rearrange("r h k -> r (h k)"),
                                         part[:, j, :]).then_inc(m_stacked[j].sem, 16)
                    u = s - LAG - 1
                    if u >= 0 and u % KV == KV - 1:
                        j = u // KV
                        sp.wait_ge(act_emptied.sem, empty(g, "pv", 2 * j + 1))
                        if again:
                            sp.wait_ge(nd_loaded[j].sem, nd_loaded[j].at(g - 1, 2))
                        for q in range(KV):
                            sp.dma_start(ud[j, :, q, :, :].rearrange("r h k -> r (h k)"),
                                         U[32 * q:32 * q + HD + 1, :, :].rearrange("r h k -> r (h k)"))\
                                .then_inc(u_stored.sem, 16)
                        sp.wait_ge(u_stored.sem, u_stored.at(g, KV * (j + 1)))
                        if again:
                            sp.sem_inc(passed.sem, 1)
                        if not last:
                            sp.wait_ge(front_ready.sem, full(g + 1, "s", GB // 2 - 1))
                        else:
                            sp.wait_ge(tiles_ready.sem, full(g - 1, "o1", j // 2))
                        sp.dma_start(num[:, j, :], ud[j, 0:HD].rearrange("r q h k -> (r q h) k"))\
                            .then_inc(nd_loaded[j].sem, 16)
                        sp.dma_start(den[:, j, :], ud[j, HD].rearrange("(o q) h k -> o (q h) k", o=1)
                                     .broadcast_to([HD, H, T])).then_inc(nd_loaded[j].sem, 16)
                sp.wait_ge(dve_emptied.sem, empty(g, "down4", GB // 2 - 1))
                sp.dma_start(a["out"][bass.ts(g, GB)].rearrange("b s d -> s b d"), y_out[:]).then_inc(stored.sem, 16)

            body(0, False)
            with sp.Fori(1, NG - 1) as g:
                body(g, True)
            body(NG - 1, True, last=True)
            sp.wait_ge(stored.sem, stored.at(NG - 1, 1))

        @block.gpsimd
        def _(pool):
            pool.memset(ident[:], 0.0).then_inc(zeroed.sem, 1)
            pool.wait_ge(zeroed.sem, zeroed.at(0, 1))
            pool.affine_select(out=ident[:], in_=ident[:], compare_op=ALU.not_equal, fill=1.0, base=0,
                               pattern=[[-1, P]], channel_multiplier=1).then_inc(consts.sem, 1)
            pool.memset(KS[:], 1.0).then_inc(pads.sem, 1)
            pool.memset(Vs[:], 0.0).then_inc(zeroed.sem, 1)
            pool.wait_ge(zeroed.sem, zeroed.at(0, 2))
            pool.memset(Vs[:, :, :, :, HD:HD + 1], 1.0).then_inc(pads.sem, 1)
            pool.memset(comb[:, :, E:ES], 1.0).then_inc(pads.sem, 1)
            pool.memset(minus_half[:], -0.5).then_inc(pads.sem, 1)
            pool.wait_ge(pads.sem, pads.at(0, 4))

            def quantise_sums():
                for n, src in enumerate(("wup", "wgate", "wdown")):
                    if n:
                        pool.wait_ge(tern_done.sem, tern_done.at(0, n))
                    pool.dma_start(raw, a[src]).then_inc(raw_in.sem, 16)
                    pool.wait_ge(abs_sums.sem, abs_sums.at(0, n + 1))
                    pool.partition_all_reduce(wsum[:, n, 1:2], wsum[:, n, 0:1], P, bass.bass_isa.ReduceOp.add)\
                        .then_inc(abs_total.sem, 1)

            def rsqrt(g, again, n):
                pool.wait_ge(ln_mv[n].sem, ln_mv[n].at(g, 1))
                if again:
                    pool.sem_inc(passed.sem, 1)
                pool.tensor_scalar(var[:], mv[:, :, 1], LN_EPS, None, ALU.add).then_inc(ln_var[n].sem, 1)
                pool.wait_ge(ln_var[n].sem, ln_var[n].at(g, 1))
                pool.tensor_tensor(rstd[:], var[:], minus_half[:], ALU.pow).then_inc(ln_rstd[n].sem, 1)

            def body(g, again, last=False):
                def clear(j):
                    pool.memset(QS[:, j, :, :], 0.0).then_inc(q_cleared.sem, 1)

                if again:
                    pool.wait_ge(tiles_ready.sem, full(g - 1, "down4", GB // 2 - 1))
                    pool.sem_inc(passed.sem, 1)
                for j in range(GB - 1):
                    clear(j)
                if not again:
                    quantise_sums()
                if not last:
                    rsqrt(g + 1, again, 0)
                pool.wait_ge(tiles_ready.sem, full(g, "down", 2 * ES - 1))
                if again:
                    pool.sem_inc(passed.sem, 1)
                clear(GB - 1)
                rsqrt(g, again, 2)
                rsqrt(g, again, 3)
                for e in range(EB):
                    pool.wait_ge(h_hi.sem, h_hi.at(g, e + 1))
                    if e == 0:
                        if again:
                            pool.wait_ge(tiles_ready.sem, full(g - 1, "down4", GB // 2 - 1))
                    pool.tensor_tensor(hlo[:, e, :], h_sb[:, e % 2, :], hhi[:, e, :], ALU.subtract)\
                        .then_inc(h_lo.sem, 1)
                    if e == LN_NEXT_AT and not last:
                        rsqrt(g + 1, again, 1)

            rsqrt(0, False, 0)
            rsqrt(0, False, 1)
            body(0, False)
            with pool.Fori(1, NG - 1) as g:
                body(g, True)
            body(NG - 1, True, last=True)

        @block.scalar
        def _(act):
            def turned_rows_and_queries(g):
                for d in range(DB):
                    act.wait_ge(front_ready.sem, full(g, "xt", d))
                    act.activation(xnT[:, d, :], tile("xt", d), ACT.Copy).then_inc(act_front.sem, 1)
                for e in range(DB):
                    act.wait_ge(front_ready.sem, full(g, "q", e))
                    act.activation(qT[:, e, :], tile("q", e), ACT.Copy, scale=1.0 / 16.0)\
                        .then_inc(act_front.sem, 1)

            def exponentials(g):
                for j in range(GB):
                    act.wait_ge(neg_max.sem, neg_max.at(g, j // 2 + 1))
                    t = tile("s", j // 2)[:, (j % 2) * D:(j % 2 + 1) * D]
                    act.activation(pr[:, j, :], t, ACT.Exp, bias=nmax[:, j:j + 1], accum_out=rsum[:, j:j + 1])\
                        .then_inc(act_front.sem, 1)

            def attended(g):
                for n in range(GB // 2):
                    act.wait_ge(front_ready.sem, full(g, "at", n))
                    act.activation(atT[:, 2 * n:2 * n + 2, :, :].rearrange("p a b c -> p (a b c)"), tile("at", n),
                                   ACT.Copy).then_inc(act_front.sem, 1)

            def body(g, again, last=False):
                for n in range(2):
                    rotated = kres_done if n else kr_done
                    act.wait_ge(rotated.sem, rotated.at(g, 1))
                    if n == 0:
                        if again:
                            act.wait_ge(k_stored.sem, k_stored.at(g - 1, 1))
                    act.activation(ksplit[:, n, :], kr[:, 2, :] if n == 0 else kres, ACT.Copy)\
                        .then_inc(k_hi.sem, 1)
                for d in range(DB):
                    act.wait_ge(tiles_ready.sem, full(g, "xt2", d))
                    act.activation(xnT[:, d, :], tile("xt2", d), ACT.Copy).then_inc(act_emptied.sem, 1)
                act.wait_ge(tiles_ready.sem, full(g, "route", 0))
                act.activation(el, tile("route", 0)[:, 0:GB * E].rearrange("p (b e) -> p b e", b=GB), ACT.Exp,
                               scale=-1.0).then_inc(act_emptied.sem, 1)

                def gelu(e):
                    act.wait_ge(tiles_ready.sem, full(g, "gate", e))
                    if e == 0 and not again:
                        act.wait_ge(w_experts.sem, w_experts.at(0, 7))
                    if e >= 2:
                        act.wait_ge(dve_emptied.sem, empty(g, "up", e - 2))
                    else:
                        if again:
                            act.wait_ge(dve_emptied.sem, empty(g - 1, "up", ES - 2 + e))
                    act.activation(g_sb[:, e % 2, :], tile("gate", e), ACT.Gelu, bias=gb[:, e:e + 1])\
                        .then_inc(act_emptied.sem, 1)

                gelu(0)
                gelu(1)
                act.wait_ge(tiles_ready.sem, full(g, "ct", 0))
                act.activation(combT, tile("ct", 0)[0:ES, :], ACT.Copy).then_inc(act_emptied.sem, 1)
                for e in range(2, ES):
                    gelu(e)
                if not last:
                    turned_rows_and_queries(g + 1)
                for n in range(GB // 2):
                    act.wait_ge(q_rotated.sem, q_rotated.at(g, n + 1))
                    if again:
                        act.wait_ge(q_stored[n].sem, q_stored[n].at(g - 1, 2))
                    for k in range(2):
                        if k:
                            act.wait_ge(q_res_done.sem, q_res_done.at(g, n + 1))
                        act.activation(qsplit[:, 2 * n:2 * n + 2, k, :],
                                       (q_rot if k == 0 else qres)[:, 2 * n:2 * n + 2, :], ACT.Copy)\
                            .then_inc(q_hi.sem, 1)
                if not last:
                    exponentials(g + 1)
                for s in range(STEPS):
                    u = s - LAG
                    if 0 <= u < UNITS:
                        for kb in range(2):
                            act.wait_ge(tiles_ready.sem, full(g, "st", 2 * u + kb))
                            if u >= 2 or again:
                                used, count = weighted(g if u >= 2 else g - 1, (u - 2) % UNITS)
                                act.wait_ge(used, count)
                            act.activation(PT[:, 2 * (u % 2) + kb, :, :].rearrange("p a b -> p (a b)"),
                                           tile("st", 2 * u + kb, 2), ACT.Exp, scale=float(HD) ** -0.5)\
                                .then_inc(act_emptied.sem, 1)
                    u = s - LAG - 1
                    if u >= 0 and u % 2 == 1:
                        act.wait_ge(tiles_ready.sem, full(g, "pv", u // 2))
                        j = u // KV
                        if u % KV == 1:
                            if j or again:
                                act.wait_ge(u_stored.sem, u_stored.at(g, KV * j))
                        act.activation(U[:, u % KV - 1:u % KV + 1, :].rearrange("p h k -> p (h k)"),
                                       tile("pv", u // 2), ACT.Copy).then_inc(act_emptied.sem, 1)
                if not last:
                    attended(g + 1)
                for d in range(DB):
                    act.wait_ge(tiles_ready.sem, full(g, "xt4", d))
                    act.activation(xhi[:, d, :], tile("xt4", d), ACT.Copy).then_inc(x_hi.sem, 1)
                if not again:
                    act.wait_ge(ffn_consts.sem, ffn_consts.at(0, 7))
                for e in range(EB):
                    act.wait_ge(tiles_ready.sem, full(g, "up4", e))
                    if e >= 2 or again:
                        act.wait_ge(dve_emptied.sem, empty(g if e >= 2 else g - 1, "gate4", (e - 2) % EB))
                    act.activation(s_sb[:, e % 2, :], tile("up4", e), ACT.Silu, scale=ffn_c[:, 0:1])\
                        .then_inc(act_emptied.sem, 1)
                    if e:
                        hidden_hi(g, again, e - 1)
                hidden_hi(g, again, EB - 1)

            def hidden_hi(g, again, e):
                act.wait_ge(dve_emptied.sem, empty(g, "gate4", e))
                if e == 0:
                    if again:
                        act.wait_ge(tiles_ready.sem, full(g - 1, "down4", GB // 2 - 1))
                act.activation(hhi[:, e, :], h_sb[:, e % 2, :], ACT.Copy).then_inc(h_hi.sem, 1)

            turned_rows_and_queries(0)
            exponentials(0)
            attended(0)
            body(0, False)
            with act.Fori(1, NG - 1) as g:
                body(g, True)
            body(NG - 1, True, last=True)

        @block.tensor
        def _(pe):
            def done(i):
                i.then_inc(tiles_ready.sem, 1)

            def mm(out, lhsT, rhs, first=True, last=True):
                return pe.matmul(out, lhsT, rhs, start=first, stop=last)

            def transposes(body, phase, stage, g, ln, rows):
                for d in range(DB):
                    for held, count in before(body, phase, stage, d):
                        pe.wait_ge(held, count)
                    for j in range(GB):
                        if d == 0:
                            pe.wait_ge(ln_done[ln].sem, ln_done[ln].at(g, j + 1))
                        i = pe.transpose(tile(stage, d)[:, j * P:(j + 1) * P], rows[:, j, d * P:(d + 1) * P], ident[:])
                    (front_done if stage in FRONT else done)(i)

            def front_done(i):
                i.then_inc(front_ready.sem, 1)

            def project(body, phase, g, stage, w):
                for e in range(DB):
                    for held, count in before(body, phase, stage, e):
                        pe.wait_ge(held, count)
                    if stage == "q" and e == 0:
                        pe.wait_ge(act_front.sem, empty(g, "xt", DB - 1))
                    for d in range(DB):
                        i = mm(tile(stage, e), w[:, d, e * P:(e + 1) * P], xnT[:, d, :], d == 0, d == DB - 1)
                    front_done(i)

            def scores(body, phase, g):
                for n in range(GB // 2):
                    for held, count in before(body, phase, "s", n):
                        pe.wait_ge(held, count)
                    if n == 0:
                        pe.wait_ge(act_front.sem, empty(g, "q", DB - 1))
                        pe.wait_ge(dve_front.sem, empty(g, "k", DB - 1))
                        pe.wait_ge(ctxT_loaded.sem, ctxT_loaded.at(g, DB))
                    for j in (2 * n, 2 * n + 1):
                        for e in range(DB):
                            i = mm(tile("s", n)[:, (j % 2) * D:(j % 2 + 1) * D], qT[:, e, j * P:(j + 1) * P],
                                   kcat[:, e, j, :, :].rearrange("p a b -> p (a b)"), e == 0, e == DB - 1)
                    front_done(i)

            def values_and_attended(body, phase, g):
                for n in range(GB // 2):
                    for held, count in before(body, phase, "v", n):
                        pe.wait_ge(held, count)
                    for j in (2 * n, 2 * n + 1):
                        for d in range(DB):
                            i = mm(tile("v", n)[:, (j % 2) * D:(j % 2 + 1) * D], xnT[:, d, j * P:(j + 1) * P],
                                   wv0[:, d, :], d == 0, d == DB - 1)
                    front_done(i)
                for n in range(GB // 2):
                    for held, count in before(body, phase, "pt", n):
                        pe.wait_ge(held, count)
                    for j in (2 * n, 2 * n + 1):
                        pe.wait_ge(act_front.sem, empty(g, "s", n, j % 2 + 1))
                        for kb in range(2):
                            i = pe.transpose(tile("pt", n)[:, (j % 2) * D + kb * P:(j % 2) * D + (kb + 1) * P],
                                             pr[:, j, kb * P:(kb + 1) * P], ident[:])
                    front_done(i)
                pe.wait_ge(ctx_loaded.sem, ctx_loaded.at(g, 1))
                for n in range(GB // 2):
                    for held, count in before(body, phase, "at", n):
                        pe.wait_ge(held, count)
                    pe.wait_ge(dve_front.sem, empty(g, "pt", n))
                    for j in (2 * n, 2 * n + 1):
                        for d in range(DB):
                            for kb, v in enumerate((ctx_sb, v_sb)):
                                i = mm(tile("at", n)[:, (j % 2) * D + d * P:(j % 2) * D + (d + 1) * P],
                                       v[:, j, d * P:(d + 1) * P], prT[:, j, kb, :], kb == 0, kb == 1)
                    front_done(i)

            def output(body, phase, g):
                for n in range(GB // 2):
                    for held, count in before(body, phase, "o", n):
                        pe.wait_ge(held, count)
                    pe.wait_ge(act_front.sem, empty(g, "at", n))
                    for j in (2 * n, 2 * n + 1):
                        for d in range(DB):
                            i = mm(tile("o", n)[:, (j % 2) * D:(j % 2 + 1) * D], atT[:, j, d, :], wo0[:, d, :],
                                   d == 0, d == DB - 1)
                    front_done(i)

            def body(g, phase):
                again, last = phase in ("again", "last"), phase == "last"
                for held, count in before(g, phase, "k1", 0):
                    pe.wait_ge(held, count)
                if not again:
                    pe.wait_ge(w_attn1.sem, w_attn1.at(0, 12))
                for r, w in enumerate((wk1, wk1r)):
                    for j in range(GB):
                        i = mm(tile("k1", 0)[32 * j:32 * j + 32, r * T:(r + 1) * T], w[:], ctx_sb[:, j, :])
                done(i)
                for held, count in before(g, phase, "v1", 0):
                    pe.wait_ge(held, count)
                for j in range(GB):
                    for kb in range(2):
                        n = 2 * j + kb
                        i = mm(tile("v1", 0)[:, 32 * n:32 * n + 32], ctx_sb[:, j, kb * P:(kb + 1) * P], wv1[:])
                done(i)
                transposes(g, phase, "xt2", g, 1, xn)
                for held, count in before(g, phase, "route", 0):
                    pe.wait_ge(held, count)
                pe.wait_ge(act_emptied.sem, empty(g, "xt2", DB - 1))
                if not again:
                    pe.wait_ge(w_experts.sem, w_experts.at(0, 7))
                for j in range(GB):
                    for d in range(DB):
                        i = mm(tile("route", 0)[:, j * E:(j + 1) * E], xnT[:, d, j * P:(j + 1) * P], wa[:, d, :],
                               d == 0, d == DB - 1)
                done(i)

                def up(e):
                    for stage, w in (("gate", wg), ("up", wu)):
                        for held, count in before(g, phase, stage, e):
                            pe.wait_ge(held, count)
                        for d in range(DB):
                            i = mm(tile(stage, e), w[:, e, d, :], xnT[:, d, :], d == 0, d == DB - 1)
                        done(i)

                up(0)
                up(1)
                for held, count in before(g, phase, "ct", 0):
                    pe.wait_ge(held, count)
                pe.wait_ge(comb_done.sem, comb_done.at(g, 1))
                for j in range(GB):
                    i = pe.transpose(tile("ct", 0)[0:ES, j * P:(j + 1) * P], comb[:, j, :], ident[:])
                done(i)
                for n in range(GB // 2):
                    for held, count in before(g, phase, "bias2", n):
                        pe.wait_ge(held, count)
                    pe.wait_ge(act_emptied.sem, empty(g, "ct", 0))
                    for j in (2 * n, 2 * n + 1):
                        i = mm(tile("bias2", n)[:, (j % 2) * D:(j % 2 + 1) * D], combT[:, j * P:(j + 1) * P], b2[:])
                    done(i)
                for e in range(ES):
                    pe.wait_ge(dve_emptied.sem, empty(g, "up", e))
                    for n in range(GB // 2):
                        for held, count in before(g, phase, "down", 2 * e + n):
                            pe.wait_ge(held, count)
                        for j in (2 * n, 2 * n + 1):
                            i = mm(tile("down", 2 * e + n)[:, (j % 2) * D:(j % 2 + 1) * D],
                                   y_sb[:, e % 2, j * P:(j + 1) * P], w2[:, e, :])
                        done(i)
                    if e + 2 < ES:
                        up(e + 2)
                if not last:
                    transposes(g, phase, "xt", g + 1, 0, xn0)
                    project(g, phase, g + 1, "q", wq0)
                for n in range(GB // 2):
                    for stage, w in (("q1", wq1), ("q1r", wq1r)):
                        for held, count in before(g, phase, stage, n):
                            pe.wait_ge(held, count)
                        pe.wait_ge(ln_done[2].sem, ln_done[2].at(g, 2 * n + 2))
                        done(mm(tile(stage, n), w[:], xn[:, 2 * n:2 * n + 2, :].rearrange("p a b -> p (a b)")))
                if not last:
                    project(g, phase, g + 1, "k", wk0)
                    scores(g, phase, g + 1)
                for s in range(STEPS):
                    if s < UNITS:
                        j, kv = divmod(s, KV)
                        if kv == 0:
                            pe.wait_ge(q_stacked[j].sem, q_stacked[j].at(g, 3))
                            if j == 0:
                                pe.wait_ge(k_stacked.sem, k_stacked.at(g, 6))
                                if not again:
                                    pe.wait_ge(pads.sem, pads.at(0, 4))
                        for hh in range(KV):
                            h = KV * kv + hh
                            for held, count in before(g, phase, "smax", 4 * s + hh):
                                pe.wait_ge(held, count)
                            for qb in range(2):
                                i = mm(tile("smax", 4 * s + hh)[:, qb * T:(qb + 1) * T],
                                       QS[:, j, h, qb * P:(qb + 1) * P], KS[:, j, kv, :])
                            done(i)
                    if s % KV == 0 and s >= KV and s // KV - 1 < GB:
                        j = s // KV - 1
                        for held, count in before(g, phase, "mt", j):
                            pe.wait_ge(held, count)
                        pe.wait_ge(dve_emptied.sem, empty(g, "smax", 16 * j + 15))
                        done(pe.transpose(tile("mt", j)[0:2 * H, 0:P], M[:, j, :], ident[:]))
                    u = s - LAG
                    if 0 <= u < UNITS:
                        j, kv = divmod(u, KV)
                        if kv == 0:
                            pe.wait_ge(m_stacked[j].sem, m_stacked[j].at(g, 2))
                        for kb in range(2):
                            for held, count in before(g, phase, "st", 2 * u + kb):
                                pe.wait_ge(held, count)
                            for half in range(2):
                                i = mm(tile("st", 2 * u + kb, 2)[:, half * 512:(half + 1) * 512],
                                       KS[:, j, kv, kb * P:(kb + 1) * P],
                                       QS[:, j, KV * kv + 2 * half:KV * kv + 2 * half + 2, :]
                                       .rearrange("p a b -> p (a b)"))
                            done(i)
                    u = s - LAG - 1
                    if 0 <= u < UNITS:
                        j, kv = divmod(u, KV)
                        if u % 2 == 0:
                            for held, count in before(g, phase, "pv", u // 2):
                                pe.wait_ge(held, count)
                        pe.wait_ge(act_emptied.sem, empty(g, "st", 2 * u + 1))
                        if u == 0:
                            pe.wait_ge(dve_emptied.sem, empty(g, "v1", 0))
                        for kb in range(2):
                            for hh in range(KV):
                                i = mm(tile("pv", u // 2)[32 * hh:32 * hh + 32, (u % 2) * T:(u % 2 + 1) * T],
                                       Vs[:, j, kb, kv, :], PT[:, 2 * (u % 2) + kb, hh // 2, (hh % 2) * T:(hh % 2 + 1) * T],
                                       kb == 0, kb == 1)
                        if u % 2:
                            done(i)
                        else:
                            i.then_inc(pv_even.sem, 1)
                if not last:
                    values_and_attended(g, phase, g + 1)
                for n in range(GB // 2):
                    for held, count in before(g, phase, "o1", n):
                        pe.wait_ge(held, count)
                    for j in (2 * n, 2 * n + 1):
                        pe.wait_ge(normed.sem, normed.at(g, j + 1))
                        i = mm(tile("o1", n)[:, (j % 2) * T:(j % 2 + 1) * T], wo1[:], num[:, j, :])
                    done(i)
                if not last:
                    output(g, phase, g + 1)
                transposes(g, phase, "xt4", g, 3, xn)
                for e in range(EB):
                    for k, stage in enumerate(("up4", "gate4")):
                        for held, count in before(g, phase, stage, e):
                            pe.wait_ge(held, count)
                        if e == 0 and k == 0:
                            pe.wait_ge(dve_emptied.sem, empty(g, "xt4", DB - 1))
                            if not again:
                                pe.wait_ge(ffn_consts.sem, ffn_consts.at(0, 7))
                        n = 0
                        for part in (xhi, xlo):
                            for d in range(DB):
                                i = mm(tile(stage, e), tern[k][:, d * DE + e * P:d * DE + (e + 1) * P], part[:, d, :],
                                       n == 0, n == 3)
                                n += 1
                        done(i)
                for n in range(GB // 2):
                    for held, count in before(g, phase, "down4", n):
                        pe.wait_ge(held, count)
                    for j in (2 * n, 2 * n + 1):
                        k = 0
                        for part, sem in ((hhi, h_hi), (hlo, h_lo)):
                            for e in range(EB):
                                if n == 0 and j == 0:
                                    pe.wait_ge(sem.sem, sem.at(g, e + 1))
                                i = mm(tile("down4", n)[:, (j % 2) * D:(j % 2 + 1) * D], part[:, e, j * P:(j + 1) * P],
                                       tern[2][:, e * D:(e + 1) * D], k == 0, k == 2 * EB - 1)
                                k += 1
                    done(i)

            pe.wait_ge(consts.sem, consts.at(0, 1))
            transposes(-1, "front", "xt", 0, 0, xn0)
            pe.wait_ge(w_attn0.sem, w_attn0.at(0, 2))
            project(-1, "front", 0, "q", wq0)
            project(-1, "front", 0, "k", wk0)
            scores(-1, "front", 0)
            pe.wait_ge(w_attn0v.sem, w_attn0v.at(0, 2))
            values_and_attended(-1, "front", 0)
            output(-1, "front", 0)
            body(0, "first")
            with pe.Fori(1, NG - 1) as g:
                body(g, "again")
            body(NG - 1, "last")

        @block.vector
        def _(dve):
            def layernorm(g, again, n, src, dst):
                for j in range(GB):
                    dve.bn_stats(stats[:, j, :], src[:, j, :]).then_inc(ln_stats[n].sem, 1)
                for j in range(GB):
                    dve.wait_ge(ln_stats[n].sem, ln_stats[n].at(g, j + 1))
                    if again:
                        dve.sem_inc(passed.sem, 1)
                    i = dve.bn_aggr(mv[:, j, :], stats[:, j, :])
                i.then_inc(ln_mv[n].sem, 1)
                dve.wait_ge(ln_rstd[n].sem, ln_rstd[n].at(g, 1))
                dve.wait_ge(ln_mv[n].sem, ln_mv[n].at(g, 1))
                for j in range(GB):
                    dve.tensor_scalar(dst[:, j, :], src[:, j, :], mv[:, j, 0:1], rstd[:, j:j + 1], ALU.subtract,
                                      ALU.mult).then_inc(ln_done[n].sem, 1)

            def quantise(n):
                steps = [4 * n]

                def step(i):
                    steps[0] += 1
                    i.then_inc(quant_step.sem, 1)
                    dve.wait_ge(quant_step.sem, quant_step.at(0, steps[0]))

                dve.wait_ge(raw_in.sem, raw_in.at(0, n + 1))
                dve.tensor_reduce(wsum[:, n, 0:1], raw, AX.X, ALU.add, apply_absolute_value=True)\
                    .then_inc(abs_sums.sem, 1)
                dve.wait_ge(abs_total.sem, abs_total.at(0, n + 1))
                step(dve.tensor_scalar(wscale[:, n:n + 1], wsum[:, n, 1:2], 1.0 / (D * DE), QUANT_EPS, ALU.mult, ALU.add))
                step(dve.tensor_scalar(half[:, n, 0:1], wscale[:, n:n + 1], 0.5, None, ALU.mult))
                step(dve.tensor_scalar(half[:, n, 1:2], wscale[:, n:n + 1], -0.5, None, ALU.mult))
                step(dve.tensor_scalar(tpos, raw, half[:, n, 0:1], None, ALU.is_gt))
                dve.scalar_tensor_tensor(out=tern[n][:], in0=raw, scalar=half[:, n, 1:2], in1=tpos, op0=ALU.is_lt,
                                         op1=ALU.subtract).then_inc(tern_done.sem, 1)

            def ffn_scales():
                def step(n, i):
                    i.then_inc(ffn_consts.sem, 1)
                    dve.wait_ge(ffn_consts.sem, ffn_consts.at(0, n))

                step(1, dve.tensor_scalar(ffn_c[:, 0:1], wscale[:, 0:1], -1.0, None, ALU.mult))
                step(2, dve.reciprocal(ffn_c[:, 2:3], ffn_c[:, 0:1]))
                step(3, dve.tensor_scalar(ffn_c[:, 1:2], ffn_c[:, 2:3], 0.5, None, ALU.mult))
                step(4, dve.tensor_tensor(ffn_c[:, 2:3], wscale[:, 1:2], wscale[:, 2:3], ALU.mult))
                step(5, dve.tensor_tensor(ffn_c[:, 3:4], ffn_c[:, 0:1], ffn_c[:, 2:3], ALU.mult))
                step(6, dve.tensor_scalar(ffn_c[:, 2:3], ffn_c[:, 3:4], 2.0, None, ALU.mult))
                dve.wait_ge(tern_done.sem, tern_done.at(0, 3))
                dve.tensor_copy(ffn_c[:, 3:4], ffn_c[:, 2:3]).then_inc(ffn_consts.sem, 1)

            out = dve_emptied.sem

            def next_rows(g, again):
                dve.wait_ge(x_loaded.sem, x_loaded.at(g, 1))
                layernorm(g, again, 0, x_in, xn0)

            def keys(g):
                for e in range(DB):
                    dve.wait_ge(front_ready.sem, full(g, "k", e))
                    dve.tensor_copy(kcat[:, e, :, 1, :], tile("k", e).rearrange("p (b k) -> p b k", b=GB))\
                        .then_inc(dve_front.sem, 1)

            def maxima(g):
                for n in range(GB // 2):
                    dve.wait_ge(front_ready.sem, full(g, "s", n))
                    dve.tensor_reduce(nmax[:, 2 * n:2 * n + 2], tile("s", n).rearrange("p (a b) -> p a b", a=2), AX.X,
                                      ALU.max, negate=True).then_inc(neg_max.sem, 1)

            def values_and_turned(g):
                for n in range(GB // 2):
                    dve.wait_ge(front_ready.sem, full(g, "v", n))
                    dve.tensor_copy(v_sb[:, 2 * n:2 * n + 2, :].rearrange("p a b -> p (a b)"), tile("v", n))\
                        .then_inc(dve_front.sem, 1)
                for n in range(GB // 2):
                    dve.wait_ge(front_ready.sem, full(g, "pt", n))
                    dve.tensor_copy(prT[:, 2 * n:2 * n + 2, :, :].rearrange("p a b c -> p (a b c)"), tile("pt", n))\
                        .then_inc(dve_front.sem, 1)

            def output(g):
                dve.wait_ge(act_front.sem, empty(g, "s", GB // 2 - 1))
                dve.reciprocal(rinv[:], rsum[:]).then_inc(sums_inv.sem, 1)
                dve.wait_ge(sums_inv.sem, sums_inv.at(g, 1))
                for n in range(GB // 2):
                    dve.wait_ge(front_ready.sem, full(g, "o", n))
                    for j in (2 * n, 2 * n + 1):
                        i = dve.scalar_tensor_tensor(out=x_res[:, j, :], in0=tile("o", n)[:, (j % 2) * D:(j % 2 + 1) * D],
                                                     scalar=rinv[:, j:j + 1], in1=x_in[:, j, :], op0=ALU.mult,
                                                     op1=ALU.add)
                        i.then_inc(dve_front.sem, 1)

            def expert_rows(g, again):
                dve.wait_ge(dve_front.sem, empty(g, "o", GB // 2 - 1))
                layernorm(g, again, 1, x_res, xn)
                dve.wait_ge(ln_done[1].sem, ln_done[1].at(g, GB))
                dve.tensor_tensor(acc[:].rearrange("p a b -> p (a b)"), x_res[:].rearrange("p a b -> p (a b)"),
                                  xn[:].rearrange("p a b -> p (a b)"), ALU.add).then_inc(base_sum.sem, 1)

            def body(g, again, last=False):
                dve.wait_ge(tiles_ready.sem, full(g, "k1", 0))
                if not again:
                    dve.wait_ge(w_attn1.sem, w_attn1.at(0, 12))
                    dve.wait_ge(pads.sem, pads.at(0, 4))
                kt = tile("k1", 0)
                for r in range(2):
                    dve.scalar_tensor_tensor(out=kr[:, r, :], in0=kt[:, r * T:(r + 1) * T], scalar=bk1[:, r:r + 1],
                                             in1=rope[:, 2 + r, :], op0=ALU.add, op1=ALU.mult).then_inc(out, 1)
                dve.wait_ge(dve_emptied.sem, empty(g, "k1", 0))
                dve.tensor_tensor(kr[:, 2, :], kr[:, 0, :], kr[:, 1, :], ALU.add).then_inc(kr_done.sem, 1)
                dve.wait_ge(tiles_ready.sem, full(g, "v1", 0))
                if again:
                    dve.wait_ge(tiles_ready.sem, full(g - 1, "pv", UNITS // 2 - 1))
                dve.tensor_tensor(Vs[:].rearrange("p b k h c -> p (b k) h c")[:, :, :, 0:HD],
                                  tile("v1", 0)[:, 0:8 * 32].rearrange("p (n h d) -> p n h d", n=8, h=KV),
                                  bv1[:].rearrange("p (o h d) -> p o h d", o=1, h=KV).broadcast_to([P, 8, KV, HD]),
                                  ALU.add).then_inc(out, 1)
                dve.wait_ge(kr_done.sem, kr_done.at(g, 1))
                dve.wait_ge(k_hi.sem, k_hi.at(g, 1))
                dve.tensor_tensor(kres, kr[:, 2, :], ksplit[:, 0, :], ALU.subtract).then_inc(kres_done.sem, 1)
                dve.wait_ge(kres_done.sem, kres_done.at(g, 1))
                dve.wait_ge(k_hi.sem, k_hi.at(g, 2))
                dve.tensor_tensor(ksplit[:, 2, :], kres, ksplit[:, 1, :], ALU.subtract)\
                    .then_inc(k_split_done.sem, 1)
                dve.wait_ge(act_emptied.sem, empty(g, "route", 0))
                dve.tensor_scalar(el1, el, 1.0, None, ALU.add).then_inc(route_step.sem, 1)
                dve.wait_ge(route_step.sem, route_step.at(g, 1))
                dve.reciprocal(prob, el1).then_inc(route_step.sem, 1)
                dve.wait_ge(route_step.sem, route_step.at(g, 2))
                if again:
                    dve.sem_inc(passed.sem, 1)
                for j in range(GB):
                    dve.max(top[:, j, :], prob[:, j, :]).then_inc(top_step.sem, 1)
                for j in range(GB):
                    dve.wait_ge(top_step.sem, top_step.at(g, j + 1))
                    if again:
                        dve.sem_inc(passed.sem, 1)
                    dve.max_index(topi[:, j, :], top[:, j, :], prob[:, j, :]).then_inc(top_step.sem, 1)
                dve.tensor_tensor(psum2[:], top[:, :, 0:1], top[:, :, 1:2], ALU.add).then_inc(route_step.sem, 1)
                dve.wait_ge(route_step.sem, route_step.at(g, 3))
                dve.reciprocal(pinv[:], psum2[:]).then_inc(route_step.sem, 1)
                dve.wait_ge(top_step.sem, top_step.at(g, 2 * GB))
                dve.tensor_copy(topf[:], topi[:, :, 0:2]).then_inc(route_step.sem, 1)
                dve.wait_ge(route_step.sem, route_step.at(g, 4))
                for j in range(GB):
                    dve.tensor_scalar(topw[:, j, :], top[:, j, 0:2], pinv[:, j, 0:1], None, ALU.mult)\
                        .then_inc(route_step.sem, 1)
                dve.wait_ge(route_step.sem, route_step.at(g, 5 + GB))
                for j in range(GB):
                    for k, hot in enumerate((hot0, hot1)):
                        dve.tensor_scalar(hot[:, j, :], iota_e[:], topf[:, j, k:k + 1], topw[:, j, k:k + 1],
                                          ALU.is_equal, ALU.mult).then_inc(hots.sem, 1)
                dve.wait_ge(hots.sem, hots.at(g, 2 * GB))
                dve.tensor_tensor(comb[:, :, 0:E], hot0, hot1, ALU.add).then_inc(comb_done.sem, 1)

                def product(e):
                    dve.wait_ge(tiles_ready.sem, full(g, "up", e))
                    dve.wait_ge(act_emptied.sem, empty(g, "gate", e))
                    if e >= 2:
                        dve.wait_ge(tiles_ready.sem, full(g, "down", 2 * (e - 2) + 1))
                    else:
                        if again:
                            dve.wait_ge(tiles_ready.sem, full(g - 1, "down", 2 * (ES - 2 + e) + 1))
                    dve.scalar_tensor_tensor(out=y_sb[:, e % 2, :], in0=tile("up", e), scalar=ub[:, e:e + 1],
                                             in1=g_sb[:, e % 2, :], op0=ALU.add, op1=ALU.mult).then_inc(out, 1)

                product(0)
                product(1)
                for n in range(GB // 2):
                    dve.wait_ge(tiles_ready.sem, full(g, "bias2", n))
                    dve.wait_ge(base_sum.sem, base_sum.at(g, 1))
                    half = acc[:, 2 * n:2 * n + 2, :].rearrange("p a b -> p (a b)")
                    dve.tensor_tensor(half, half, tile("bias2", n), ALU.add).then_inc(out, 1)
                dve.wait_ge(comb_done.sem, comb_done.at(g, 1))
                for e in range(ES):
                    for n in range(GB // 2):
                        dve.wait_ge(tiles_ready.sem, full(g, "down", 2 * e + n))
                        if e == 0:
                            dve.wait_ge(dve_emptied.sem, empty(g, "bias2", n))
                        for j in (2 * n, 2 * n + 1):
                            if e:
                                dve.wait_ge(dve_emptied.sem, empty(g, "down", 2 * (e - 1) + n, j % 2 + 1))
                            t = tile("down", 2 * e + n)[:, (j % 2) * D:(j % 2 + 1) * D]
                            dve.scalar_tensor_tensor(out=acc[:, j, :], in0=t, scalar=comb[:, j, e:e + 1],
                                                     in1=acc[:, j, :], op0=ALU.mult, op1=ALU.add)\
                                .then_inc(out, 1)
                    if e + 2 < ES:
                        product(e + 2)
                    if e == ROWS_NEXT_AT and not last:
                        next_rows(g + 1, again)
                    if not again and e in QUANT_AT:
                        quantise(QUANT_AT.index(e))
                if not again:
                    ffn_scales()
                dve.wait_ge(dve_emptied.sem, empty(g, "down", 2 * ES - 1))
                layernorm(g, again, 2, acc, xn)
                for n in range(GB // 2):
                    for r, stage in enumerate(("q1", "q1r")):
                        dve.wait_ge(tiles_ready.sem, full(g, stage, n))
                        dve.scalar_tensor_tensor(out=qr[:, r, :, :].rearrange("p b k -> p b k"),
                                                 in0=tile(stage, n).rearrange("p (b k) -> p b k", b=2),
                                                 scalar=bq1[:, r:r + 1],
                                                 in1=rope[:, r:r + 1, :].broadcast_to([P, 2, T]),
                                                 op0=ALU.add, op1=ALU.mult).then_inc(out, 1)
                    dve.wait_ge(dve_emptied.sem, empty(g, "q1r", n))
                    if n == 0:
                        if again:
                            dve.wait_ge(stored.sem, stored.at(g - 1, 1))
                    dve.tensor_tensor(q_rot[:, 2 * n:2 * n + 2, :], qr[:, 0, :, :], qr[:, 1, :, :], ALU.add)\
                        .then_inc(q_rotated.sem, 1)
                    dve.wait_ge(q_rotated.sem, q_rotated.at(g, n + 1))
                    dve.wait_ge(q_hi.sem, q_hi.at(g, 2 * n + 1))
                    dve.tensor_tensor(qres[:, 2 * n:2 * n + 2, :], q_rot[:, 2 * n:2 * n + 2, :],
                                      qsplit[:, 2 * n:2 * n + 2, 0, :], ALU.subtract).then_inc(q_res_done.sem, 1)
                    dve.wait_ge(q_res_done.sem, q_res_done.at(g, n + 1))
                    dve.wait_ge(q_hi.sem, q_hi.at(g, 2 * n + 2))
                    dve.tensor_tensor(qsplit[:, 2 * n:2 * n + 2, 2, :], qres[:, 2 * n:2 * n + 2, :],
                                      qsplit[:, 2 * n:2 * n + 2, 1, :], ALU.subtract).then_inc(q_split_done.sem, 1)
                    if n == 0 and not last:
                        keys(g + 1)
                if not last:
                    maxima(g + 1)
                for s in range(STEPS):
                    if s < UNITS:
                        j, kv = divmod(s, KV)
                        for hh in range(KV):
                            h = KV * kv + hh
                            dve.wait_ge(tiles_ready.sem, full(g, "smax", 4 * s + hh))
                            dve.tensor_reduce(M[:, j, 2 * h:2 * h + 2],
                                              tile("smax", 4 * s + hh).rearrange("p (a b) -> p a b", a=2), AX.X,
                                              ALU.max).then_inc(out, 1)
                    if s % KV == 0 and s >= KV and s // KV - 1 < GB:
                        j = s // KV - 1
                        dve.wait_ge(tiles_ready.sem, full(g, "mt", j))
                        if again:
                            dve.wait_ge(m_stacked[j].sem, m_stacked[j].at(g - 1, 2))
                        t = tile("mt", j)[0:2 * H, 0:P]
                        dve.tensor_scalar(mhi[:, j, :], t, -1.0, None, ALU.mult).then_inc(out, 1)
                        dve.wait_ge(dve_emptied.sem, empty(g, "mt", j, 1))
                        dve.scalar_tensor_tensor(out=mlo[:, j, :], in0=t, scalar=-1.0, in1=mhi[:, j, :],
                                                 op0=ALU.mult, op1=ALU.subtract).then_inc(out, 1)
                for j in range(GB):
                    if j == GB - 1 and not last:
                        values_and_turned(g + 1)
                    dve.wait_ge(nd_loaded[j].sem, nd_loaded[j].at(g, 2))
                    dve.reciprocal(den[:, j, :], den[:, j, :]).then_inc(den_inv.sem, 1)
                    dve.wait_ge(den_inv.sem, den_inv.at(g, j + 1))
                    dve.tensor_tensor(num[:, j, :], num[:, j, :], den[:, j, :], ALU.mult).then_inc(normed.sem, 1)
                for n in range(GB // 2):
                    dve.wait_ge(tiles_ready.sem, full(g, "o1", n))
                    dve.scalar_tensor_tensor(out=x3[:, 2 * n:2 * n + 2, :].rearrange("p a b -> p (a b)"),
                                             in0=tile("o1", n), scalar=bo1[:, 0:1],
                                             in1=acc[:, 2 * n:2 * n + 2, :].rearrange("p a b -> p (a b)"),
                                             op0=ALU.add, op1=ALU.add).then_inc(out, 1)
                dve.wait_ge(dve_emptied.sem, empty(g, "o1", GB // 2 - 1))
                layernorm(g, again, 3, x3, xn)
                if not last:
                    output(g + 1)
                for d in range(DB):
                    dve.wait_ge(x_hi.sem, x_hi.at(g, d + 1))
                    dve.wait_ge(tiles_ready.sem, full(g, "xt4", d))
                    dve.tensor_tensor(xlo[:, d, :], tile("xt4", d), xhi[:, d, :], ALU.subtract).then_inc(out, 1)
                for e in range(EB):
                    dve.wait_ge(tiles_ready.sem, full(g, "gate4", e))
                    dve.wait_ge(act_emptied.sem, empty(g, "up4", e))
                    if e >= 2:
                        dve.wait_ge(h_lo.sem, h_lo.at(g, e - 1))
                        dve.wait_ge(h_hi.sem, h_hi.at(g, e - 1))
                    else:
                        if again:
                            dve.wait_ge(h_lo.sem, h_lo.at(g - 1, EB - 1 + e))
                        if again:
                            dve.wait_ge(h_hi.sem, h_hi.at(g - 1, EB - 1 + e))
                    dve.scalar_tensor_tensor(out=h_sb[:, e % 2, :], in0=tile("gate4", e), scalar=ffn_c[:, 1:2],
                                             in1=s_sb[:, e % 2, :], op0=ALU.mult, op1=ALU.mult)\
                        .then_inc(out, 1)
                    if e == LN_NEXT_AT and not last:
                        expert_rows(g + 1, again)
                for n in range(GB // 2):
                    dve.wait_ge(tiles_ready.sem, full(g, "down4", n))
                    for j in (2 * n, 2 * n + 1):
                        dve.scalar_tensor_tensor(out=y_out[:, j, :], in0=tile("down4", n)[:, (j % 2) * D:(j % 2 + 1) * D],
                                                 scalar=ffn_c[:, 3:4], in1=x3[:, j, :], op0=ALU.mult, op1=ALU.add)\
                            .then_inc(out, 1)

            next_rows(0, False)
            keys(0)
            maxima(0)
            values_and_turned(0)
            output(0)
            expert_rows(0, False)
            body(0, False)
            with dve.Fori(1, NG - 1) as g:
                body(g, True)
            body(NG - 1, True, last=True)


def layouts(i):
    f = lambda v: np.ascontiguousarray(v)
    heads = np.arange(P).reshape(H, HD)
    by_d = heads.T.reshape(-1)
    turned = np.roll(heads, -(HD // 2), axis=1).T.reshape(-1)
    kheads = np.arange(KV * HD).reshape(KV, HD)
    k_by_d = kheads.T.reshape(-1)
    k_turned = np.roll(kheads, -(HD // 2), axis=1).T.reshape(-1)
    pv = np.arange(P).reshape(KV, KV, HD).transpose(2, 1, 0).reshape(-1)
    Wq, Wk, Wv, Wo = (i[f"L1_xattn_W{n}"] for n in "qkvo")
    bq, bk = i["L1_xattn_bq"], i["L1_xattn_bk"]
    halves = lambda w: f(w.T.reshape(DB, P, DE).transpose(1, 0, 2).reshape(P, DB * DE))
    return {
        "x": f(i["x"]), "ctx": f(i["ctx_2048"]),
        "ctxT": f(i["ctx_2048"].transpose(0, 2, 1).reshape(B, DB, P, P)),
        "wq0": f(i["L0_xattn_wq"].T), "wk0": f(i["L0_xattn_wk"].T), "wv0": f(i["L0_xattn_wv"].T),
        "wo0": f(i["L0_xattn_wo"].T), "wa": f(i["L0_ffn_wa"]),
        "wg": f(np.concatenate([i["L0_ffn_rg"], i["L0_ffn_sg"]])), "wu": f(np.concatenate([i["L0_ffn_rw1"], i["L0_ffn_sw1"]])),
        "w2": f(np.concatenate([i["L0_ffn_rw2"], i["L0_ffn_sw2"]])),
        "gb": f(np.concatenate([i["L0_ffn_rgb"], i["L0_ffn_sgb"]]).T), "ub": f(np.concatenate([i["L0_ffn_rb1"], i["L0_ffn_sb1"]]).T),
        "b2": f(np.concatenate([i["L0_ffn_rb2"], i["L0_ffn_sb2"]])),
        "wq1": f(Wq[by_d].T), "wq1r": f(Wq[turned].T), "wk1": f(Wk[k_by_d].T), "wk1r": f(Wk[k_turned].T), "wv1": f(Wv.T),
        "bq1": f(np.stack([bq[by_d], bq[turned]], axis=1)),
        "bk1": f(np.tile(np.stack([bk[k_by_d], bk[k_turned]], axis=1), (GB, 1))),
        "bv1": f(i["L1_xattn_bv"][None]), "wo1": f(Wo.T[pv]), "bo1": f(i["L1_xattn_bo"][:, None]),
        "wup": halves(i["L1_ffn_W_up"]), "wgate": halves(i["L1_ffn_W_gate"]),
        "wdown": f(i["L1_ffn_W_down"].T.reshape(EB, P, D).transpose(1, 0, 2).reshape(P, EB * D)),
        "rope": rope_tables(), "iota": np.arange(E, dtype=np.float32)[None],
    }


def kernel(**inputs):
    import concourse.bacc as bacc
    from concourse.bass_utils import run_bass_kernel_spmd

    arrays = layouts({k: np.asarray(v) for k, v in inputs.items() if k != "mask_BxSx4224_bf0"})
    nc = bacc.Bacc("TRN2", target_bir_lowering=False, num_devices=1)
    aps = {n: nc.dram_tensor(f"in_{n}", v.shape, mybir.dt.from_np(v.dtype), kind="ExternalInput").ap() for n, v in arrays.items()}
    aps["out"] = nc.dram_tensor("out", (B, P, D), F32, kind="ExternalOutput").ap()
    build(nc, aps)
    r = run_bass_kernel_spmd(nc, [{f"in_{n}": v for n, v in arrays.items()}], core_ids=[0])
    return r.results[0]["out"]
```

```python
from contextlib import ExitStack

import numpy as np

import concourse.bass as bass
from concourse import mybir

ALU = mybir.AluOpType
ACT = mybir.ActivationFunctionType
AX = mybir.AxisListType
F32 = mybir.dt.float32
BF16 = mybir.dt.bfloat16
F16 = mybir.dt.float16
U32 = mybir.dt.uint32

P = 128
B = 16
D = 256
DB = D // P
GB = 4
NG = B // GB
TOK = GB * P
E = 16
ES = 18
F = 128
DE = 1024
EB = DE // P
H = 16
KV = 4
HD = P // H
T = D
TERMS = 3
ROWS = 48
MROW = ROWS
UNITS = GB * KV
SCORES_AT = 1
LAG = 4
STEPS = UNITS + LAG + 1
SMAX_BANKS = 1
SMAX_TILES = KV // SMAX_BANKS
MT_AT = 2
GPSIMD_FROM = 2
KEYS_AT = 1
LN_NEXT_AT = 7
ROWS_NEXT_AT = 8
THIRDS = 3
ET = ES // THIRDS
CHUNK = ET * D
CHUNKS = 3 * THIRDS
SLOTS = 4
MAG_AT = {6: 2, 7: 3, 8: 3}
SCALES_AT = {1: 0, 2: 4}
HIGH_AT = {3: 0, 4: 1, 5: 2, 6: 4, 7: 5, 8: 6}
X_SCALE = 2048.0
SPLIT_TOP = 32768.0
TINY = 1e-12
ABS_AT = (7, 11, 15)
QUANT_AT = (8, 12, 16)
LN_EPS = 1e-5
QUANT_EPS = 1e-8


BANKS = 8
PV_BANK = 7


FRONT = ("xt", "q", "k", "s", "v", "pt", "at", "o")


def tile_order():
    pairs = range(GB // 2)
    t = [("xt2", d, 1, "act", 1) for d in range(DB)]
    t += [("k1", 0, 1, "dve", 2), ("v1", 0, 1, "dve", 1)]
    t += [("route", 0, 1, "act", 1), ("gate", 0, 1, "act", 1), ("up", 0, 1, "dve", 1)]
    t += [("gate", 1, 1, "act", 1), ("up", 1, 1, "dve", 1), ("ct", 0, 1, "act", 1)]
    t += [("bias2", n, 1, "dve", 1) for n in pairs]
    for e in range(ES):
        if e == ES - 1:
            t += [("xt", d, 1, "act", 1) for d in range(DB)]
        t += [("down", 2 * e + n, 1, "dve", 2) for n in pairs]
        if e + 2 < ES:
            t += [("gate", e + 2, 1, "act", 1), ("up", e + 2, 1, "dve", 1)]
    t += [("q", e, 1, "act", 1) for e in range(DB)]
    t += [("q1", j, 1, "dve", 2) for j in range(GB)]
    t += [("k", e, 1, "dve", 1) for e in range(DB)]
    for s in range(STEPS):
        for n in range(SMAX_TILES):
            if n == MT_AT and s % 2 == 0 and 0 <= s // 2 - 1 < UNITS // 2:
                t += [("mt", s // 2 - 1, 1, "dve", 2)]
            if s < UNITS:
                t += [("smax", SMAX_TILES * s + n, SMAX_BANKS, "dve", 1)]
        if s == SCORES_AT:
            t += [("s", n, 1, "act", 2) for n in pairs]
        if 0 <= s - LAG < UNITS:
            t += [("st", 2 * (s - LAG) + kb, 2, "act", 1) for kb in range(2)]
        if 0 <= s - LAG - 1 < UNITS and (s - LAG - 1) % 2:
            t += [("pv", (s - LAG - 1) // 2, 0, "act", 1)]
    t += [("v", n, 1, "dve", 1) for n in pairs]
    t += [("pt", n, 1, "dve", 1) for n in pairs]
    t += [("at", n, 1, "act", 1) for n in pairs]
    t += [("o1", n, 1, "dve", 1) for n in pairs]
    t += [("o", n, 1, "dve", 2) for n in pairs]
    t += [("xt4", d, 1, "dve", 1) for d in range(DB)]
    for e in range(EB):
        t += [("up4", e, 1, "act", 1), ("gate4", e, 1, "dve", 1)]
    t += [("down4", n, 1, "dve", 2) for n in pairs]
    return t


class Ring:

    def __init__(self):
        self.bank, self.full, self.empty = {}, {}, {}
        self.counts = {(kind, front): 0 for kind in ("full", "act", "dve") for front in (False, True)}
        order, places, at = tile_order(), [], 0
        for stage, n, banks, engine, parts in order:
            if at % PV_BANK + banks > PV_BANK:
                at += PV_BANK - at % PV_BANK
            places.append([PV_BANK] if not banks else [(at + b) % PV_BANK for b in range(banks)])
            at += banks
            front = stage in FRONT
            self.counts["full", front] += 1
            self.counts[engine, front] += parts
            self.bank[stage, n] = places[-1][0]
            self.full[stage, n] = self.counts["full", front]
            self.empty[stage, n] = (engine, self.counts[engine, front])
        self.after = {}
        owner = {}
        for body, phase in enumerate(("front", "first", "again", "last")):
            for (stage, n, *_), banks in zip(order, places):
                if (phase == "front" and stage not in FRONT) or (phase == "last" and stage in FRONT):
                    continue
                self.after[phase, stage, n] = sorted({(owner[b][0] < body, *owner[b][1:]) for b in banks if b in owner})
                for b in banks:
                    owner[b] = (body, stage, n)


RING = Ring()
PARTS = {stage: parts for stage, _, _, _, parts in tile_order()}


def rope_tables():
    inv = (np.float32(1.0) / np.float32(10000.0) ** (np.arange(0, HD, 2, dtype=np.float32) / np.float32(HD)))
    freq = np.arange(T, dtype=np.float32)[:, None] * inv.astype(np.float32)[None, :]
    emb = np.concatenate([freq, freq], axis=-1).astype(np.float32)
    cos, sin = np.cos(emb).astype(np.float32), np.sin(emb).astype(np.float32)
    sin[:, : HD // 2] = -sin[:, : HD // 2]
    q = [np.repeat(a.T, H, axis=0) for a in (cos, sin)]
    k = [np.tile(np.repeat(a.T, KV, axis=0), (GB, 1)) for a in (cos, sin)]
    return np.ascontiguousarray(np.stack(q + k, axis=1))


def build(nc, a):
    with ExitStack() as ctx:
        def sb(name, shape, dt=F32):
            return ctx.enter_context(nc.sbuf_tensor(name, shape, dt))

        class Sem:

            def __init__(self, name, per, step=1):
                self.sem, self.per, self.step = ctx.enter_context(nc.semaphore(name)), per, step

            def at(self, g, n):
                return (g * self.per + n) * self.step

        ident = sb("ident", [P, P])
        wq0, wk0, wv0, wo0 = (sb(f"w{n}0", [P, DB, D]) for n in "qkvo")
        wa = sb("wa", [P, DB, E])
        whi = [sb(f"whi_{n}", [P, ES, D], F16) for n in ("gate", "up", "down")]
        wlo = [sb(f"wlo_{n}", [P, ES, D], F16) for n in ("gate", "up", "down")]
        mags, mags_all = sb("mags", [P, THIRDS, 6]), sb("mags_all", [P, THIRDS, 6])
        lim, sc = sb("lim", [P, 2]), sb("sc", [P, 5, 4])
        fac = sb("fac", [P, THIRDS, 8])
        ubs = sb("ubs", [P, ES])
        gb = sb("gb", [P, ES])
        ub = sb("ub", [P, ES])
        b2 = sb("b2", [ES, D])
        wq1, wq1r = sb("wq1", [P, P]), sb("wq1r", [P, P])
        wk1, wk1r, wv1 = sb("wk1", [P, KV * HD]), sb("wk1r", [P, KV * HD]), sb("wv1", [P, KV * HD])
        bq1 = sb("bq1", [P, 2])
        bk1 = sb("bk1", [P, 2])
        bv1 = sb("bv1", [P, KV * HD])
        wo1 = sb("wo1", [P, P])
        bo1 = sb("bo1", [P, 1])
        rope = sb("rope", [P, 4, T])
        tern = [sb(f"tern_{n}", [P, 2048], F16) for n in ("up", "gate", "down")]
        iota_e = sb("iota_e", [P, E])
        wsum = sb("wsum", [P, 3, 2])
        wscale = sb("wscale", [P, 3])
        half = sb("half", [P, 3, 2])
        ffn_c = sb("ffn_c", [P, 4])
        x_in = sb("x_in", [P, GB, D])
        ctx_sb = sb("ctx_sb", [P, GB, D])
        kcat = sb("kcat", [P, DB, GB, 2, P])
        stats = sb("stats", [P, GB, 6])
        mv = sb("mv", [P, GB, 2])
        rstd, var, minus_half = sb("rstd", [P, GB]), sb("var", [P, GB]), sb("minus_half", [P, GB])
        xn = sb("xn", [P, GB, D])
        pr = sb("pr", [P, GB, D])
        xnT = sb("xnT", [P, DB, TOK])
        nmax = sb("nmax", [P, GB])
        rsum = sb("rsum", [P, GB])
        rinv = sb("rinv", [P, GB])
        acc = sb("acc", [P, GB, D])
        x3 = sb("x3", [P, GB, D])
        top = sb("top", [P, GB, 8])
        topi = sb("topi", [P, GB, 8], U32)
        topf = sb("topf", [P, GB, 2])
        psum2 = sb("psum2", [P, GB, 1])
        pinv = sb("pinv", [P, GB, 1])
        topw = sb("topw", [P, GB, 2])
        comb = sb("comb", [P, GB, ES])
        ksplit = sb("ksplit", [P, TERMS, T], BF16)
        KS = sb("KS", [P, GB, KV, T], BF16)
        Vs = sb("Vs", [P, GB, 2, KV, 32])
        M = sb("M", [P, GB, 2 * H])
        ps = ctx.enter_context(nc.psum_tensor("ps", [P, BANKS, 512], F32))

        def part(region, at, size, dt=F32):
            v = region[:, at:at + size]
            return v if dt == F32 else v.bitcast(dt)

        r1 = sb("r1", [P, 8192])
        g_sb = part(r1, 6144, 1024).rearrange("p (a b) -> p a b", a=2)
        y_sb = part(r1, 7168, 1024).rearrange("p (a b) -> p a b", a=2)
        s_sb = part(r1, 0, 1024).rearrange("p (a b) -> p a b", a=2)
        h_sb = part(r1, 1024, 1024).rearrange("p (a b) -> p a b", a=2)
        hhi = part(r1, 2048, 2048, F16).rearrange("p (a b) -> p a b", a=EB)
        hlo = part(r1, 4096, 2048, F16).rearrange("p (a b) -> p a b", a=EB)
        QS = part(r1, 0, 8192, BF16).rearrange("p (b h k) -> p b h k", b=GB, h=H)
        r2 = sb("r2", [P, 4096])
        v_sb = part(r2, 1024, 1024).rearrange("p (a b) -> p a b", a=GB)
        prT = part(r2, 3072, 1024).rearrange("p (a b c) -> p a b c", a=GB, b=2)
        PT = part(r2, 0, 4096).rearrange("p (n a b) -> p n a b", n=4, a=2)
        r3 = sb("r3", [P, 1024])
        combT = part(r3, 0, TOK)[0:ES, :]
        mhi, mlo = (part(r3, at, 512, BF16)[0:H, :].rearrange("p (b k) -> p b k", b=UNITS // 2) for at in (0, 512))
        xhi = part(r3, 0, 512, F16).rearrange("p (a b) -> p a b", a=DB)
        xlo = part(r3, 512, 512, F16).rearrange("p (a b) -> p a b", a=DB)
        r4 = sb("r4", [P, 2048])
        raw = part(r4, 0, 2048)
        qr = part(r4, 0, 1024).rearrange("p (r a b) -> p r a b", r=2, a=2)
        qres = part(r4, 1024, 1024).rearrange("p (a b) -> p a b", a=GB)
        U = part(r4, 1024, 1024).rearrange("p (a b) -> p a b", a=KV)
        atT = part(r4, 0, 1024).rearrange("p (a b c) -> p a b c", a=GB, b=DB)
        r5 = sb("r5", [P, 1536])
        tpos = part(r5, 0, 1024, F16)
        el, el1, prob, hot0, hot1 = (part(r5, 1024 + n * GB * E, GB * E).rearrange("p (b e) -> p b e", b=GB)
                                     for n in range(5))
        combs = part(r5, 1024 + 5 * GB * E, GB * ES).rearrange("p (b e) -> p b e", b=GB)
        qsplit = part(r5, 0, 1536, BF16).rearrange("p (b t k) -> p b t k", b=GB, t=TERMS)
        r6 = sb("r6", [P, 2048])
        kr = part(r6, 0, 768).rearrange("p (a b) -> p a b", a=3)
        kres = part(r6, 768, 256)
        num = part(r6, 0, 1024).rearrange("p (a b) -> p a b", a=GB)
        den = part(r6, 1024, 1024).rearrange("p (a b) -> p a b", a=GB)
        xn0 = part(r6, 0, 1024).rearrange("p (a b) -> p a b", a=GB)
        staged = part(r1, 0, SLOTS * CHUNK).rearrange("p (s k) -> p s k", s=SLOTS)
        exhi, exlo = (part(r2, 512 * n, 512, F16).rearrange("p (a b) -> p a b", a=DB) for n in range(2))
        yhi, ylo = (part(r2, 1024 + 512 * n, 512, F16).rearrange("p (a b) -> p a b", a=2) for n in range(2))
        qT = part(r6, 1024, 1024).rearrange("p (a b) -> p a b", a=DB)
        x_res = acc
        q_rot = y_out = x3

        qd = nc.dram_tensor("q_scratch", [GB, TERMS, P, T], BF16, kind="Internal").ap()
        kd = nc.dram_tensor("k_scratch", [TERMS, GB, HD, KV, T], BF16, kind="Internal").ap()
        ud = nc.dram_tensor("pv_scratch", [GB, HD + 1, KV, KV, T], F32, kind="Internal").ap()

        w_attn0, w_attn0v = Sem("w_attn0", 2, 16), Sem("w_attn0v", 2, 16)
        w_experts = Sem("w_experts", 4, 16)
        w_chunk = [Sem(f"w_chunk{n}", 0, 16) for n in range(SLOTS)]
        mags_done, mags_full = Sem("mags_done", 5 * THIRDS), Sem("mags_full", THIRDS)
        scale_step = Sem("scale_step", 14 * THIRDS)
        w_scaled, w_high, w_low = Sem("w_scaled", CHUNKS - 3), Sem("w_high", CHUNKS), Sem("w_low", CHUNKS)
        w_attn1 = Sem("w_attn1", 12, 16)
        raw_in = Sem("raw_in", 3, 16)
        consts = Sem("consts", 1)
        passed = Sem("passed", 0)
        zeroed = Sem("zeroed", 3)
        pads = Sem("pads", 4)
        abs_sums, abs_total = Sem("abs_sums", 3), Sem("abs_total", 3)
        quant_step, tern_done = Sem("quant_step", 12), Sem("tern_done", 3)
        ffn_consts = Sem("ffn_consts", 7)
        x_loaded, ctx_loaded = Sem("x_loaded", 1, 16), Sem("ctx_loaded", 1, 16)
        ctxT_loaded = Sem("ctxT_loaded", DB, 16)
        tiles_ready, front_ready = Sem("tiles_ready", RING.counts["full", False]), Sem("front_ready", RING.counts["full", True])
        act_emptied = Sem("act_emptied", RING.counts["act", False])
        dve_emptied = Sem("dve_emptied", RING.counts["dve", False])
        act_front, dve_front = Sem("act_front", RING.counts["act", True]), Sem("dve_front", RING.counts["dve", True])
        ln_stats = [Sem(f"ln_stats{n}", GB) for n in range(4)]
        ln_mv, ln_var, ln_rstd = ([Sem(f"{name}{n}", 1) for n in range(4)] for name in ("ln_mv", "ln_var", "ln_rstd"))
        ln_done = [Sem(f"ln_done{n}", GB) for n in range(4)]
        neg_max = Sem("neg_max", GB // 2)
        sums_inv = Sem("sums_inv", 1)
        base_sum = Sem("base_sum", 1)
        route_step = Sem("route_step", 5 + GB)
        top_step = Sem("top_step", 2 * GB)
        hots = Sem("hots", 2 * GB)
        comb_done = Sem("comb_done", 1)
        comb_scaled = Sem("comb_scaled", THIRDS)
        ex_hi, ex_lo = Sem("ex_hi", DB), Sem("ex_lo", DB)
        y_hi, y_lo = Sem("y_hi", ES), Sem("y_lo", ES)
        kr_done, kres_done = Sem("kr_done", 1), Sem("kres_done", 1)
        k_hi = Sem("k_hi", 2)
        k_split_done = Sem("k_split_done", 1)
        k_stored, k_stacked = Sem("k_stored", 1, 16), Sem("k_stacked", 6, 16)
        q_rotated, q_res_done = Sem("q_rotated", GB), Sem("q_res_done", GB)
        q_hi = Sem("q_hi", 2 * GB)
        pv_even = Sem("pv_even", UNITS // 2)
        x_hi = Sem("x_hi", DB)
        q_split_done = Sem("q_split_done", GB)
        q_cleared = Sem("q_cleared", GB)
        q_stored = [Sem(f"q_stored{j}", 1, 16) for j in range(GB)]
        q_stacked = [Sem(f"q_stacked{j}", 3, 16) for j in range(GB)]
        m_stacked = [Sem(f"m_stacked{n}", 2, 16) for n in range(UNITS // 2)]
        u_stored = Sem("u_stored", KV * GB, 16)
        nd_loaded = [Sem(f"nd_loaded{j}", 2, 16) for j in range(GB)]
        den_inv, normed = Sem("den_inv", GB), Sem("normed", GB)
        h_hi, h_lo = Sem("h_hi", EB), Sem("h_lo", EB)
        stored = Sem("stored", 1, 16)

        block = ctx.enter_context(nc.Block())

        def tile(stage, n, banks=1):
            at = RING.bank[stage, n]
            return ps[:, at, :] if banks == 1 else ps[:, at:at + banks, :].rearrange("p a b -> p (a b)")

        def full(g, stage, n):
            return g * (front_ready if stage in FRONT else tiles_ready).per + RING.full[stage, n]

        def empty(g, stage, n, part=None):
            engine, count = RING.empty[stage, n]
            return g * RING.counts[engine, stage in FRONT] + (count if part is None else count - PARTS[stage] + part)

        def before(body, phase, stage, n):
            for earlier, st, k in RING.after[phase, stage, n]:
                ahead = (st in FRONT) - earlier
                sems = (act_front, dve_front) if st in FRONT else (act_emptied, dve_emptied)
                yield sems[RING.empty[st, k][0] == "dve"].sem, empty(body + ahead if ahead else body, st, k)

        def weighted(g, u):
            if u % 2:
                return tiles_ready.sem, full(g, "pv", u // 2)
            return pv_even.sem, pv_even.at(g, u // 2 + 1)

        @block.sync
        def _(sp):
            def load_x(g):
                sp.dma_start(x_in[:], a["x"][bass.ts(g, GB)].rearrange("b s d -> s b d")).then_inc(x_loaded.sem, 16)

            def load_ctx(g):
                sp.dma_start(ctx_sb[:], a["ctx"][bass.ts(g, GB)].rearrange("b s d -> s b d")).then_inc(ctx_loaded.sem, 16)
                for eb in range(DB):
                    sp.dma_start(kcat[:, eb, :, 0, :], a["ctxT"][bass.ts(g, GB), eb].rearrange("b p k -> p b k"))\
                        .then_inc(ctxT_loaded.sem, 16)

            load_x(0)
            for dst, src in ((wq0, "wq0"), (wk0, "wk0")):
                sp.dma_start(dst[:], a[src].rearrange("(b p) e -> p b e", p=P)).then_inc(w_attn0.sem, 16)
            load_ctx(0)
            for dst, src in ((wv0, "wv0"), (wo0, "wo0")):
                sp.dma_start(dst[:], a[src].rearrange("(b p) e -> p b e", p=P)).then_inc(w_attn0v.sem, 16)
            sp.dma_start(wa[:], a["wa"].rearrange("(b p) e -> p b e", p=P)).then_inc(w_experts.sem, 16)
            for dst, src in ((gb, "gb"), (ub, "ub")):
                sp.dma_start(dst[:], a[src]).then_inc(w_experts.sem, 16)
            sp.dma_start(b2[:], a["b2"]).then_inc(w_experts.sem, 16)
            def load_chunk(c):
                third, m = divmod(c, 3)
                if c >= SLOTS:
                    sp.wait_ge(w_low.sem, w_low.at(0, c - SLOTS + 1))
                w = a[("wg", "wu", "w2")[m]][third * ET:(third + 1) * ET]
                w = w.rearrange("e f d -> f e d") if m == 2 else w.rearrange("e (b p) f -> p (e b) f", p=P)
                sp.dma_start(staged[:, c % SLOTS, :].rearrange("p (e k) -> p e k", k=w.shape[2]), w)\
                    .then_inc(w_chunk[c % SLOTS].sem, 16)

            for c in range(3):
                load_chunk(c)
            for dst, src in ((wq1, "wq1"), (wq1r, "wq1r"), (wk1, "wk1"), (wk1r, "wk1r"), (wv1, "wv1"), (bq1, "bq1"),
                             (bk1, "bk1"), (wo1, "wo1"), (bo1, "bo1"), (rope, "rope")):
                sp.dma_start(dst[:], a[src]).then_inc(w_attn1.sem, 16)
            sp.dma_start(bv1[:], a["bv1"].broadcast_to([P, KV * HD])).then_inc(w_attn1.sem, 16)
            sp.dma_start(iota_e[:], a["iota"].broadcast_to([P, E])).then_inc(w_attn1.sem, 16)
            for c in range(3, CHUNKS):
                load_chunk(c)

            def body(g, again, last=False):
                if not last:
                    sp.wait_ge(tiles_ready.sem, full(g, "v1", 0))
                    load_ctx(g + 1)
                    sp.wait_ge(dve_front.sem, empty(g, "o", GB // 2 - 1))
                    load_x(g + 1)
                sp.wait_ge(k_split_done.sem, k_split_done.at(g, 1))
                if again:
                    sp.wait_ge(k_stacked.sem, k_stacked.at(g - 1, 6))
                sp.dma_start(kd.rearrange("t b d h k -> (b d h) t k"), ksplit[:]).then_inc(k_stored.sem, 16)
                sp.wait_ge(k_stored.sem, k_stored.at(g, 1))
                if again:
                    sp.wait_ge(tiles_ready.sem, full(g - 1, "st", 2 * UNITS - 1))
                sp.wait_ge(pads.sem, pads.at(0, 4))
                for r, term in enumerate((0, 0, 0, 1, 1, 2)):
                    sp.dma_start(KS[8 * r:8 * r + 8, :, :, :].rearrange("d b h k -> d b (h k)"),
                                 kd[term].rearrange("b d h k -> d b (h k)")).then_inc(k_stacked.sem, 16)
                for j in range(GB):
                    sp.wait_ge(q_split_done.sem, q_split_done.at(g, j + 1))
                    if again:
                        sp.wait_ge(q_stacked[j].sem, q_stacked[j].at(g - 1, 3))
                    sp.dma_start(qd[j].rearrange("t p k -> p t k"), qsplit[:, j, :, :]).then_inc(q_stored[j].sem, 16)
                    sp.wait_ge(q_stored[j].sem, q_stored[j].at(g, 1))
                    if again:
                        sp.sem_inc(passed.sem, 1)
                    flat = qd[j].rearrange("t (d h) k -> (t d) (h k)", h=H)
                    sp.wait_ge(q_cleared.sem, q_cleared.at(g, j + 1))
                    for r0, rows in ((0, 3), (3, 2), (5, 1)):
                        sp.dma_start(QS[8 * r0:8 * r0 + 8 * rows, j, :, :].rearrange("r h k -> r (h k)"),
                                     flat[0:8 * rows]).then_inc(q_stacked[j].sem, 16)
                for j in range(GB):
                    sp.wait_ge(act_emptied.sem, empty(g, "pv", 2 * j + 1))
                    if again:
                        sp.wait_ge(nd_loaded[j].sem, nd_loaded[j].at(g - 1, 2))
                    for q in range(KV):
                        sp.dma_start(ud[j, :, q, :, :].rearrange("r h k -> r (h k)"),
                                     U[32 * q:32 * q + HD + 1, :, :].rearrange("r h k -> r (h k)"))\
                            .then_inc(u_stored.sem, 16)
                    sp.wait_ge(u_stored.sem, u_stored.at(g, KV * (j + 1)))
                    if again:
                        sp.sem_inc(passed.sem, 1)
                    if not last:
                        sp.wait_ge(front_ready.sem, full(g + 1, "s", GB // 2 - 1))
                    else:
                        sp.wait_ge(tiles_ready.sem, full(g - 1, "o1", j // 2))
                    sp.dma_start(num[:, j, :], ud[j, 0:HD].rearrange("r q h k -> (r q h) k"))\
                        .then_inc(nd_loaded[j].sem, 16)
                    sp.dma_start(den[:, j, :], ud[j, HD].rearrange("(o q) h k -> o (q h) k", o=1)
                                 .broadcast_to([HD, H, T])).then_inc(nd_loaded[j].sem, 16)
                sp.wait_ge(dve_emptied.sem, empty(g, "down4", GB // 2 - 1))
                sp.dma_start(a["out"][bass.ts(g, GB)].rearrange("b s d -> s b d"), y_out[:]).then_inc(stored.sem, 16)

            body(0, False)
            with sp.Fori(1, NG - 1) as g:
                body(g, True)
            body(NG - 1, True, last=True)
            sp.wait_ge(stored.sem, stored.at(NG - 1, 1))

        @block.gpsimd
        def _(pool):
            pool.memset(ident[:], 0.0).then_inc(zeroed.sem, 1)
            pool.wait_ge(zeroed.sem, zeroed.at(0, 1))
            pool.affine_select(out=ident[:], in_=ident[:], compare_op=ALU.not_equal, fill=1.0, base=0,
                               pattern=[[-1, P]], channel_multiplier=1).then_inc(consts.sem, 1)
            pool.memset(KS[:], 1.0).then_inc(pads.sem, 1)
            pool.memset(Vs[:], 0.0).then_inc(zeroed.sem, 1)
            pool.wait_ge(zeroed.sem, zeroed.at(0, 2))
            pool.memset(Vs[:, :, :, :, HD:HD + 1], 1.0).then_inc(pads.sem, 1)
            pool.memset(comb[:, :, E:ES], 1.0).then_inc(pads.sem, 1)
            pool.memset(minus_half[:], -0.5).then_inc(pads.sem, 1)
            pool.memset(mags[:], 0.0).then_inc(zeroed.sem, 1)
            pool.wait_ge(pads.sem, pads.at(0, 4))

            def all_magnitudes(third):
                pool.wait_ge(mags_done.sem, mags_done.at(0, 5 * (third + 1)))
                pool.partition_all_reduce(mags_all[:, third, :], mags[:, third, :], P, bass.bass_isa.ReduceOp.max)\
                    .then_inc(mags_full.sem, 1)

            def weights_low(c):
                third, m = divmod(c, 3)
                pool.wait_ge(w_high.sem, w_high.at(0, c + 1))
                experts = slice(third * ET, (third + 1) * ET)
                pool.tensor_tensor(wlo[m][:, experts, :].rearrange("p e k -> p (e k)"), staged[:, c % SLOTS, :],
                                   whi[m][:, experts, :].rearrange("p e k -> p (e k)"), ALU.subtract)\
                    .then_inc(w_low.sem, 1)

            def quantise_sum(n):
                if n:
                    pool.wait_ge(tern_done.sem, tern_done.at(0, n))
                    pool.dma_start(raw, a[("wup", "wgate", "wdown")[n]]).then_inc(raw_in.sem, 16)
                pool.wait_ge(abs_sums.sem, abs_sums.at(0, n + 1))
                pool.partition_all_reduce(wsum[:, n, 1:2], wsum[:, n, 0:1], P, bass.bass_isa.ReduceOp.add)\
                    .then_inc(abs_total.sem, 1)

            def rsqrt(g, again, n):
                pool.wait_ge(ln_mv[n].sem, ln_mv[n].at(g, 1))
                if again:
                    pool.sem_inc(passed.sem, 1)
                pool.tensor_scalar(var[:], mv[:, :, 1], LN_EPS, None, ALU.add).then_inc(ln_var[n].sem, 1)
                pool.wait_ge(ln_var[n].sem, ln_var[n].at(g, 1))
                pool.tensor_tensor(rstd[:], var[:], minus_half[:], ALU.pow).then_inc(ln_rstd[n].sem, 1)

            def body(g, again, last=False):
                def clear(j):
                    pool.memset(QS[:, j, :, :], 0.0).then_inc(q_cleared.sem, 1)

                if not again:
                    pool.dma_start(raw, a["wup"]).then_inc(raw_in.sem, 16)
                    for third in range(1, THIRDS):
                        all_magnitudes(third)
                        for c in range(3 * third, 3 * third + 3):
                            weights_low(c)
                    pool.wait_ge(w_low.sem, w_low.at(0, CHUNKS))
                    quantise_sum(0)
                    for j in range(GB - 1):
                        clear(j)
                    quantise_sum(1)
                if again:
                    pool.wait_ge(tiles_ready.sem, full(g - 1, "down4", GB // 2 - 1))
                    pool.sem_inc(passed.sem, 1)
                    for j in range(GB - 1):
                        clear(j)
                if not last:
                    rsqrt(g + 1, again, 0)
                if not again:
                    quantise_sum(2)
                pool.wait_ge(tiles_ready.sem, full(g, "down", 2 * ES - 1))
                if again:
                    pool.sem_inc(passed.sem, 1)
                clear(GB - 1)
                rsqrt(g, again, 2)
                for j in range(GPSIMD_FROM, GB):
                    pool.wait_ge(dve_emptied.sem, empty(g, "q1", j))
                    pool.tensor_tensor(q_rot[:, j, :], qr[:, 0, j % 2, :], qr[:, 1, j % 2, :], ALU.add)\
                        .then_inc(q_rotated.sem, 1)
                    pool.wait_ge(q_hi.sem, q_hi.at(g, 2 * j + 1))
                    pool.tensor_tensor(qres[:, j, :], q_rot[:, j, :], qsplit[:, j, 0, :], ALU.subtract)\
                        .then_inc(q_res_done.sem, 1)
                    pool.wait_ge(q_hi.sem, q_hi.at(g, 2 * j + 2))
                    pool.tensor_tensor(qsplit[:, j, 2, :], qres[:, j, :], qsplit[:, j, 1, :], ALU.subtract)\
                        .then_inc(q_split_done.sem, 1)
                rsqrt(g, again, 3)
                for e in range(EB):
                    pool.wait_ge(h_hi.sem, h_hi.at(g, e + 1))
                    if e == 0:
                        if again:
                            pool.wait_ge(tiles_ready.sem, full(g - 1, "down4", GB // 2 - 1))
                    pool.tensor_tensor(hlo[:, e, :], h_sb[:, e % 2, :], hhi[:, e, :], ALU.subtract)\
                        .then_inc(h_lo.sem, 1)
                    if e == LN_NEXT_AT and not last:
                        rsqrt(g + 1, again, 1)

            rsqrt(0, False, 0)
            all_magnitudes(0)
            rsqrt(0, False, 1)
            body(0, False)
            with pool.Fori(1, NG - 1) as g:
                body(g, True)
            body(NG - 1, True, last=True)

        @block.scalar
        def _(act):
            def turned_rows_and_queries(g):
                for d in range(DB):
                    act.wait_ge(front_ready.sem, full(g, "xt", d))
                    act.activation(xnT[:, d, :], tile("xt", d), ACT.Copy).then_inc(act_front.sem, 1)
                for e in range(DB):
                    act.wait_ge(front_ready.sem, full(g, "q", e))
                    act.activation(qT[:, e, :], tile("q", e), ACT.Copy, scale=1.0 / 16.0)\
                        .then_inc(act_front.sem, 1)

            def exponentials(g):
                for j in range(GB):
                    act.wait_ge(neg_max.sem, neg_max.at(g, j // 2 + 1))
                    t = tile("s", j // 2)[:, (j % 2) * D:(j % 2 + 1) * D]
                    act.activation(pr[:, j, :], t, ACT.Exp, bias=nmax[:, j:j + 1], accum_out=rsum[:, j:j + 1])\
                        .then_inc(act_front.sem, 1)

            def attended(g):
                for n in range(GB // 2):
                    act.wait_ge(front_ready.sem, full(g, "at", n))
                    act.activation(atT[:, 2 * n:2 * n + 2, :, :].rearrange("p a b c -> p (a b c)"), tile("at", n),
                                   ACT.Copy).then_inc(act_front.sem, 1)

            def body(g, again, last=False):
                for d in range(DB):
                    act.wait_ge(tiles_ready.sem, full(g, "xt2", d))
                    act.activation(xnT[:, d, :], tile("xt2", d), ACT.Copy).then_inc(act_emptied.sem, 1)
                for d in range(DB):
                    act.wait_ge(act_emptied.sem, empty(g, "xt2", d))
                    act.activation(exhi[:, d, :], xnT[:, d, :], ACT.Copy, scale=X_SCALE).then_inc(ex_hi.sem, 1)
                for n in range(2):
                    rotated = kres_done if n else kr_done
                    act.wait_ge(rotated.sem, rotated.at(g, 1))
                    if n == 0:
                        if again:
                            act.wait_ge(k_stored.sem, k_stored.at(g - 1, 1))
                    act.activation(ksplit[:, n, :], kr[:, 2, :] if n == 0 else kres, ACT.Copy)\
                        .then_inc(k_hi.sem, 1)
                act.wait_ge(tiles_ready.sem, full(g, "route", 0))
                act.activation(el, tile("route", 0)[:, 0:GB * E].rearrange("p (b e) -> p b e", b=GB), ACT.Exp,
                               scale=-1.0).then_inc(act_emptied.sem, 1)

                def gelu(e):
                    act.wait_ge(tiles_ready.sem, full(g, "gate", e))
                    if e == 0 and not again:
                        act.wait_ge(w_experts.sem, w_experts.at(0, 4))
                    if e % ET == 0 and not again:
                        act.wait_ge(scale_step.sem, scale_step.at(0, 14 * (e // ET + 1)))
                    if e >= 2:
                        act.wait_ge(dve_emptied.sem, empty(g, "up", e - 2))
                    else:
                        if again:
                            act.wait_ge(dve_emptied.sem, empty(g - 1, "up", ES - 2 + e))
                    act.activation(g_sb[:, e % 2, :], tile("gate", e), ACT.Gelu, bias=gb[:, e:e + 1],
                                   scale=fac[:, e // ET, 2:3]).then_inc(act_emptied.sem, 1)

                def hidden_high(e):
                    act.wait_ge(dve_emptied.sem, empty(g, "up", e))
                    if e >= 2 or again:
                        act.wait_ge(tiles_ready.sem, full(g if e >= 2 else g - 1, "down", 2 * ((e - 2) % ES) + 1))
                    act.activation(yhi[:, e % 2, :], y_sb[:, e % 2, :], ACT.Copy, scale=fac[:, e // ET, 4:5])\
                        .then_inc(y_hi.sem, 1)

                gelu(0)
                gelu(1)
                act.wait_ge(tiles_ready.sem, full(g, "ct", 0))
                act.activation(combT, tile("ct", 0)[0:ES, :], ACT.Copy).then_inc(act_emptied.sem, 1)
                hidden_high(0)
                hidden_high(1)
                for e in range(2, ES):
                    gelu(e)
                    hidden_high(e)
                    for c in range(3, CHUNKS):
                        if HIGH_AT[c] == e - 2 and not again:
                            weights_high(c)
                    if not again and e - 2 in ABS_AT:
                        n = ABS_AT.index(e - 2)
                        act.wait_ge(raw_in.sem, raw_in.at(0, n + 1))
                        act.activation(tern[n][:], raw, ACT.Abs, accum_out=wsum[:, n, 0:1]).then_inc(abs_sums.sem, 1)
                if not last:
                    turned_rows_and_queries(g + 1)
                for j in range(GB):
                    act.wait_ge(q_rotated.sem, q_rotated.at(g, j + 1))
                    if again:
                        act.wait_ge(q_stored[j].sem, q_stored[j].at(g - 1, 1))
                    for k in range(2):
                        if k:
                            act.wait_ge(q_res_done.sem, q_res_done.at(g, j + 1))
                        act.activation(qsplit[:, j, k, :], (q_rot if k == 0 else qres)[:, j, :], ACT.Copy)\
                            .then_inc(q_hi.sem, 1)
                for s in range(STEPS):
                    if s == SCORES_AT and not last:
                        exponentials(g + 1)
                    u = s - LAG
                    if 0 <= u < UNITS:
                        for kb in range(2):
                            act.wait_ge(tiles_ready.sem, full(g, "st", 2 * u + kb))
                            if u >= 2 or again:
                                used, count = weighted(g if u >= 2 else g - 1, (u - 2) % UNITS)
                                act.wait_ge(used, count)
                            act.activation(PT[:, 2 * (u % 2) + kb, :, :].rearrange("p a b -> p (a b)"),
                                           tile("st", 2 * u + kb, 2), ACT.Exp, scale=float(HD) ** -0.5)\
                                .then_inc(act_emptied.sem, 1)
                    if s % 2 == 0 and 0 <= s // 2 - 1 < UNITS // 2:
                        n = s // 2 - 1
                        j, heads = n // 2, slice(H // 2 * (n % 2), H // 2 * (n % 2) + H // 2)
                        for r, part in enumerate((mhi, mlo)):
                            act.wait_ge(dve_emptied.sem, empty(g, "mt", n, r + 1))
                            act.dma_start(QS[MROW + r:MROW + r + 1, j, heads, :].rearrange("r h k -> r (h k)"),
                                          part[:, n, :]).then_inc(m_stacked[n].sem, 16)
                    u = s - LAG - 1
                    if u >= 0 and u % 2 == 1:
                        act.wait_ge(tiles_ready.sem, full(g, "pv", u // 2))
                        j = u // KV
                        if u % KV == 1:
                            if j or again:
                                act.wait_ge(u_stored.sem, u_stored.at(g, KV * j))
                            if j == 0:
                                act.wait_ge(q_split_done.sem, q_split_done.at(g, GB))
                        act.activation(U[:, u % KV - 1:u % KV + 1, :].rearrange("p h k -> p (h k)"),
                                       tile("pv", u // 2), ACT.Copy).then_inc(act_emptied.sem, 1)
                if not last:
                    attended(g + 1)
                for d in range(DB):
                    act.wait_ge(tiles_ready.sem, full(g, "xt4", d))
                    act.activation(xhi[:, d, :], tile("xt4", d), ACT.Copy).then_inc(x_hi.sem, 1)
                if not again:
                    act.wait_ge(ffn_consts.sem, ffn_consts.at(0, 7))
                for e in range(EB):
                    act.wait_ge(tiles_ready.sem, full(g, "up4", e))
                    if e >= 2 or again:
                        act.wait_ge(dve_emptied.sem, empty(g if e >= 2 else g - 1, "gate4", (e - 2) % EB))
                    act.activation(s_sb[:, e % 2, :], tile("up4", e), ACT.Silu, scale=ffn_c[:, 0:1])\
                        .then_inc(act_emptied.sem, 1)
                    if e:
                        hidden_hi(g, again, e - 1)
                hidden_hi(g, again, EB - 1)

            def hidden_hi(g, again, e):
                act.wait_ge(dve_emptied.sem, empty(g, "gate4", e))
                if e == 0:
                    if again:
                        act.wait_ge(tiles_ready.sem, full(g - 1, "down4", GB // 2 - 1))
                act.activation(hhi[:, e, :], h_sb[:, e % 2, :], ACT.Copy).then_inc(h_hi.sem, 1)

            def weights_high(c):
                third, m = divmod(c, 3)
                act.wait_ge(scale_step.sem, scale_step.at(0, 14 * (third + 1)))
                raw_w, scale = staged[:, c % SLOTS, :], sc[:, 4, m:m + 1]
                if third:
                    act.activation(raw_w, raw_w, ACT.Copy, scale=scale).then_inc(w_scaled.sem, 1)
                    act.wait_ge(w_scaled.sem, w_scaled.at(0, c - 2))
                    scale = 1.0
                act.activation(whi[m][:, third * ET:(third + 1) * ET, :].rearrange("p e k -> p (e k)"), raw_w,
                               ACT.Copy, scale=scale).then_inc(w_high.sem, 1)

            turned_rows_and_queries(0)
            exponentials(0)
            attended(0)
            for c in range(3):
                weights_high(c)
            body(0, False)
            with act.Fori(1, NG - 1) as g:
                body(g, True)
            body(NG - 1, True, last=True)

        @block.tensor
        def _(pe):
            def done(i):
                i.then_inc(tiles_ready.sem, 1)

            def mm(out, lhsT, rhs, first=True, last=True):
                return pe.matmul(out, lhsT, rhs, start=first, stop=last)

            def transposes(body, phase, stage, g, ln, rows):
                for d in range(DB):
                    for held, count in before(body, phase, stage, d):
                        pe.wait_ge(held, count)
                    for j in range(GB):
                        if d == 0:
                            pe.wait_ge(ln_done[ln].sem, ln_done[ln].at(g, j + 1))
                        i = pe.transpose(tile(stage, d)[:, j * P:(j + 1) * P], rows[:, j, d * P:(d + 1) * P], ident[:])
                    (front_done if stage in FRONT else done)(i)

            def front_done(i):
                i.then_inc(front_ready.sem, 1)

            def project(body, phase, g, stage, w):
                for e in range(DB):
                    for held, count in before(body, phase, stage, e):
                        pe.wait_ge(held, count)
                    if stage == "q" and e == 0:
                        pe.wait_ge(act_front.sem, empty(g, "xt", DB - 1))
                    for d in range(DB):
                        i = mm(tile(stage, e), w[:, d, e * P:(e + 1) * P], xnT[:, d, :], d == 0, d == DB - 1)
                    front_done(i)

            def scores(body, phase, g):
                for n in range(GB // 2):
                    for held, count in before(body, phase, "s", n):
                        pe.wait_ge(held, count)
                    if n == 0:
                        pe.wait_ge(act_front.sem, empty(g, "q", DB - 1))
                        pe.wait_ge(dve_front.sem, empty(g, "k", DB - 1))
                        pe.wait_ge(ctxT_loaded.sem, ctxT_loaded.at(g, DB))
                    for j in (2 * n, 2 * n + 1):
                        for e in range(DB):
                            i = mm(tile("s", n)[:, (j % 2) * D:(j % 2 + 1) * D], qT[:, e, j * P:(j + 1) * P],
                                   kcat[:, e, j, :, :].rearrange("p a b -> p (a b)"), e == 0, e == DB - 1)
                    front_done(i)

            def values_and_attended(body, phase, g):
                for n in range(GB // 2):
                    for held, count in before(body, phase, "v", n):
                        pe.wait_ge(held, count)
                    for j in (2 * n, 2 * n + 1):
                        for d in range(DB):
                            i = mm(tile("v", n)[:, (j % 2) * D:(j % 2 + 1) * D], xnT[:, d, j * P:(j + 1) * P],
                                   wv0[:, d, :], d == 0, d == DB - 1)
                    front_done(i)
                for n in range(GB // 2):
                    for held, count in before(body, phase, "pt", n):
                        pe.wait_ge(held, count)
                    for j in (2 * n, 2 * n + 1):
                        pe.wait_ge(act_front.sem, empty(g, "s", n, j % 2 + 1))
                        for kb in range(2):
                            i = pe.transpose(tile("pt", n)[:, (j % 2) * D + kb * P:(j % 2) * D + (kb + 1) * P],
                                             pr[:, j, kb * P:(kb + 1) * P], ident[:])
                    front_done(i)
                pe.wait_ge(ctx_loaded.sem, ctx_loaded.at(g, 1))
                for n in range(GB // 2):
                    for held, count in before(body, phase, "at", n):
                        pe.wait_ge(held, count)
                    pe.wait_ge(dve_front.sem, empty(g, "pt", n))
                    for j in (2 * n, 2 * n + 1):
                        for d in range(DB):
                            for kb, v in enumerate((ctx_sb, v_sb)):
                                i = mm(tile("at", n)[:, (j % 2) * D + d * P:(j % 2) * D + (d + 1) * P],
                                       v[:, j, d * P:(d + 1) * P], prT[:, j, kb, :], kb == 0, kb == 1)
                    front_done(i)

            def output(body, phase, g):
                for n in range(GB // 2):
                    for held, count in before(body, phase, "o", n):
                        pe.wait_ge(held, count)
                    pe.wait_ge(act_front.sem, empty(g, "at", n))
                    for j in (2 * n, 2 * n + 1):
                        for d in range(DB):
                            i = mm(tile("o", n)[:, (j % 2) * D:(j % 2 + 1) * D], atT[:, j, d, :], wo0[:, d, :],
                                   d == 0, d == DB - 1)
                    front_done(i)

            def body(g, phase):
                again, last = phase in ("again", "last"), phase == "last"
                transposes(g, phase, "xt2", g, 1, xn)
                for held, count in before(g, phase, "k1", 0):
                    pe.wait_ge(held, count)
                if not again:
                    pe.wait_ge(w_attn1.sem, w_attn1.at(0, 12))
                for r, w in enumerate((wk1, wk1r)):
                    for j in range(GB):
                        i = mm(tile("k1", 0)[32 * j:32 * j + 32, r * T:(r + 1) * T], w[:], ctx_sb[:, j, :])
                done(i)
                for held, count in before(g, phase, "v1", 0):
                    pe.wait_ge(held, count)
                for j in range(GB):
                    for kb in range(2):
                        n = 2 * j + kb
                        i = mm(tile("v1", 0)[:, 32 * n:32 * n + 32], ctx_sb[:, j, kb * P:(kb + 1) * P], wv1[:])
                done(i)
                for held, count in before(g, phase, "route", 0):
                    pe.wait_ge(held, count)
                pe.wait_ge(act_emptied.sem, empty(g, "xt2", DB - 1))
                if not again:
                    pe.wait_ge(w_experts.sem, w_experts.at(0, 4))
                for j in range(GB):
                    for d in range(DB):
                        i = mm(tile("route", 0)[:, j * E:(j + 1) * E], xnT[:, d, j * P:(j + 1) * P], wa[:, d, :],
                               d == 0, d == DB - 1)
                done(i)

                def up(e):
                    if e % ET == 0 and not again:
                        pe.wait_ge(w_low.sem, w_low.at(0, 3 * (e // ET + 1)))
                    for m, stage in enumerate(("gate", "up")):
                        for held, count in before(g, phase, stage, e):
                            pe.wait_ge(held, count)
                        for n, (w, rows) in enumerate(((whi, exhi), (wlo, exhi), (whi, exlo))):
                            if e == 0 and m == 0 and n == 0:
                                pe.wait_ge(ex_hi.sem, ex_hi.at(g, DB))
                            if e == 0 and m == 0 and n == 2:
                                pe.wait_ge(ex_lo.sem, ex_lo.at(g, DB))
                            for d in range(DB):
                                i = mm(tile(stage, e), w[m][:, e, d * F:(d + 1) * F], rows[:, d, :],
                                       n == 0 and d == 0, n == 2 and d == DB - 1)
                        done(i)

                up(0)
                up(1)
                for held, count in before(g, phase, "ct", 0):
                    pe.wait_ge(held, count)
                pe.wait_ge(comb_done.sem, comb_done.at(g, 1))
                for j in range(GB):
                    i = pe.transpose(tile("ct", 0)[0:ES, j * P:(j + 1) * P], comb[:, j, :], ident[:])
                done(i)
                for n in range(GB // 2):
                    for held, count in before(g, phase, "bias2", n):
                        pe.wait_ge(held, count)
                    pe.wait_ge(act_emptied.sem, empty(g, "ct", 0))
                    for j in (2 * n, 2 * n + 1):
                        i = mm(tile("bias2", n)[:, (j % 2) * D:(j % 2 + 1) * D], combT[:, j * P:(j + 1) * P], b2[:])
                    done(i)
                for e in range(ES):
                    if e == ES - 1 and not last:
                        transposes(g, phase, "xt", g + 1, 0, xn0)
                    pe.wait_ge(y_lo.sem, y_lo.at(g, e + 1))
                    for n in range(GB // 2):
                        for held, count in before(g, phase, "down", 2 * e + n):
                            pe.wait_ge(held, count)
                        for j in (2 * n, 2 * n + 1):
                            for k, (rows, w) in enumerate(((yhi, whi), (yhi, wlo), (ylo, whi))):
                                i = mm(tile("down", 2 * e + n)[:, (j % 2) * D:(j % 2 + 1) * D],
                                       rows[:, e % 2, j * P:(j + 1) * P], w[2][:, e, :], k == 0, k == 2)
                        done(i)
                    if e + 2 < ES:
                        up(e + 2)
                if not last:
                    project(g, phase, g + 1, "q", wq0)
                for j in range(GB):
                    for held, count in before(g, phase, "q1", j):
                        pe.wait_ge(held, count)
                    pe.wait_ge(ln_done[2].sem, ln_done[2].at(g, j + 1))
                    for r, w in enumerate((wq1, wq1r)):
                        i = mm(tile("q1", j)[:, r * T:(r + 1) * T], w[:], xn[:, j, :])
                    done(i)
                if not last:
                    project(g, phase, g + 1, "k", wk0)
                def turned_maxima(n):
                    for held, count in before(g, phase, "mt", n):
                        pe.wait_ge(held, count)
                    pe.wait_ge(dve_emptied.sem, empty(g, "smax", SMAX_TILES * (2 * n + 2) - 1))
                    done(pe.transpose(tile("mt", n)[0:H, 0:P], M[:, n // 2, H * (n % 2):H * (n % 2) + H], ident[:]))

                for s in range(STEPS):
                    if s < UNITS:
                        j, kv = divmod(s, KV)
                        if kv == 0:
                            pe.wait_ge(q_stacked[j].sem, q_stacked[j].at(g, 3))
                            if j == 0:
                                pe.wait_ge(k_stacked.sem, k_stacked.at(g, 6))
                                if not again:
                                    pe.wait_ge(pads.sem, pads.at(0, 4))
                    for n in range(SMAX_TILES):
                        if n == MT_AT and s % 2 == 0 and 0 <= s // 2 - 1 < UNITS // 2:
                            turned_maxima(s // 2 - 1)
                        if s < UNITS:
                            t = SMAX_TILES * s + n
                            for held, count in before(g, phase, "smax", t):
                                pe.wait_ge(held, count)
                            for b in range(2 * SMAX_BANKS):
                                hh, qb = divmod(b, 2)
                                i = mm(tile("smax", t, SMAX_BANKS)[:, b * T:(b + 1) * T],
                                       QS[:, j, KV * kv + SMAX_BANKS * n + hh, qb * P:(qb + 1) * P], KS[:, j, kv, :])
                            done(i)
                    if s == SCORES_AT and not last:
                        scores(g, phase, g + 1)
                    u = s - LAG
                    if 0 <= u < UNITS:
                        j, kv = divmod(u, KV)
                        if u % 2 == 0:
                            pe.wait_ge(m_stacked[u // 2].sem, m_stacked[u // 2].at(g, 2))
                        for kb in range(2):
                            for held, count in before(g, phase, "st", 2 * u + kb):
                                pe.wait_ge(held, count)
                            for half in range(2):
                                i = mm(tile("st", 2 * u + kb, 2)[:, half * 512:(half + 1) * 512],
                                       KS[:, j, kv, kb * P:(kb + 1) * P],
                                       QS[:, j, KV * kv + 2 * half:KV * kv + 2 * half + 2, :]
                                       .rearrange("p a b -> p (a b)"))
                            done(i)
                    u = s - LAG - 1
                    if 0 <= u < UNITS:
                        j, kv = divmod(u, KV)
                        if u % 2 == 0:
                            for held, count in before(g, phase, "pv", u // 2):
                                pe.wait_ge(held, count)
                        pe.wait_ge(act_emptied.sem, empty(g, "st", 2 * u + 1))
                        if u == 0:
                            pe.wait_ge(dve_emptied.sem, empty(g, "v1", 0))
                        for kb in range(2):
                            for hh in range(KV):
                                i = mm(tile("pv", u // 2)[32 * hh:32 * hh + 32, (u % 2) * T:(u % 2 + 1) * T],
                                       Vs[:, j, kb, kv, :], PT[:, 2 * (u % 2) + kb, hh // 2, (hh % 2) * T:(hh % 2 + 1) * T],
                                       kb == 0, kb == 1)
                        if u % 2:
                            done(i)
                        else:
                            i.then_inc(pv_even.sem, 1)
                if not last:
                    values_and_attended(g, phase, g + 1)
                for n in range(GB // 2):
                    for held, count in before(g, phase, "o1", n):
                        pe.wait_ge(held, count)
                    for j in (2 * n, 2 * n + 1):
                        pe.wait_ge(normed.sem, normed.at(g, j + 1))
                        i = mm(tile("o1", n)[:, (j % 2) * T:(j % 2 + 1) * T], wo1[:], num[:, j, :])
                    done(i)
                if not last:
                    output(g, phase, g + 1)
                transposes(g, phase, "xt4", g, 3, xn)
                for e in range(EB):
                    for k, stage in enumerate(("up4", "gate4")):
                        for held, count in before(g, phase, stage, e):
                            pe.wait_ge(held, count)
                        if e == 0 and k == 0:
                            pe.wait_ge(dve_emptied.sem, empty(g, "xt4", DB - 1))
                            if not again:
                                pe.wait_ge(ffn_consts.sem, ffn_consts.at(0, 7))
                        n = 0
                        for part in (xhi, xlo):
                            for d in range(DB):
                                i = mm(tile(stage, e), tern[k][:, d * DE + e * P:d * DE + (e + 1) * P], part[:, d, :],
                                       n == 0, n == 3)
                                n += 1
                        done(i)
                for n in range(GB // 2):
                    for held, count in before(g, phase, "down4", n):
                        pe.wait_ge(held, count)
                    for j in (2 * n, 2 * n + 1):
                        k = 0
                        for part, sem in ((hhi, h_hi), (hlo, h_lo)):
                            for e in range(EB):
                                if n == 0 and j == 0:
                                    pe.wait_ge(sem.sem, sem.at(g, e + 1))
                                i = mm(tile("down4", n)[:, (j % 2) * D:(j % 2 + 1) * D], part[:, e, j * P:(j + 1) * P],
                                       tern[2][:, e * D:(e + 1) * D], k == 0, k == 2 * EB - 1)
                                k += 1
                    done(i)

            pe.wait_ge(consts.sem, consts.at(0, 1))
            transposes(-1, "front", "xt", 0, 0, xn0)
            pe.wait_ge(w_attn0.sem, w_attn0.at(0, 2))
            project(-1, "front", 0, "q", wq0)
            project(-1, "front", 0, "k", wk0)
            scores(-1, "front", 0)
            pe.wait_ge(w_attn0v.sem, w_attn0v.at(0, 2))
            values_and_attended(-1, "front", 0)
            output(-1, "front", 0)
            body(0, "first")
            with pe.Fori(1, NG - 1) as g:
                body(g, "again")
            body(NG - 1, "last")

        @block.vector
        def _(dve):
            def statistics(g, n, src, j):
                dve.bn_stats(stats[:, j, :], src[:, j, :]).then_inc(ln_stats[n].sem, 1)

            def mean_and_variance(g, again, n):
                for j in range(GB):
                    dve.wait_ge(ln_stats[n].sem, ln_stats[n].at(g, j + 1))
                    if again:
                        dve.sem_inc(passed.sem, 1)
                    i = dve.bn_aggr(mv[:, j, :], stats[:, j, :])
                i.then_inc(ln_mv[n].sem, 1)

            def normalise(g, n, src, dst, j):
                if j == 0:
                    dve.wait_ge(ln_rstd[n].sem, ln_rstd[n].at(g, 1))
                    dve.wait_ge(ln_mv[n].sem, ln_mv[n].at(g, 1))
                dve.tensor_scalar(dst[:, j, :], src[:, j, :], mv[:, j, 0:1], rstd[:, j:j + 1], ALU.subtract,
                                  ALU.mult).then_inc(ln_done[n].sem, 1)

            def layernorm(g, again, n, src, dst):
                for j in range(GB):
                    statistics(g, n, src, j)
                mean_and_variance(g, again, n)
                for j in range(GB):
                    normalise(g, n, src, dst, j)

            def magnitude(c):
                third, m = divmod(c, 3)
                if c == 0:
                    dve.wait_ge(zeroed.sem, zeroed.at(0, 3))
                    dve.wait_ge(w_experts.sem, w_experts.at(0, 4))
                dve.wait_ge(w_chunk[c % SLOTS].sem, 16 * (c // SLOTS + 1))
                dve.tensor_reduce(mags[:, third, m:m + 1], staged[:, c % SLOTS, :], AX.X, ALU.max,
                                  apply_absolute_value=True).then_inc(mags_done.sem, 1)
                if m == 2:
                    for n, bias in enumerate((gb, ub)):
                        dve.tensor_reduce(mags[:, third, 4 + n:5 + n], bias[:, third * ET:(third + 1) * ET], AX.X,
                                          ALU.max, apply_absolute_value=True).then_inc(mags_done.sem, 1)

            def scales(third):
                steps = [14 * third]

                def step(i):
                    steps[0] += 1
                    i.then_inc(scale_step.sem, 1)
                    dve.wait_ge(scale_step.sem, scale_step.at(0, steps[0]))

                m, f = mags_all[:, third, :], fac[:, third, :]
                dve.wait_ge(mags_full.sem, mags_full.at(0, third + 1))
                step(dve.scalar_tensor_tensor(out=lim[:], in0=m[:, 0:2], scalar=float(D), in1=m[:, 4:6], op0=ALU.mult,
                                              op1=ALU.add))
                step(dve.tensor_tensor(m[:, 3:4], lim[:, 0:1], lim[:, 1:2], ALU.mult))
                step(dve.tensor_scalar(m[:, 0:4], m[:, 0:4], TINY, None, ALU.max))
                step(dve.reciprocal(sc[:, 0, :], m[:, 0:4]))
                step(dve.tensor_scalar(sc[:, 1, :], sc[:, 0, :], float(2 ** 23 + 1), None, ALU.mult))
                step(dve.tensor_tensor(sc[:, 2, :], sc[:, 1, :], sc[:, 0, :], ALU.subtract))
                step(dve.tensor_tensor(sc[:, 3, :], sc[:, 1, :], sc[:, 2, :], ALU.subtract))
                if third:
                    dve.wait_ge(w_high.sem, w_high.at(0, 3 * third))
                    dve.wait_ge(w_low.sem, w_low.at(0, 3 * third))
                step(dve.tensor_scalar(sc[:, 4, :], sc[:, 3, :], SPLIT_TOP, None, ALU.mult))
                step(dve.tensor_scalar(f[:, 0:2], sc[:, 4, 0:2], X_SCALE, None, ALU.mult))
                step(dve.reciprocal(f[:, 2:4], f[:, 0:2]))
                step(dve.tensor_tensor(f[:, 4:5], sc[:, 4, 3:4], f[:, 3:4], ALU.mult))
                step(dve.tensor_tensor(f[:, 5:6], sc[:, 4, 3:4], sc[:, 4, 2:3], ALU.mult))
                step(dve.reciprocal(f[:, 6:7], f[:, 5:6]))
                step(dve.tensor_scalar(ubs[:, third * ET:(third + 1) * ET], ub[:, third * ET:(third + 1) * ET],
                                       f[:, 1:2], None, ALU.mult))

            def weights_low(c):
                third, m = divmod(c, 3)
                dve.wait_ge(w_high.sem, w_high.at(0, c + 1))
                experts = slice(third * ET, (third + 1) * ET)
                dve.scalar_tensor_tensor(out=wlo[m][:, experts, :].rearrange("p e k -> p (e k)"),
                                         in0=staged[:, c % SLOTS, :], scalar=sc[:, 4, m:m + 1],
                                         in1=whi[m][:, experts, :].rearrange("p e k -> p (e k)"), op0=ALU.mult,
                                         op1=ALU.subtract).then_inc(w_low.sem, 1)

            def quantise(n):
                steps = [4 * n]

                def step(i):
                    steps[0] += 1
                    i.then_inc(quant_step.sem, 1)
                    dve.wait_ge(quant_step.sem, quant_step.at(0, steps[0]))

                dve.wait_ge(abs_total.sem, abs_total.at(0, n + 1))
                step(dve.tensor_scalar(wscale[:, n:n + 1], wsum[:, n, 1:2], 1.0 / (D * DE), QUANT_EPS, ALU.mult, ALU.add))
                step(dve.tensor_scalar(half[:, n, 0:1], wscale[:, n:n + 1], 0.5, None, ALU.mult))
                step(dve.tensor_scalar(half[:, n, 1:2], wscale[:, n:n + 1], -0.5, None, ALU.mult))
                step(dve.tensor_scalar(tpos, raw, half[:, n, 0:1], None, ALU.is_gt))
                dve.scalar_tensor_tensor(out=tern[n][:], in0=raw, scalar=half[:, n, 1:2], in1=tpos, op0=ALU.is_lt,
                                         op1=ALU.subtract).then_inc(tern_done.sem, 1)

            def ffn_scales():
                def step(n, i):
                    i.then_inc(ffn_consts.sem, 1)
                    dve.wait_ge(ffn_consts.sem, ffn_consts.at(0, n))

                step(1, dve.tensor_scalar(ffn_c[:, 0:1], wscale[:, 0:1], -1.0, None, ALU.mult))
                step(2, dve.reciprocal(ffn_c[:, 2:3], ffn_c[:, 0:1]))
                step(3, dve.tensor_scalar(ffn_c[:, 1:2], ffn_c[:, 2:3], 0.5, None, ALU.mult))
                step(4, dve.tensor_tensor(ffn_c[:, 2:3], wscale[:, 1:2], wscale[:, 2:3], ALU.mult))
                step(5, dve.tensor_tensor(ffn_c[:, 3:4], ffn_c[:, 0:1], ffn_c[:, 2:3], ALU.mult))
                step(6, dve.tensor_scalar(ffn_c[:, 2:3], ffn_c[:, 3:4], 2.0, None, ALU.mult))
                dve.wait_ge(tern_done.sem, tern_done.at(0, 3))
                dve.tensor_copy(ffn_c[:, 3:4], ffn_c[:, 2:3]).then_inc(ffn_consts.sem, 1)

            out = dve_emptied.sem

            def keys(g):
                for e in range(DB):
                    dve.wait_ge(front_ready.sem, full(g, "k", e))
                    dve.tensor_copy(kcat[:, e, :, 1, :], tile("k", e).rearrange("p (b k) -> p b k", b=GB))\
                        .then_inc(dve_front.sem, 1)

            def maxima(g):
                for n in range(GB // 2):
                    dve.wait_ge(front_ready.sem, full(g, "s", n))
                    dve.tensor_reduce(nmax[:, 2 * n:2 * n + 2], tile("s", n).rearrange("p (a b) -> p a b", a=2), AX.X,
                                      ALU.max, negate=True).then_inc(neg_max.sem, 1)

            def values_and_turned(g):
                for n in range(GB // 2):
                    dve.wait_ge(front_ready.sem, full(g, "v", n))
                    dve.tensor_copy(v_sb[:, 2 * n:2 * n + 2, :].rearrange("p a b -> p (a b)"), tile("v", n))\
                        .then_inc(dve_front.sem, 1)
                for n in range(GB // 2):
                    dve.wait_ge(front_ready.sem, full(g, "pt", n))
                    dve.tensor_copy(prT[:, 2 * n:2 * n + 2, :, :].rearrange("p a b c -> p (a b c)"), tile("pt", n))\
                        .then_inc(dve_front.sem, 1)

            def output(g):
                dve.wait_ge(act_front.sem, empty(g, "s", GB // 2 - 1))
                dve.reciprocal(rinv[:], rsum[:]).then_inc(sums_inv.sem, 1)
                dve.wait_ge(sums_inv.sem, sums_inv.at(g, 1))
                for n in range(GB // 2):
                    dve.wait_ge(front_ready.sem, full(g, "o", n))
                    for j in (2 * n, 2 * n + 1):
                        i = dve.scalar_tensor_tensor(out=x_res[:, j, :], in0=tile("o", n)[:, (j % 2) * D:(j % 2 + 1) * D],
                                                     scalar=rinv[:, j:j + 1], in1=x_in[:, j, :], op0=ALU.mult,
                                                     op1=ALU.add)
                        i.then_inc(dve_front.sem, 1)

            def expert_rows(g, again):
                dve.wait_ge(dve_front.sem, empty(g, "o", GB // 2 - 1))
                layernorm(g, again, 1, x_res, xn)
                dve.wait_ge(ln_done[1].sem, ln_done[1].at(g, GB))
                dve.tensor_tensor(acc[:].rearrange("p a b -> p (a b)"), x_res[:].rearrange("p a b -> p (a b)"),
                                  xn[:].rearrange("p a b -> p (a b)"), ALU.add).then_inc(base_sum.sem, 1)

            def body(g, again, last=False):
                dve.wait_ge(tiles_ready.sem, full(g, "k1", 0))
                if not again:
                    dve.wait_ge(w_attn1.sem, w_attn1.at(0, 12))
                    dve.wait_ge(pads.sem, pads.at(0, 4))
                kt = tile("k1", 0)
                for r in range(2):
                    dve.scalar_tensor_tensor(out=kr[:, r, :], in0=kt[:, r * T:(r + 1) * T], scalar=bk1[:, r:r + 1],
                                             in1=rope[:, 2 + r, :], op0=ALU.add, op1=ALU.mult).then_inc(out, 1)
                dve.wait_ge(dve_emptied.sem, empty(g, "k1", 0))
                dve.tensor_tensor(kr[:, 2, :], kr[:, 0, :], kr[:, 1, :], ALU.add).then_inc(kr_done.sem, 1)
                dve.wait_ge(tiles_ready.sem, full(g, "v1", 0))
                if again:
                    dve.wait_ge(tiles_ready.sem, full(g - 1, "pv", UNITS // 2 - 1))
                dve.tensor_tensor(Vs[:].rearrange("p b k h c -> p (b k) h c")[:, :, :, 0:HD],
                                  tile("v1", 0)[:, 0:8 * 32].rearrange("p (n h d) -> p n h d", n=8, h=KV),
                                  bv1[:].rearrange("p (o h d) -> p o h d", o=1, h=KV).broadcast_to([P, 8, KV, HD]),
                                  ALU.add).then_inc(out, 1)
                dve.wait_ge(kr_done.sem, kr_done.at(g, 1))
                dve.wait_ge(k_hi.sem, k_hi.at(g, 1))
                dve.tensor_tensor(kres, kr[:, 2, :], ksplit[:, 0, :], ALU.subtract).then_inc(kres_done.sem, 1)
                dve.wait_ge(kres_done.sem, kres_done.at(g, 1))
                dve.wait_ge(k_hi.sem, k_hi.at(g, 2))
                dve.tensor_tensor(ksplit[:, 2, :], kres, ksplit[:, 1, :], ALU.subtract)\
                    .then_inc(k_split_done.sem, 1)
                for d in range(DB):
                    dve.wait_ge(ex_hi.sem, ex_hi.at(g, d + 1))
                    dve.scalar_tensor_tensor(out=exlo[:, d, :], in0=xnT[:, d, :], scalar=X_SCALE, in1=exhi[:, d, :],
                                             op0=ALU.mult, op1=ALU.subtract).then_inc(ex_lo.sem, 1)
                dve.wait_ge(act_emptied.sem, empty(g, "route", 0))
                dve.tensor_scalar(el1, el, 1.0, None, ALU.add).then_inc(route_step.sem, 1)
                dve.wait_ge(route_step.sem, route_step.at(g, 1))
                dve.reciprocal(prob, el1).then_inc(route_step.sem, 1)
                dve.wait_ge(route_step.sem, route_step.at(g, 2))
                if again:
                    dve.sem_inc(passed.sem, 1)
                for j in range(GB):
                    dve.max(top[:, j, :], prob[:, j, :]).then_inc(top_step.sem, 1)
                for j in range(GB):
                    dve.wait_ge(top_step.sem, top_step.at(g, j + 1))
                    if again:
                        dve.sem_inc(passed.sem, 1)
                    dve.max_index(topi[:, j, :], top[:, j, :], prob[:, j, :]).then_inc(top_step.sem, 1)
                dve.tensor_tensor(psum2[:], top[:, :, 0:1], top[:, :, 1:2], ALU.add).then_inc(route_step.sem, 1)
                dve.wait_ge(route_step.sem, route_step.at(g, 3))
                dve.reciprocal(pinv[:], psum2[:]).then_inc(route_step.sem, 1)
                dve.wait_ge(top_step.sem, top_step.at(g, 2 * GB))
                dve.tensor_copy(topf[:], topi[:, :, 0:2]).then_inc(route_step.sem, 1)
                dve.wait_ge(route_step.sem, route_step.at(g, 4))
                for j in range(GB):
                    dve.tensor_scalar(topw[:, j, :], top[:, j, 0:2], pinv[:, j, 0:1], None, ALU.mult)\
                        .then_inc(route_step.sem, 1)
                dve.wait_ge(route_step.sem, route_step.at(g, 5 + GB))
                for j in range(GB):
                    for k, hot in enumerate((hot0, hot1)):
                        dve.tensor_scalar(hot[:, j, :], iota_e[:], topf[:, j, k:k + 1], topw[:, j, k:k + 1],
                                          ALU.is_equal, ALU.mult).then_inc(hots.sem, 1)
                dve.wait_ge(hots.sem, hots.at(g, 2 * GB))
                dve.tensor_tensor(comb[:, :, 0:E], hot0, hot1, ALU.add).then_inc(comb_done.sem, 1)

                def product(e):
                    dve.wait_ge(tiles_ready.sem, full(g, "up", e))
                    dve.wait_ge(act_emptied.sem, empty(g, "gate", e))
                    if e >= 2:
                        dve.wait_ge(y_hi.sem, y_hi.at(g, e - 1))
                    else:
                        if again:
                            dve.wait_ge(y_hi.sem, y_hi.at(g - 1, ES - 1 + e))
                    dve.scalar_tensor_tensor(out=y_sb[:, e % 2, :], in0=tile("up", e), scalar=ubs[:, e:e + 1],
                                             in1=g_sb[:, e % 2, :], op0=ALU.add, op1=ALU.mult).then_inc(out, 1)

                def hidden_low(e):
                    dve.wait_ge(y_hi.sem, y_hi.at(g, e + 1))
                    dve.wait_ge(dve_emptied.sem, empty(g, "up", e))
                    dve.scalar_tensor_tensor(out=ylo[:, e % 2, :], in0=y_sb[:, e % 2, :], scalar=fac[:, e // ET, 4:5],
                                             in1=yhi[:, e % 2, :], op0=ALU.mult, op1=ALU.subtract)\
                        .then_inc(y_lo.sem, 1)

                def share(third):
                    dve.tensor_scalar(combs[:, :, third * ET:(third + 1) * ET], comb[:, :, third * ET:(third + 1) * ET],
                                      fac[:, third, 6:7], None, ALU.mult).then_inc(comb_scaled.sem, 1)

                product(0)
                product(1)
                hidden_low(0)
                if not again:
                    for c in range(3, 6):
                        magnitude(c)
                for n in range(GB // 2):
                    dve.wait_ge(tiles_ready.sem, full(g, "bias2", n))
                    dve.wait_ge(base_sum.sem, base_sum.at(g, 1))
                    half = acc[:, 2 * n:2 * n + 2, :].rearrange("p a b -> p (a b)")
                    dve.tensor_tensor(half, half, tile("bias2", n), ALU.add).then_inc(out, 1)
                dve.wait_ge(comb_done.sem, comb_done.at(g, 1))
                for third in range(THIRDS if again else 1):
                    share(third)
                for e in range(ES):
                    if e + 1 < ES:
                        hidden_low(e + 1)
                    if e % ET == 0:
                        dve.wait_ge(comb_scaled.sem, comb_scaled.at(g, e // ET + 1))
                    for n in range(GB // 2):
                        dve.wait_ge(tiles_ready.sem, full(g, "down", 2 * e + n))
                        if e == 0:
                            dve.wait_ge(dve_emptied.sem, empty(g, "bias2", n))
                        for j in (2 * n, 2 * n + 1):
                            if e:
                                dve.wait_ge(dve_emptied.sem, empty(g, "down", 2 * (e - 1) + n, j % 2 + 1))
                            t = tile("down", 2 * e + n)[:, (j % 2) * D:(j % 2 + 1) * D]
                            dve.scalar_tensor_tensor(out=acc[:, j, :], in0=t, scalar=combs[:, j, e:e + 1],
                                                     in1=acc[:, j, :], op0=ALU.mult, op1=ALU.add)\
                                .then_inc(out, 1)
                    if e + 2 < ES:
                        product(e + 2)
                    for c in range(3, CHUNKS):
                        if MAG_AT.get(c) == e and not again:
                            magnitude(c)
                        if SCALES_AT.get(c // 3) == e and c % 3 == 0 and not again:
                            scales(c // 3)
                            share(c // 3)
                    if e == ROWS_NEXT_AT and not last:
                        dve.wait_ge(x_loaded.sem, x_loaded.at(g + 1, 1))
                    if 0 <= e - ROWS_NEXT_AT < GB and not last:
                        statistics(g + 1, 0, x_in, e - ROWS_NEXT_AT)
                    if e == ROWS_NEXT_AT + GB - 1 and not last:
                        mean_and_variance(g + 1, again, 0)
                    if 0 <= e - ROWS_NEXT_AT - GB < GB and not last:
                        normalise(g + 1, 0, x_in, xn0, e - ROWS_NEXT_AT - GB)
                    if not again and e in QUANT_AT:
                        quantise(QUANT_AT.index(e))
                if not again:
                    ffn_scales()
                dve.wait_ge(dve_emptied.sem, empty(g, "down", 2 * ES - 1))
                layernorm(g, again, 2, acc, xn)
                if again:
                    dve.wait_ge(stored.sem, stored.at(g - 1, 1))
                for j in range(GB):
                    dve.wait_ge(tiles_ready.sem, full(g, "q1", j))
                    if j >= 2:
                        dve.wait_ge(q_rotated.sem, q_rotated.at(g, j - 1))
                    for r in range(2):
                        dve.scalar_tensor_tensor(out=qr[:, r, j % 2, :], in0=tile("q1", j)[:, r * T:(r + 1) * T],
                                                 scalar=bq1[:, r:r + 1], in1=rope[:, r, :], op0=ALU.add,
                                                 op1=ALU.mult).then_inc(out, 1)
                    if j < GPSIMD_FROM:
                        dve.wait_ge(dve_emptied.sem, empty(g, "q1", j))
                        dve.tensor_tensor(q_rot[:, j, :], qr[:, 0, j % 2, :], qr[:, 1, j % 2, :], ALU.add)\
                            .then_inc(q_rotated.sem, 1)
                        dve.wait_ge(q_rotated.sem, q_rotated.at(g, j + 1))
                        dve.wait_ge(q_hi.sem, q_hi.at(g, 2 * j + 1))
                        dve.tensor_tensor(qres[:, j, :], q_rot[:, j, :], qsplit[:, j, 0, :], ALU.subtract)\
                            .then_inc(q_res_done.sem, 1)
                        dve.wait_ge(q_res_done.sem, q_res_done.at(g, j + 1))
                        dve.wait_ge(q_hi.sem, q_hi.at(g, 2 * j + 2))
                        dve.tensor_tensor(qsplit[:, j, 2, :], qres[:, j, :], qsplit[:, j, 1, :], ALU.subtract)\
                            .then_inc(q_split_done.sem, 1)
                    if j == KEYS_AT and not last:
                        keys(g + 1)
                def split_maxima(n):
                    dve.wait_ge(tiles_ready.sem, full(g, "mt", n))
                    if again:
                        dve.wait_ge(m_stacked[n].sem, m_stacked[n].at(g - 1, 2))
                    t = tile("mt", n)[0:H, 0:P]
                    dve.tensor_scalar(mhi[:, n, :], t, -1.0, None, ALU.mult).then_inc(out, 1)
                    dve.wait_ge(dve_emptied.sem, empty(g, "mt", n, 1))
                    dve.scalar_tensor_tensor(out=mlo[:, n, :], in0=t, scalar=-1.0, in1=mhi[:, n, :],
                                             op0=ALU.mult, op1=ALU.subtract).then_inc(out, 1)

                for s in range(STEPS):
                    j, kv = divmod(s, KV)
                    for n in range(SMAX_TILES):
                        if n == MT_AT and s % 2 == 0 and 0 <= s // 2 - 1 < UNITS // 2:
                            split_maxima(s // 2 - 1)
                        if s < UNITS:
                            t, at = SMAX_TILES * s + n, 2 * (KV * kv + SMAX_BANKS * n)
                            dve.wait_ge(tiles_ready.sem, full(g, "smax", t))
                            dve.tensor_reduce(M[:, j, at:at + 2 * SMAX_BANKS],
                                              tile("smax", t, SMAX_BANKS).rearrange("p (a b) -> p a b", b=T), AX.X,
                                              ALU.max).then_inc(out, 1)
                    if s == SCORES_AT and not last:
                        maxima(g + 1)
                for j in range(GB):
                    if j == GB - 1 and not last:
                        values_and_turned(g + 1)
                    dve.wait_ge(nd_loaded[j].sem, nd_loaded[j].at(g, 2))
                    dve.reciprocal(den[:, j, :], den[:, j, :]).then_inc(den_inv.sem, 1)
                    dve.wait_ge(den_inv.sem, den_inv.at(g, j + 1))
                    dve.tensor_tensor(num[:, j, :], num[:, j, :], den[:, j, :], ALU.mult).then_inc(normed.sem, 1)
                for n in range(GB // 2):
                    dve.wait_ge(tiles_ready.sem, full(g, "o1", n))
                    dve.scalar_tensor_tensor(out=x3[:, 2 * n:2 * n + 2, :].rearrange("p a b -> p (a b)"),
                                             in0=tile("o1", n), scalar=bo1[:, 0:1],
                                             in1=acc[:, 2 * n:2 * n + 2, :].rearrange("p a b -> p (a b)"),
                                             op0=ALU.add, op1=ALU.add).then_inc(out, 1)
                dve.wait_ge(dve_emptied.sem, empty(g, "o1", GB // 2 - 1))
                layernorm(g, again, 3, x3, xn)
                if not last:
                    output(g + 1)
                for d in range(DB):
                    dve.wait_ge(x_hi.sem, x_hi.at(g, d + 1))
                    dve.wait_ge(tiles_ready.sem, full(g, "xt4", d))
                    dve.tensor_tensor(xlo[:, d, :], tile("xt4", d), xhi[:, d, :], ALU.subtract).then_inc(out, 1)
                for e in range(EB):
                    dve.wait_ge(tiles_ready.sem, full(g, "gate4", e))
                    dve.wait_ge(act_emptied.sem, empty(g, "up4", e))
                    if e >= 2:
                        dve.wait_ge(h_lo.sem, h_lo.at(g, e - 1))
                        dve.wait_ge(h_hi.sem, h_hi.at(g, e - 1))
                    else:
                        if again:
                            dve.wait_ge(h_lo.sem, h_lo.at(g - 1, EB - 1 + e))
                        if again:
                            dve.wait_ge(h_hi.sem, h_hi.at(g - 1, EB - 1 + e))
                    dve.scalar_tensor_tensor(out=h_sb[:, e % 2, :], in0=tile("gate4", e), scalar=ffn_c[:, 1:2],
                                             in1=s_sb[:, e % 2, :], op0=ALU.mult, op1=ALU.mult)\
                        .then_inc(out, 1)
                    if e == LN_NEXT_AT and not last:
                        expert_rows(g + 1, again)
                for n in range(GB // 2):
                    dve.wait_ge(tiles_ready.sem, full(g, "down4", n))
                    for j in (2 * n, 2 * n + 1):
                        dve.scalar_tensor_tensor(out=y_out[:, j, :], in0=tile("down4", n)[:, (j % 2) * D:(j % 2 + 1) * D],
                                                 scalar=ffn_c[:, 3:4], in1=x3[:, j, :], op0=ALU.mult, op1=ALU.add)\
                            .then_inc(out, 1)

            dve.wait_ge(x_loaded.sem, x_loaded.at(0, 1))
            layernorm(0, False, 0, x_in, xn0)
            keys(0)
            maxima(0)
            magnitude(0)
            values_and_turned(0)
            magnitude(1)
            magnitude(2)
            scales(0)
            output(0)
            expert_rows(0, False)
            for c in range(3):
                weights_low(c)
            body(0, False)
            with dve.Fori(1, NG - 1) as g:
                body(g, True)
            body(NG - 1, True, last=True)


def layouts(i):
    f = lambda v: np.ascontiguousarray(v)
    heads = np.arange(P).reshape(H, HD)
    by_d = heads.T.reshape(-1)
    turned = np.roll(heads, -(HD // 2), axis=1).T.reshape(-1)
    kheads = np.arange(KV * HD).reshape(KV, HD)
    k_by_d = kheads.T.reshape(-1)
    k_turned = np.roll(kheads, -(HD // 2), axis=1).T.reshape(-1)
    pv = np.arange(P).reshape(KV, KV, HD).transpose(2, 1, 0).reshape(-1)
    Wq, Wk, Wv, Wo = (i[f"L1_xattn_W{n}"] for n in "qkvo")
    bq, bk = i["L1_xattn_bq"], i["L1_xattn_bk"]
    halves = lambda w: f(w.T.reshape(DB, P, DE).transpose(1, 0, 2).reshape(P, DB * DE))
    return {
        "x": f(i["x"]), "ctx": f(i["ctx_2048"]),
        "ctxT": f(i["ctx_2048"].transpose(0, 2, 1).reshape(B, DB, P, P)),
        "wq0": f(i["L0_xattn_wq"].T), "wk0": f(i["L0_xattn_wk"].T), "wv0": f(i["L0_xattn_wv"].T),
        "wo0": f(i["L0_xattn_wo"].T), "wa": f(i["L0_ffn_wa"]),
        "wg": f(np.concatenate([i["L0_ffn_rg"], i["L0_ffn_sg"]])), "wu": f(np.concatenate([i["L0_ffn_rw1"], i["L0_ffn_sw1"]])),
        "w2": f(np.concatenate([i["L0_ffn_rw2"], i["L0_ffn_sw2"]])),
        "gb": f(np.concatenate([i["L0_ffn_rgb"], i["L0_ffn_sgb"]]).T), "ub": f(np.concatenate([i["L0_ffn_rb1"], i["L0_ffn_sb1"]]).T),
        "b2": f(np.concatenate([i["L0_ffn_rb2"], i["L0_ffn_sb2"]])),
        "wq1": f(Wq[by_d].T), "wq1r": f(Wq[turned].T), "wk1": f(Wk[k_by_d].T), "wk1r": f(Wk[k_turned].T), "wv1": f(Wv.T),
        "bq1": f(np.stack([bq[by_d], bq[turned]], axis=1)),
        "bk1": f(np.tile(np.stack([bk[k_by_d], bk[k_turned]], axis=1), (GB, 1))),
        "bv1": f(i["L1_xattn_bv"][None]), "wo1": f(Wo.T[pv]), "bo1": f(i["L1_xattn_bo"][:, None]),
        "wup": halves(i["L1_ffn_W_up"]), "wgate": halves(i["L1_ffn_W_gate"]),
        "wdown": f(i["L1_ffn_W_down"].T.reshape(EB, P, D).transpose(1, 0, 2).reshape(P, EB * D)),
        "rope": rope_tables(), "iota": np.arange(E, dtype=np.float32)[None],
    }


def kernel(**inputs):
    import concourse.bacc as bacc
    from concourse.bass_utils import run_bass_kernel_spmd

    arrays = layouts({k: np.asarray(v) for k, v in inputs.items() if k != "mask_BxSx4224_bf0"})
    nc = bacc.Bacc("TRN2", target_bir_lowering=False, num_devices=1)
    aps = {n: nc.dram_tensor(f"in_{n}", v.shape, mybir.dt.from_np(v.dtype), kind="ExternalInput").ap() for n, v in arrays.items()}
    aps["out"] = nc.dram_tensor("out", (B, P, D), F32, kind="ExternalOutput").ap()
    build(nc, aps)
    r = run_bass_kernel_spmd(nc, [{f"in_{n}": v for n, v in arrays.items()}], core_ids=[0])
    return r.results[0]["out"]
```
